# Optimizing a Trainium2 kernel written in Bass

```python
import numpy as np
import jax
import jax.numpy as jnp

def _softmax(x, axis=-1):
    return jax.nn.softmax(x, axis=axis)

def _gelu(x):
    return jax.nn.gelu(x, approximate=True)

def _silu(x):
    return jax.nn.silu(x)

def _sigmoid(x):
    return jax.nn.sigmoid(x)

def _layernorm(x, axis=-1, eps=1e-05):
    m = jnp.mean(x, axis=axis, keepdims=True)
    v = jnp.var(x, axis=axis, keepdims=True)
    return (x - m) / jnp.sqrt(v + eps)

def _scatter_add(tgt, idx, src, axis=0):
    return tgt.at[idx].add(src)

def _segment_sum(src, seg, n):
    return jax.ops.segment_sum(src, seg, n)
kernel_name = 'mk_decoder_postln_d2_seqx_r8_69ca25'

def setup_inputs(seed: int=0):
    np.random.seed(seed)
    _w = jnp.asarray

    def _rec_inputs():
        import jax
        import jax.numpy as jnp
        _rk = jax.random.key(seed)
        x = 0.5 + 0.2887 * jax.random.normal(jax.random.fold_in(_rk, 1), (4, 256, 256), jnp.float32)
        _lenS = 256 - jax.random.randint(jax.random.fold_in(_rk, 7), (4,), 0, max(1, 256 // 4) + 1, jnp.int32)
        _lenS2 = 256 - jax.random.randint(jax.random.fold_in(_rk, 8), (4,), 0, max(1, 256 // 4) + 1, jnp.int32)
        _ctx_512P = jax.random.normal(jax.random.fold_in(_rk, 11), (4, 16, 64), jnp.float32)
        _ctx_512c = jax.random.dirichlet(jax.random.fold_in(_rk, 511), 0.3 * jnp.ones((16,), jnp.float32), (4, 256))
        _ctx_512t = jnp.einsum('bsk,bkd->bsd', _ctx_512c, _ctx_512P)
        _ctx_512t = _ctx_512t * jax.lax.rsqrt(jnp.mean(jnp.square(_ctx_512t)) + 1e-12) * 0.953939
        ctx_512 = -0.000392918 + 0.999932 * (_ctx_512t + 0.3 * jax.random.normal(jax.random.fold_in(_rk, 611), (4, 256, 64), jnp.float32))
        return (x, ctx_512)
    x, ctx_512 = _rec_inputs()

    def _L0_attn_setup():
        import jax, jax.numpy as jnp
        import numpy as np
        B, T, D_MODEL = (4, 256, 256)
        NUM_HEADS, HEAD_SIZE = (16, 128)
        MODEL_SIZE = 256
        key = jax.random.key(seed)
        ks = jax.random.split(key, 9)
        s = 0.02 / np.sqrt(D_MODEL)
        so = 0.02 / np.sqrt(NUM_HEADS * HEAD_SIZE)
        return {'query': jax.random.normal(ks[0], (B, T, D_MODEL), jnp.float32), 'w_q': jax.random.normal(ks[1], (D_MODEL, NUM_HEADS * HEAD_SIZE), jnp.float32) * s, 'b_q': jnp.zeros((NUM_HEADS * HEAD_SIZE,), jnp.float32), 'w_k': jax.random.normal(ks[2], (D_MODEL, NUM_HEADS * HEAD_SIZE), jnp.float32) * s, 'b_k': jnp.zeros((NUM_HEADS * HEAD_SIZE,), jnp.float32), 'w_v': jax.random.normal(ks[3], (D_MODEL, NUM_HEADS * HEAD_SIZE), jnp.float32) * s, 'b_v': jnp.zeros((NUM_HEADS * HEAD_SIZE,), jnp.float32), 'w_o': jax.random.normal(ks[4], (NUM_HEADS * HEAD_SIZE, MODEL_SIZE), jnp.float32) * so, 'b_o': jnp.zeros((MODEL_SIZE,), jnp.float32)}
    _L0_attn_all = _L0_attn_setup()
    _L0_attn_in = {k: v for k, v in _L0_attn_all.items() if k in ('w_q', 'b_q', 'w_k', 'b_k', 'w_v', 'b_v', 'w_o', 'b_o')}
    del _L0_attn_all

    def _L0_xattn_setup():
        import jax, jax.numpy as jnp
        import numpy as np
        B, N, D = (16, 256, 64)
        H = 4
        TOP_K_RATIO = 0.3
        key = jax.random.key(seed)
        k1, k2, k3, k4 = jax.random.split(key, 4)
        h = jax.random.normal(k1, (B, N, D), dtype=jnp.float32)
        adj_raw = jax.random.uniform(k2, (B, N, N), dtype=jnp.float32)
        lim = 1.0 / np.sqrt(D)
        Wq = jax.random.uniform(k3, (D, D), minval=-lim, maxval=lim, dtype=jnp.float32)
        Wk = jax.random.uniform(k4, (D, D), minval=-lim, maxval=lim, dtype=jnp.float32)
        gamma_raw = jnp.float32(-0.85)
        return {'h': h, 'adj_raw': adj_raw, 'Wq': Wq, 'Wk': Wk, 'gamma_raw': gamma_raw}
    _L0_xattn_all = _L0_xattn_setup()
    _L0_xattn_in = {k: v for k, v in _L0_xattn_all.items() if k in ('Wq', 'Wk', 'gamma_raw')}
    del _L0_xattn_all

    def _L0_ffn_setup():
        import jax, jax.numpy as jnp
        import numpy as np
        B, S, D_IN, D_OUT, E = (4, 128, 256, 256, 32)
        MASK_DENSITY = 0.3
        THRESH = 0.5
        key = jax.random.key(seed)
        k_x, k_w, k_m, k_r = jax.random.split(key, 4)
        x = jax.random.normal(k_x, (B, S, D_IN), dtype=jnp.float32)
        bound = np.sqrt(1.0 / D_IN) * np.sqrt(3.0)
        weight = jax.random.uniform(k_w, (D_OUT, D_IN), minval=-bound, maxval=bound, dtype=jnp.float32)
        scale = jnp.ones((D_OUT,), dtype=jnp.float32)
        expert_masks = (jax.random.uniform(k_m, (E, D_OUT, D_IN)) < MASK_DENSITY).astype(jnp.float32)
        router_w = 0.01 * jax.random.normal(k_r, (E, D_IN), dtype=jnp.float32)
        return {'x': x, 'weight': weight, 'scale': scale, 'expert_masks': expert_masks, 'router_w': router_w}
    _L0_ffn_all = _L0_ffn_setup()
    _L0_ffn_in = {k: v for k, v in _L0_ffn_all.items() if k in ('weight', 'scale', 'expert_masks', 'router_w')}
    del _L0_ffn_all

    def _L1_attn_setup():
        import jax, jax.numpy as jnp
        import numpy as np
        HEADS = 16
        KV_HEADS = 4
        DIM_HEAD = 128
        DIM = 256
        ROPE_BASE = 10000.0

        def rotate_half(t):
            t1, t2 = jnp.split(t, 2, axis=-1)
            return jnp.concatenate((-t2, t1), axis=-1)

        def apply_rotary(t, cos, sin):
            return t * cos + rotate_half(t) * sin
        key = jax.random.key(seed)
        ks = jax.random.split(key, 6)
        b, n = (4, 128)
        s = 1.0 / np.sqrt(DIM)
        x = jax.random.normal(ks[0], (b, n, DIM), dtype=jnp.float32)
        Wq = jax.random.normal(ks[1], (DIM, HEADS * DIM_HEAD), dtype=jnp.float32) * s
        Wk = jax.random.normal(ks[2], (DIM, KV_HEADS * DIM_HEAD), dtype=jnp.float32) * s
        Wv = jax.random.normal(ks[3], (DIM, KV_HEADS * DIM_HEAD), dtype=jnp.float32) * s
        Wo = jax.random.normal(ks[4], (HEADS * DIM_HEAD, DIM), dtype=jnp.float32) * s
        head_scale = 1.0 + 0.02 * jax.random.normal(ks[5], (1, HEADS, 1, 1), dtype=jnp.float32)
        return {'x': x, 'Wq': Wq, 'Wk': Wk, 'Wv': Wv, 'Wo': Wo, 'head_scale': head_scale}
    _L1_attn_all = _L1_attn_setup()
    _L1_attn_in = {k: v for k, v in _L1_attn_all.items() if k in ('Wq', 'Wk', 'Wv', 'Wo', 'head_scale')}
    del _L1_attn_all

    def _L1_xattn_setup():
        import jax, jax.numpy as jnp
        import numpy as np
        EPS = 1e-06
        IMAGE_DIMS = 256
        key = jax.random.key(seed)
        k1, k2, k3 = jax.random.split(key, 3)
        B, I, J, D = (16, 256, 256, 64)
        p = jax.random.normal(k1, (B, I, J), dtype=jnp.float32)
        k_v = jax.random.normal(k2, (B, J, D), dtype=jnp.float32)
        W_k = jax.random.normal(k3, (D, D), dtype=jnp.float32) * (1.0 / np.sqrt(D))
        b_k = jnp.zeros((D,), dtype=jnp.float32)
        ln_gamma = jnp.ones((J,), dtype=jnp.float32)
        ln_beta = jnp.zeros((J,), dtype=jnp.float32)
        return {'p': p, 'k_v': k_v, 'W_k': W_k, 'b_k': b_k, 'ln_gamma': ln_gamma, 'ln_beta': ln_beta}
    _L1_xattn_all = _L1_xattn_setup()
    _L1_xattn_in = {k: v for k, v in _L1_xattn_all.items() if k in ('W_k', 'b_k', 'ln_gamma', 'ln_beta')}
    del _L1_xattn_all

    def _L1_ffn_setup():
        import jax, jax.numpy as jnp
        import numpy as np
        TOP_K = 4
        key = jax.random.key(seed)
        ks = jax.random.split(key, 8)
        B, S, D, E, H, HS = (2, 256, 256, 16, 128, 512)
        scaled = lambda k, shape, fan: jax.random.normal(k, shape, jnp.float32) * fan ** (-0.5)
        return {'x': jax.random.normal(ks[0], (B, S, D), jnp.float32), 'w_router': scaled(ks[1], (D, E), D), 'we1': scaled(ks[2], (E, D, H), D), 'we3': scaled(ks[3], (E, D, H), D), 'we2': scaled(ks[4], (E, H, D), H), 'ws1': scaled(ks[5], (D, HS), D), 'ws3': scaled(ks[6], (D, HS), D), 'ws2': scaled(ks[7], (HS, D), HS)}
    _L1_ffn_all = _L1_ffn_setup()
    _L1_ffn_in = {k: v for k, v in _L1_ffn_all.items() if k in ('w_router', 'we1', 'we3', 'we2', 'ws1', 'ws3', 'ws2')}
    del _L1_ffn_all
    return {'x': x, 'ctx_512': ctx_512, 'L0_attn_w_q': _L0_attn_in['w_q'], 'L0_attn_b_q': _L0_attn_in['b_q'], 'L0_attn_w_k': _L0_attn_in['w_k'], 'L0_attn_b_k': _L0_attn_in['b_k'], 'L0_attn_w_v': _L0_attn_in['w_v'], 'L0_attn_b_v': _L0_attn_in['b_v'], 'L0_attn_w_o': _L0_attn_in['w_o'], 'L0_attn_b_o': _L0_attn_in['b_o'], 'L0_xattn_Wq': _L0_xattn_in['Wq'], 'L0_xattn_Wk': _L0_xattn_in['Wk'], 'L0_xattn_gamma_raw': _L0_xattn_in['gamma_raw'], 'L0_ffn_weight': _L0_ffn_in['weight'], 'L0_ffn_scale': _L0_ffn_in['scale'], 'L0_ffn_expert_masks': _L0_ffn_in['expert_masks'], 'L0_ffn_router_w': _L0_ffn_in['router_w'], 'L1_attn_Wq': _L1_attn_in['Wq'], 'L1_attn_Wk': _L1_attn_in['Wk'], 'L1_attn_Wv': _L1_attn_in['Wv'], 'L1_attn_Wo': _L1_attn_in['Wo'], 'L1_attn_head_scale': _L1_attn_in['head_scale'], 'L1_xattn_W_k': _L1_xattn_in['W_k'], 'L1_xattn_b_k': _L1_xattn_in['b_k'], 'L1_xattn_ln_gamma': _L1_xattn_in['ln_gamma'], 'L1_xattn_ln_beta': _L1_xattn_in['ln_beta'], 'L1_ffn_w_router': _L1_ffn_in['w_router'], 'L1_ffn_we1': _L1_ffn_in['we1'], 'L1_ffn_we3': _L1_ffn_in['we3'], 'L1_ffn_we2': _L1_ffn_in['we2'], 'L1_ffn_ws1': _L1_ffn_in['ws1'], 'L1_ffn_ws3': _L1_ffn_in['ws3'], 'L1_ffn_ws2': _L1_ffn_in['ws2']}

def reference(x, ctx_512, L0_attn_w_q, L0_attn_b_q, L0_attn_w_k, L0_attn_b_k, L0_attn_w_v, L0_attn_b_v, L0_attn_w_o, L0_attn_b_o, L0_xattn_Wq, L0_xattn_Wk, L0_xattn_gamma_raw, L0_ffn_weight, L0_ffn_scale, L0_ffn_expert_masks, L0_ffn_router_w, L1_attn_Wq, L1_attn_Wk, L1_attn_Wv, L1_attn_Wo, L1_attn_head_scale, L1_xattn_W_k, L1_xattn_b_k, L1_xattn_ln_gamma, L1_xattn_ln_beta, L1_ffn_w_router, L1_ffn_we1, L1_ffn_we3, L1_ffn_we2, L1_ffn_ws1, L1_ffn_ws3, L1_ffn_ws2):
    import jax
    import jax.numpy as jnp

    def _L0_attn_ref(query, w_q, b_q, w_k, b_k, w_v, b_v, w_o, b_o):
        import jax, jax.numpy as jnp
        import numpy as np
        B, T, D_MODEL = (4, 256, 256)
        NUM_HEADS, HEAD_SIZE = (16, 128)
        MODEL_SIZE = 256
        B_, T_, _ = query.shape
        q = (query @ w_q + b_q).reshape(B_, T_, NUM_HEADS, HEAD_SIZE)
        k = (query @ w_k + b_k).reshape(B_, T_, NUM_HEADS, HEAD_SIZE)
        v = (query @ w_v + b_v).reshape(B_, T_, NUM_HEADS, HEAD_SIZE)
        logits = jnp.einsum('bthd,bThd->bhtT', q, k) * jax.lax.rsqrt(jnp.float32(HEAD_SIZE))
        i = jnp.arange(T_, dtype=jnp.int32)[:, None]
        j = jnp.arange(T_, dtype=jnp.int32)
        mask = (i >= j).astype(logits.dtype)
        logits = logits - 10000000000.0 * (1.0 - mask)
        weights = jax.nn.softmax(logits, axis=-1)
        attn = jnp.einsum('bhtT,bThd->bthd', weights, v).reshape(B_, T_, NUM_HEADS * HEAD_SIZE)
        out = attn @ w_o + b_o
        return out

    def _L0_xattn_ref(h, adj_raw, Wq, Wk, gamma_raw):
        import jax, jax.numpy as jnp
        import numpy as np
        B, N, D = (16, 256, 64)
        H = 4
        TOP_K_RATIO = 0.3
        b, n, dm = h.shape
        d = dm // H
        Q = (h @ Wq.T).reshape(b, n, H, d).transpose(0, 2, 1, 3)
        K = (h @ Wk.T).reshape(b, n, H, d).transpose(0, 2, 1, 3)
        sim = jnp.einsum('bhnd,bhmd->bnm', Q, K) / (jnp.sqrt(jnp.float32(d)) * H)
        k = max(1, int(n * TOP_K_RATIO))
        topk_vals = jax.lax.top_k(sim, k)[0]
        threshold = topk_vals[:, :, -1:]
        sparse_mask = (sim >= threshold).astype(sim.dtype)
        A_learned = jax.nn.sigmoid(sim) * sparse_mask
        A_learned = (A_learned + jnp.swapaxes(A_learned, -1, -2)) * 0.5
        gamma = jax.nn.sigmoid(gamma_raw)
        return (1.0 - gamma) * adj_raw + gamma * A_learned

    def _L0_ffn_ref(x, weight, scale, expert_masks, router_w):
        import jax, jax.numpy as jnp
        import numpy as np
        B, S, D_IN, D_OUT, E = (4, 128, 256, 256, 32)
        MASK_DENSITY = 0.3
        THRESH = 0.5
        logits = jnp.einsum('bsd,ed->bse', x, router_w)
        probs = jax.nn.softmax(logits, axis=-1)
        top1_w = jnp.max(probs, axis=-1)
        top1_idx = jnp.argmax(probs, axis=-1)
        w_q = jnp.clip(jnp.round(weight / THRESH), -1.0, 1.0)
        w_scaled = w_q * scale[:, None]
        out0 = jnp.zeros((x.shape[0], x.shape[1], weight.shape[0]), dtype=x.dtype)

        def body(out, inputs):
            e_idx, mask_e = inputs
            y = jnp.einsum('bsi,oi->bso', x, w_scaled * mask_e)
            sel = (top1_idx == e_idx)[..., None]
            out = jnp.where(sel, y * top1_w[..., None], out)
            return (out, None)
        out, _ = jax.lax.scan(body, out0, (jnp.arange(E), expert_masks))
        return out

    def _L1_attn_ref(x, Wq, Wk, Wv, Wo, head_scale):
        import jax, jax.numpy as jnp
        import numpy as np
        HEADS = 16
        KV_HEADS = 4
        DIM_HEAD = 128
        DIM = 256
        ROPE_BASE = 10000.0

        def rotate_half(t):
            t1, t2 = jnp.split(t, 2, axis=-1)
            return jnp.concatenate((-t2, t1), axis=-1)

        def apply_rotary(t, cos, sin):
            return t * cos + rotate_half(t) * sin
        b, n, _ = x.shape
        q = (x @ Wq).reshape(b, n, HEADS, DIM_HEAD).transpose(0, 2, 1, 3)
        k = (x @ Wk).reshape(b, n, KV_HEADS, DIM_HEAD).transpose(0, 2, 1, 3)
        v = (x @ Wv).reshape(b, n, KV_HEADS, DIM_HEAD).transpose(0, 2, 1, 3)
        inv_freq = 1.0 / ROPE_BASE ** (jnp.arange(0, DIM_HEAD, 2, dtype=jnp.float32) / DIM_HEAD)
        freqs = jnp.arange(n, dtype=jnp.float32)[:, None] * inv_freq[None, :]
        emb = jnp.concatenate((freqs, freqs), axis=-1)
        cos, sin = (jnp.cos(emb), jnp.sin(emb))
        q = apply_rotary(q, cos, sin)
        k = apply_rotary(k, cos, sin)
        rep = HEADS // KV_HEADS
        k = jnp.repeat(k, rep, axis=1)
        v = jnp.repeat(v, rep, axis=1)
        scale = 1.0 / jnp.sqrt(jnp.array(DIM_HEAD, dtype=x.dtype))
        scores = jnp.einsum('bhid,bhjd->bhij', q, k) * scale
        causal = jnp.tril(jnp.ones((n, n), dtype=bool))
        scores = jnp.where(causal, scores, jnp.finfo(scores.dtype).min)
        attn = jax.nn.softmax(scores, axis=-1)
        out = jnp.einsum('bhij,bhjd->bhid', attn, v)
        out = out * head_scale
        out = out.transpose(0, 2, 1, 3).reshape(b, n, HEADS * DIM_HEAD)
        return out @ Wo

    def _L1_xattn_ref(p, k_v, W_k, b_k, ln_gamma, ln_beta):
        import jax, jax.numpy as jnp
        import numpy as np
        EPS = 1e-06
        IMAGE_DIMS = 256
        kv = k_v @ W_k.T + b_k
        out = jnp.einsum('bij,bjd->bid', p, kv)
        scale = IMAGE_DIMS ** (-0.5)
        sim = jnp.einsum('bid,bjd->bij', out, kv) * scale
        mu = jnp.mean(sim, axis=-1, keepdims=True)
        var = jnp.var(sim, axis=-1, keepdims=True)
        sim = (sim - mu) * jax.lax.rsqrt(var + EPS) * ln_gamma + ln_beta
        attn = jax.nn.softmax(sim, axis=-1)
        return attn

    def _L1_ffn_ref(x, w_router, we1, we3, we2, ws1, ws3, ws2):
        import jax, jax.numpy as jnp
        import numpy as np
        TOP_K = 4
        B, S, D = x.shape
        T = B * S
        E = w_router.shape[1]
        xt = x.reshape(T, D)
        probs = jax.nn.softmax(xt @ w_router, axis=-1)
        top_w, top_i = jax.lax.top_k(probs, TOP_K)
        top_w = top_w / jnp.sum(top_w, axis=-1, keepdims=True)
        cw = jnp.zeros((T, E), xt.dtype).at[jnp.arange(T)[:, None], top_i].add(top_w)
        g = jax.nn.silu(jnp.einsum('td,edh->teh', xt, we1)) * jnp.einsum('td,edh->teh', xt, we3)
        g = g * cw[:, :, None]
        moe_out = jnp.einsum('teh,ehd->td', g, we2)
        shared = jax.nn.silu(xt @ ws1) * (xt @ ws3) @ ws2
        k = TOP_K
        out = shared / (k + 1) + moe_out * (k / (k + 1))
        return out.reshape(B, S, D)
    x = _layernorm(x + _L0_attn_ref(x, L0_attn_w_q, L0_attn_b_q, L0_attn_w_k, L0_attn_b_k, L0_attn_w_v, L0_attn_b_v, L0_attn_w_o, L0_attn_b_o), axis=-1)
    x = _layernorm(x + _L0_xattn_ref(ctx_512, x, L0_xattn_Wq, L0_xattn_Wk, L0_xattn_gamma_raw), axis=-1)
    x = _layernorm(x + _L0_ffn_ref(x, L0_ffn_weight, L0_ffn_scale, L0_ffn_expert_masks, L0_ffn_router_w), axis=-1)
    x = _layernorm(x + _L1_attn_ref(x, L1_attn_Wq, L1_attn_Wk, L1_attn_Wv, L1_attn_Wo, L1_attn_head_scale), axis=-1)
    x = _layernorm(x + _L1_xattn_ref(x, ctx_512, L1_xattn_W_k, L1_xattn_b_k, L1_xattn_ln_gamma, L1_xattn_ln_beta), axis=-1)
    x = _layernorm(x + _L1_ffn_ref(x, L1_ffn_w_router, L1_ffn_we1, L1_ffn_we3, L1_ffn_we2, L1_ffn_ws1, L1_ffn_ws3, L1_ffn_ws2), axis=-1)
    return x

_drawn_inputs = setup_inputs


def setup_inputs(seed=0):
    import zlib

    import numpy as np

    out = dict(_drawn_inputs(seed))
    spreads = {'L0_attn_b_q': (0.0, 2.0),
     'L0_attn_b_k': (0.0, 2.0),
     'L0_attn_b_v': (0.0, 0.311),
     'L0_attn_b_o': (0.0, 0.1),
     'L0_ffn_scale': (1.0, 0.2),
     'L1_xattn_b_k': (0.0, 2.0),
     'L1_xattn_ln_gamma': (1.0, 0.6),
     'L1_xattn_ln_beta': (0.0, 2.0)}
    factors = {'L0_attn_w_q': 64.0, 'L0_attn_w_k': 64.0, 'L0_attn_w_v': 21.538, 'L1_xattn_W_k': 6.612}
    for name, (base, spread) in spreads.items():
        noise = np.random.default_rng([zlib.crc32(name.encode()), seed]).standard_normal(out[name].shape)
        drawn = base * np.exp(spread * noise) if base else spread * noise
        out[name] = jnp.asarray(drawn.astype(out[name].dtype))
    for name, factor in factors.items():
        out[name] = (out[name] * factor).astype(out[name].dtype)
    return out
```

```python
import concourse.bass as bass
from concourse import mybir
from contextlib import ExitStack

F32 = mybir.dt.float32
F32R = mybir.dt.float32r
BF16 = mybir.dt.bfloat16
ALU = mybir.AluOpType
ACT = mybir.ActivationFunctionType
AX = mybir.AxisListType

P = 128
B, T, D = 4, 256, 256
NT = B * T // P
KC = D // P
NTOK = B * T
HALF = NTOK // 2
BANK = 512
HEADS, DH = 16, 128
GROUP = 4
GROUPS = HEADS // GROUP
SCALE = DH ** -0.5
DC = 64
EPS = 1e-5
EXPERTS0 = 32
EXPERTS1, HID, TOPK = 16, 128, 4
SHARED = 512 // HID
KEEP = int(T * 0.3)
HALF_BLOCK = DH // 2


class Count:

    def __init__(self, sem):
        self.sem, self.base, self.n = sem, 0, 0

    def inc(self, instruction):
        instruction.then_inc(self.sem, 1)
        self.n += 1
        return self.base + self.n

    def enter(self, i, per_turn):
        self.entry, self.per_turn = self.base + self.n, per_turn
        self.base, self.n = self.entry + i * per_turn, 0

    def leave(self, turns):
        assert self.n == self.per_turn, (self.n, self.per_turn)
        self.base, self.n = self.entry + turns * self.per_turn, 0

    @property
    def now(self):
        return self.base + self.n


def f32(ap):
    return ap.bitcast(F32)


class Chip:
    pass


def decoder(nc, a, out, upto=99):
    with ExitStack() as ctx:
        c = Chip()
        c.nc, c.a, c.out = nc, a, out
        c.sem = lambda name: ctx.enter_context(nc.semaphore(name))
        sb = lambda name, shape, dt=F32: ctx.enter_context(nc.sbuf_tensor(name, shape, dt))
        c.banks = [ctx.enter_context(nc.psum_tensor(f"bank{i}", [P, BANK], F32)) for i in range(8)]
        c.x = sb("x", [P, NT, D])
        c.xt_hi, c.xt_lo = sb("xt_hi", [P, KC, NTOK], F32R), sb("xt_lo", [P, KC, NTOK], F32R)
        c.ident = sb("ident", [P, P])
        c.ident_bf = sb("ident_bf", [P, P], BF16)
        c.causal = sb("causal", [P, P], BF16)
        c.sim = sb("sim", [P, NT, T])
        c.thr = sb("thr", [P, NT])
        c.kv_hi, c.kv_lo = sb("kv_hi", [P, NT, P], F32R), sb("kv_lo", [P, NT, P], F32R)
        c.kvt_hi, c.kvt_lo = sb("kvt_hi", [DC, NTOK], F32R), sb("kvt_lo", [DC, NTOK], F32R)
        c.bias_t = sb("bias_t", [P, 3 * HEADS])
        c.rt_hi, c.rt_lo = sb("rt_hi", [P, KC, EXPERTS0], F32R), sb("rt_lo", [P, KC, EXPERTS0], F32R)
        c.tern = sb("tern", [P, KC, D], BF16)
        c.rows = sb("rows", [P, 5, D])
        c.gamma, c.one_less = sb("gamma", [P, 1]), sb("one_less", [P, 1])
        c.half_neg, c.one = sb("half_neg", [P, NT]), sb("one", [P, 1])
        setup(c)
        if upto >= 1:
            attention(c, 0)
        if upto >= 2:
            graph_and_masked_experts(c, upto)
        if upto >= 5:
            attention(c, 1)
        if upto >= 6:
            cross_and_experts(c, upto)
        if upto < 99:
            dump(c)


def dump(c):
    nc = c.nc
    s = c.sem("s_dump")
    with nc.Block() as block:
        @block.sync
        def _(sp):
            sp.dma_start(c.out.rearrange("b (t p) d -> p (b t) d", p=P), c.x[:]).then_inc(s, 16)
            sp.wait_ge(s, 16)


def mm3(nc, out, l_hi, l_lo, r_hi, r_lo, start, stop):
    nc.tensor.matmul(out, l_hi, r_hi, start=start, stop=False)
    nc.tensor.matmul(out, l_hi, r_lo, start=False, stop=False)
    return nc.tensor.matmul(out, l_lo, r_hi, start=False, stop=stop)


ROW_BO, ROW_SCALE, ROW_GAMMA, ROW_BETA, ROW_BK = range(5)


def setup(c):
    nc, a = c.nc, c.a
    with ExitStack() as ctx:
        sb = lambda name, shape, dt=F32: ctx.enter_context(nc.sbuf_tensor(name, shape, dt))
        ctx_nat = sb("ctx_nat", [P, NT, DC])
        ctxt_hi, ctxt_lo = sb("ctxt_hi", [DC, NTOK], F32R), sb("ctxt_lo", [DC, NTOK], F32R)
        w_nat = sb("w_nat", [DC, 3, DC])
        wt_hi, wt_lo = sb("wt_hi", [DC, 3, 2, DC], F32R), sb("wt_lo", [DC, 3, 2, DC], F32R)
        qt_hi, qt_lo = sb("qt_hi", [DC, NTOK], F32R), sb("qt_lo", [DC, NTOK], F32R)
        kt_hi, kt_lo = sb("kt_hi", [DC, NTOK], F32R), sb("kt_lo", [DC, NTOK], F32R)
        kv = sb("kv", [P, NT, P])
        bias_nat = sb("bias_nat", [3 * HEADS, DH])
        bk_col = sb("bk_col", [DC, 1])
        r_nat = sb("r_nat", [EXPERTS0, D])
        w0 = sb("w0", [P, KC, D])
        w0b = sb("w0b", [P, KC, D])
        causal_f = sb("causal_f", [P, P])
        g_raw, g_exp, g_den = sb("g_raw", [P, 1]), sb("g_exp", [P, 1]), sb("g_den", [P, 1])

        s_x, s_ctx, s_w, s_const, s_bias, s_rows = (c.sem(f"su_{n}") for n in ("x", "ctx", "w", "const", "bias", "rows"))
        s_tr = c.sem("su_tr")
        s_hi = c.sem("su_hi")
        s_lo = c.sem("su_lo")
        s_pool = c.sem("su_pool")

        bank = c.banks
        with nc.Block() as block:
            @block.sync
            def _(sp):
                sp.dma_start(c.ident[:], a["ident"]).then_inc(s_const, 16)
                sp.dma_start(ctx_nat[:], a["ctx_512"].rearrange("b (t p) d -> p (b t) d", p=P)).then_inc(s_ctx, 16)
                sp.dma_start(w_nat[:, 0], a["L0_xattn_Wq"]).then_inc(s_w, 16)
                sp.dma_start(w_nat[:, 1], a["L0_xattn_Wk"]).then_inc(s_w, 16)
                sp.dma_start(w_nat[:, 2], a["L1_xattn_W_k"]).then_inc(s_w, 16)
                sp.dma_start(r_nat[:], a["L0_ffn_router_w"]).then_inc(s_w, 16)
                for i, n in enumerate(("b_q", "b_k", "b_v")):
                    sp.dma_start(bias_nat[i * HEADS:(i + 1) * HEADS], a[f"L0_attn_{n}"].rearrange("(h d) -> h d", d=DH)).then_inc(s_w, 16)
                sp.dma_start(c.x[:], a["x"].rearrange("b (t p) d -> p (b t) d", p=P)).then_inc(s_x, 16)
                sp.dma_start(causal_f[:], a["causal"]).then_inc(s_bias, 16)
                sp.dma_start(w0[:], a["L0_ffn_weight"].rearrange("(c p) i -> p c i", p=P)).then_inc(s_bias, 16)
                sp.dma_start(bk_col[:], a["L1_xattn_b_k"].rearrange("(d o) -> d o", o=1)).then_inc(s_bias, 16)
                sp.dma_start(g_raw[:], a["L0_xattn_gamma_raw"].partition_broadcast(P)).then_inc(s_bias, 16)
                sp.dma_start(c.rows[:, ROW_BK, 0:DC], a["L1_xattn_b_k"].partition_broadcast(P)).then_inc(s_rows, 16)
                sp.dma_start(c.rows[:, ROW_BK, DC:P], a["L1_xattn_b_k"].partition_broadcast(P)).then_inc(s_rows, 16)
                for r, n in ((ROW_BO, "L0_attn_b_o"), (ROW_SCALE, "L0_ffn_scale"), (ROW_GAMMA, "L1_xattn_ln_gamma"), (ROW_BETA, "L1_xattn_ln_beta")):
                    sp.dma_start(c.rows[:, r], a[n].partition_broadcast(P)).then_inc(s_rows, 16)

            @block.tensor
            def _(pe):
                pe.wait_ge(s_const, 16)
                pe.wait_ge(s_ctx, 16)
                for h in range(2):
                    for t in range(4):
                        last = nc.tensor.transpose(bank[h][0:DC, t * P:(t + 1) * P], ctx_nat[:, 4 * h + t], c.ident[:])
                    last.then_inc(s_tr, 1)
                pe.wait_ge(s_w, 7 * 16)
                for i in range(3):
                    nc.tensor.transpose(bank[2][0:DC, i * DC:(i + 1) * DC], w_nat[:, i], c.ident[0:DC, 0:DC])
                nc.tensor.transpose(bank[2][:, 192:192 + 3 * HEADS], bias_nat[:], c.ident[0:3 * HEADS, 0:3 * HEADS])
                for k in range(KC):
                    last = nc.tensor.transpose(bank[2][:, 256 + k * EXPERTS0:256 + (k + 1) * EXPERTS0], r_nat[:, k * P:(k + 1) * P],
                                               c.ident[0:EXPERTS0, 0:EXPERTS0])
                last.then_inc(s_tr, 1)
                pe.wait_ge(s_x, 16)
                for k in range(KC):
                    for h in range(2):
                        for t in range(4):
                            last = nc.tensor.transpose(bank[3 + 2 * k + h][:, t * P:(t + 1) * P], c.x[:, 4 * h + t, k * P:(k + 1) * P], c.ident[:])
                        last.then_inc(s_tr, 1)
                pe.wait_ge(s_lo, 4)
                for i in range(3):
                    for h in range(2):
                        n = 2 * i + h
                        b = bank[(7, 0, 1, 2, 3, 4)[n]]
                        pe.wait_ge(s_lo, (4, 4, 4, 4, 5, 6)[n])
                        cols = slice(h * HALF, (h + 1) * HALF)
                        w_hi, w_lo = (w[:, i].rearrange("k a n -> k (a n)") for w in (wt_hi, wt_lo))
                        mm3(nc, b[:], w_hi, w_lo, ctxt_hi[:, cols], ctxt_lo[:, cols], True, True).then_inc(s_tr, 1)
                for h in range(2):
                    pe.wait_ge(s_lo, 7 + h)
                    w_hi, w_lo = (w[:, 2].rearrange("k a n -> k (a n)") for w in (wt_hi, wt_lo))
                    for t in range(4):
                        cols = slice((4 * h + t) * P, (4 * h + t + 1) * P)
                        last = mm3(nc, bank[5 + h][:, t * P:(t + 1) * P], ctxt_hi[:, cols], ctxt_lo[:, cols], w_hi, w_lo, True, True)
                    last.then_inc(s_tr, 1)
                pe.wait_ge(s_lo, 14)
                for b in range(B):
                    for h in range(2):
                        cols = slice(b * T + h * P, b * T + (h + 1) * P)
                        keys = slice(b * T, (b + 1) * T)
                        last = mm3(nc, bank[(7, 0, 1, 2)[b]][:, h * T:(h + 1) * T], qt_hi[:, cols], qt_lo[:, cols], kt_hi[:, keys], kt_lo[:, keys], True, True)
                    last.then_inc(s_tr, 1)

            @block.scalar
            def _(act):
                hi = Count(s_hi)
                for h in range(2):
                    act.wait_ge(s_tr, h + 1)
                    hi.inc(nc.scalar.activation(ctxt_hi[:, h * HALF:(h + 1) * HALF], bank[h][0:DC], ACT.Copy))
                act.wait_ge(s_tr, 3)
                small = bank[2][0:DC, 0:3 * DC].rearrange("k (i n) -> k i n", i=3)
                nc.scalar.activation(wt_hi[:, :, 0], small, ACT.Copy)
                nc.scalar.activation(wt_hi[:, :, 1], small, ACT.Copy)
                nc.scalar.activation(c.bias_t[:], bank[2][:, 192:192 + 3 * HEADS], ACT.Copy)
                hi.inc(nc.scalar.activation(c.rt_hi[:], bank[2][:, 256:256 + KC * EXPERTS0].rearrange("p (k e) -> p k e", k=KC), ACT.Copy))
                for n in range(4):
                    act.wait_ge(s_tr, 4 + n)
                    hi.inc(nc.scalar.activation(c.xt_hi[:, n // 2, (n % 2) * HALF:(n % 2 + 1) * HALF], bank[3 + n][:], ACT.Copy))
                act.wait_ge(s_const, 16)
                nc.scalar.activation(c.ident_bf[:], c.ident[:], ACT.Copy)
                act.wait_ge(s_bias, 64)
                nc.scalar.activation(c.causal[:], causal_f[:], ACT.Copy)
                g = nc.scalar.activation(g_exp[:], g_raw[:], ACT.Exp, scale=-1.0)
                hi.inc(g)
                for i in range(3):
                    for h in range(2):
                        n = 2 * i + h
                        act.wait_ge(s_tr, 8 + n)
                        b = bank[(7, 0, 1, 2, 3, 4)[n]]
                        dst = (qt_hi, kt_hi, c.kvt_hi)[i][:, h * HALF:(h + 1) * HALF]
                        if i < 2:
                            hi.inc(nc.scalar.activation(dst, b[0:DC], ACT.Copy))
                        else:
                            hi.inc(nc.scalar.activation(dst, b[0:DC], ACT.Identity, bias=bk_col[:]))
                for h in range(2):
                    act.wait_ge(s_lo, 15 + h)
                    hi.inc(nc.scalar.activation(c.kv_hi[:, 4 * h:4 * h + 4], kv[:, 4 * h:4 * h + 4], ACT.Copy))
                for b in range(B):
                    act.wait_ge(s_tr, 16 + b)
                    src = bank[(7, 0, 1, 2)[b]][:].rearrange("p (h n) -> p h n", h=2)
                    nc.scalar.activation(c.sim[:, 2 * b:2 * b + 2], src, ACT.Copy, scale=1.0 / 16)

            @block.vector
            def _(dve):
                lo = Count(s_lo)
                nc.vector.memset(c.half_neg[:], -0.5)
                nc.vector.memset(c.one[:], 1.0)
                for h in range(2):
                    dve.wait_ge(s_hi, h + 1)
                    cols = slice(h * HALF, (h + 1) * HALF)
                    lo.inc(nc.vector.tensor_tensor(ctxt_lo[:, cols], bank[h][0:DC], f32(ctxt_hi[:, cols]), ALU.subtract))
                dve.wait_ge(s_hi, 3)
                small = bank[2][0:DC, 0:3 * DC].rearrange("k (i n) -> k i n", i=3)
                nc.vector.tensor_tensor(wt_lo[:, :, 0], small, f32(wt_hi[:, :, 0]), ALU.subtract)
                lo.inc(nc.vector.tensor_tensor(wt_lo[:, :, 1], small, f32(wt_hi[:, :, 1]), ALU.subtract))
                lo.inc(nc.vector.tensor_tensor(c.rt_lo[:], bank[2][:, 256:256 + KC * EXPERTS0].rearrange("p (k e) -> p k e", k=KC),
                                               f32(c.rt_hi[:]), ALU.subtract))
                for n in range(4):
                    dve.wait_ge(s_hi, 4 + n)
                    cols = slice((n % 2) * HALF, (n % 2 + 1) * HALF)
                    lo.inc(nc.vector.tensor_tensor(c.xt_lo[:, n // 2, cols], bank[3 + n][:], f32(c.xt_hi[:, n // 2, cols]), ALU.subtract))
                for i in range(3):
                    for h in range(2):
                        n = 2 * i + h
                        dve.wait_ge(s_hi, 9 + n)
                        b = bank[(7, 0, 1, 2, 3, 4)[n]]
                        cols = slice(h * HALF, (h + 1) * HALF)
                        if i < 2:
                            lo.inc(nc.vector.tensor_tensor((qt_lo, kt_lo)[i][:, cols], b[0:DC], f32((qt_hi, kt_hi)[i][:, cols]), ALU.subtract))
                        else:
                            lo.inc(nc.vector.scalar_tensor_tensor(c.kvt_lo[:, cols], b[0:DC], bk_col[:], f32(c.kvt_hi[:, cols]), ALU.add, ALU.subtract))
                dve.wait_ge(s_rows, 6 * 16)
                for h in range(2):
                    dve.wait_ge(s_tr, 14 + h)
                    lo.inc(nc.vector.tensor_tensor(kv[:, 4 * h:4 * h + 4], bank[5 + h][:].rearrange("p (t n) -> p t n", t=4),
                                                   c.rows[:, ROW_BK, 0:P].unsqueeze(1).broadcast_to([P, 4, P]), ALU.add))
                for h in range(2):
                    dve.wait_ge(s_hi, 15 + h)
                    lo.inc(nc.vector.tensor_tensor(c.kv_lo[:, 4 * h:4 * h + 4], kv[:, 4 * h:4 * h + 4], f32(c.kv_hi[:, 4 * h:4 * h + 4]), ALU.subtract))
                dve.wait_ge(s_hi, 8)
                n = lo.inc(nc.vector.tensor_scalar(g_den[:], g_exp[:], 1.0, None, ALU.add))
                dve.wait_ge(s_lo, n)
                n = lo.inc(nc.vector.reciprocal(c.gamma[:], g_den[:]))
                dve.wait_ge(s_lo, n)
                lo.inc(nc.vector.tensor_scalar(c.one_less[:], c.gamma[:], -1.0, 2.0, ALU.mult, ALU.add))

            @block.gpsimd
            def _(pool):
                own = Count(s_pool)
                pool.wait_ge(s_bias, 64)
                n = own.inc(nc.gpsimd.tensor_scalar(w0b[:], w0[:], 2.0, 1.0, ALU.mult, ALU.min))
                pool.wait_ge(s_pool, n)
                n = own.inc(nc.gpsimd.tensor_scalar(w0[:], w0b[:], -1.0, 12582912.0, ALU.max, ALU.add))
                pool.wait_ge(s_pool, n)
                nc.gpsimd.tensor_scalar(c.tern[:], w0[:], -12582912.0, None, ALU.add)
                pool.wait_ge(s_rows, 6 * 16)
                pool.wait_ge(s_tr, 7)
                nc.gpsimd.tensor_tensor(c.x[:], c.x[:], c.rows[:, ROW_BO].unsqueeze(1).broadcast_to([P, NT, D]), ALU.add)


def attention(c, layer):
    nc, a = c.nc, c.a
    rope = layer == 1
    names = [f"L0_attn_w_{n}" for n in "qkvo"] if not rope else [f"L1_attn_W{n}" for n in "qkvo"]
    w_q, w_k, w_v = (a[n].rearrange("(k p) n -> p k n", p=P) for n in names[:3])
    w_o = a[names[3]].rearrange("(h d) n -> d h n", d=DH)
    KVC = DH if rope else GROUP * DH
    KH = KVC // DH

    def units(h):
        if rope and h % GROUP:
            return [("q", 0), ("q", 1)]
        return [("k", 0), ("k", 1), ("q", 0), ("q", 1)]

    PROJ_TO = [sum(len(units(i)) for i in range(h + 1)) for h in range(GROUP)]
    PROJ = PROJ_TO[-1]
    VU = 2 if rope else NT
    OU = NT // 2
    NEXT = len(units(0))
    RING = 3
    TAIL = NEXT + 2 + VU + OU
    U = PROJ + 2 * GROUP + VU + OU

    first, n = {}, 0
    for h in range(GROUP):
        if h:
            first["pv", h - 1] = n
            n += 2
        first["proj", h + 1] = n
        n += len(units(h + 1))
    for step, count in ((("pv", GROUP - 1), 2), ("v", VU), ("o", OU)):
        first[step] = n
        n += count
    assert n == U and U % RING == 0

    def number(g, step, u):
        return g * U + (TAIL + first[step] + u)

    def ring_bank(step, u):
        return c.banks[5 + (TAIL + first[step] + u) % RING]

    with ExitStack() as ctx:
        sb = lambda name, shape, dt=F32: ctx.enter_context(nc.sbuf_tensor(f"a{layer}_{name}", shape, dt))
        raw_q, raw_k, raw_v = sb("raw_q", [P, KC, GROUP * DH]), sb("raw_k", [P, KC, KVC]), sb("raw_v", [P, KC, KVC])
        raw_o = sb("raw_o", [DH, GROUP, D])
        wq_hi, wq_lo = sb("wq_hi", [P, KC, GROUP * DH], F32R), sb("wq_lo", [P, KC, GROUP * DH], F32R)
        wk_hi, wk_lo = sb("wk_hi", [P, KC, KVC], F32R), sb("wk_lo", [P, KC, KVC], F32R)
        wv_hi, wv_lo = sb("wv_hi", [P, KC, KVC], F32R), sb("wv_lo", [P, KC, KVC], F32R)
        wo_hi, wo_lo = sb("wo_hi", [DH, GROUP, D], F32R), sb("wo_lo", [DH, GROUP, D], F32R)
        q_hi, q_lo = sb("q_hi", [DH, NTOK], F32R), sb("q_lo", [DH, NTOK], F32R)
        k_hi, k_lo = sb("k_hi", [DH, NTOK], F32R), sb("k_lo", [DH, NTOK], F32R)
        v_hi, v_lo = sb("v_hi", [P, NT, KVC], F32R), sb("v_lo", [P, NT, KVC], F32R)
        probs = sb("probs", [P, 3, BANK])
        pt_hi, pt_lo = sb("pt_hi", [P, 3 * BANK], F32R), sb("pt_lo", [P, 3 * BANK], F32R)
        ot_hi, ot_lo = sb("ot_hi", [DH, GROUP, NTOK], F32R), sb("ot_lo", [DH, GROUP, NTOK], F32R)
        peak, neg_peak = sb("peak", [P, NT]), sb("neg_peak", [P, NT])
        row_sum, row_inv = sb("row_sum", [P, NT]), sb("row_inv", [P, NT])
        if rope:
            cos, sin = sb("cos", [P, T]), sb("sin", [P, T])
            scale_row = sb("scale_row", [P, HEADS])
            along, across, turned = (sb(n, [P, 2, HALF]) for n in ("along", "across", "turned"))
        else:
            work = [sb(f"work{i}", [P, T]) for i in range(2)]
            top8 = sb("top8", [P, 8])

        S = lambda name: c.sem(f"a{layer}_{name}")
        s_raw = {n: S(f"raw_{n}") for n in "qkvo"}
        s_table = S("table")
        s_split_proj, s_split_v, s_split_o = S("split_proj"), S("split_v"), S("split_o")
        s_pool = S("pool")
        s_proj, s_v, s_pv, s_o = S("proj"), S("v"), S("pv"), S("o")
        s_free = S("free")
        s_proj_hi, s_v_hi, s_pv_hi = S("proj_hi"), S("v_hi"), S("pv_hi")
        s_sum, s_rope = S("sum"), S("rope")
        s_scores, s_peak, s_exp, s_norm = S("scores"), S("peak"), S("exp"), S("norm")
        s_pt, s_pt_hi, s_pt_free = S("pt"), S("pt_hi"), S("pt_free")
        s_seen = S("seen")
        s_dve = S("dve")

        def scores_bank(b, q):
            return (0, b * P, P) if q == 0 else (1 + b // 2, (b % 2) * T, T)

        def proj_index(g, h, u):
            return (g + h // GROUP) * PROJ + ((PROJ_TO[h % GROUP - 1] if h % GROUP else 0) + u)

        with nc.Block() as block:
            @block.sync
            def _(sp):
                def load(n, dst, src, g):
                    width = {"q": GROUP * DH, "k": KVC, "v": KVC, "o": GROUP}[n]
                    part = src[:, bass.ds(g * GROUP, GROUP)] if n == "o" else src[:, :, bass.ds(g * width, width)]
                    sp.dma_start(dst[:], part).then_inc(s_raw[n], 16)

                for n, dst, src in (("q", raw_q, w_q), ("k", raw_k, w_k), ("v", raw_v, w_v), ("o", raw_o, w_o)):
                    load(n, dst, src, 0)
                if rope:
                    sp.dma_start(cos[:], a["cos"]).then_inc(s_table, 16)
                    sp.dma_start(sin[:], a["sin"]).then_inc(s_table, 16)
                    sp.dma_start(scale_row[:], a["L1_attn_head_scale"].rearrange("a h b c -> (a h b c)").partition_broadcast(P)).then_inc(s_table, 16)
                with sp.Fori(0, GROUPS - 1) as g:
                    sp.wait_ge(s_split_v, g + 1)
                    load("v", raw_v, w_v, g + 1)
                    sp.wait_ge(s_split_proj, g * GROUP + GROUP)
                    load("q", raw_q, w_q, g + 1)
                    load("k", raw_k, w_k, g + 1)
                    sp.wait_ge(s_split_o, g + 1)
                    load("o", raw_o, w_o, g + 1)

            @block.gpsimd
            def _(pool):
                own = Count(s_pool)

                def split(parts, done):
                    for hi, lo, raw in parts:
                        n = own.inc(nc.gpsimd.tensor_tensor(hi, raw, c.one[:].unsqueeze(1).broadcast_to(list(raw.shape)), ALU.mult))
                    pool.wait_ge(s_pool, n)
                    for hi, lo, raw in parts:
                        last = nc.gpsimd.tensor_tensor(lo, raw, f32(hi), ALU.subtract)
                    last.then_inc(done, 1)

                def split_proj(g, h):
                    pool.wait_ge(s_raw["q"], (g + h // GROUP) * 16 + 16)
                    pool.wait_ge(s_proj, proj_index(g, h, len(units(h))))
                    s = slice((h % GROUP) * DH, (h % GROUP + 1) * DH)
                    parts = [(wq_hi[:, :, s], wq_lo[:, :, s], raw_q[:, :, s])]
                    if ("k", 0) in units(h):
                        pool.wait_ge(s_raw["k"], (g + h // GROUP) * 16 + 16)
                        s = slice((h % KH) * DH, (h % KH + 1) * DH)
                        parts.append((wk_hi[:, :, s], wk_lo[:, :, s], raw_k[:, :, s]))
                    split(parts, s_split_proj)

                def split_v(g):
                    pool.wait_ge(s_raw["v"], g * 16 + 16)
                    pool.wait_ge(s_v, g * VU + VU)
                    split([(wv_hi[:], wv_lo[:], raw_v[:])], s_split_v)

                def rope_units(g, h):
                    for u, (what, half) in enumerate(units(h)):
                        n = proj_index(g, h, u)
                        hi, lo = (q_hi, q_lo) if what == "q" else (k_hi, k_lo)
                        cols = slice(half * HALF, (half + 1) * HALF)
                        pool.wait_ge(s_free, number(g, ("proj", h), u) + (RING + 1))
                        if not (isinstance(g, int) and g < 0 and u < 2):
                            pool.wait_ge(s_rope, n - 1)
                        nc.gpsimd.tensor_tensor(turned[:, u % 2], along[:, u % 2], across[:, u % 2], ALU.add).then_inc(s_sum, 1)
                        pool.wait_ge(s_proj_hi, n + 1)
                        nc.gpsimd.tensor_tensor(lo[:, cols], turned[:, u % 2], f32(hi[:, cols]), ALU.subtract).then_inc(s_rope, 1)

                split_proj(-1, GROUP)
                split_v(0)
                if rope:
                    rope_units(-1, GROUP)

                def turn(g, more):
                    for h in range(1, GROUP + 1):
                        if h < GROUP:
                            split_proj(g, h)
                        else:
                            pool.wait_ge(s_raw["o"], g * 16 + 16)
                            pool.wait_ge(s_o, g * OU + OU)
                            split([(wo_hi[:], wo_lo[:], raw_o[:])], s_split_o)
                        if rope and h > 1:
                            rope_units(g, h - 1)
                    if more:
                        split_proj(g, GROUP)
                        split_v(g + 1)
                        if rope:
                            rope_units(g, GROUP)

                with pool.Fori(0, GROUPS - 1) as g:
                    own.enter(g, GROUP + KH + 2)
                    turn(g, True)
                own.leave(GROUPS - 1)
                turn(GROUPS - 1, False)

            @block.tensor
            def _(pe):
                pe.sem_inc(s_proj, PROJ)
                pe.sem_inc(s_v, VU)
                pe.sem_inc(s_o, OU)

                def claim(g, step, u):
                    pe.wait_ge(s_free, number(g, step, u) + 1)
                    return ring_bank(step, u)

                def proj(g, h):
                    pe.wait_ge(s_split_proj, g * GROUP + (h + 1))
                    for u, (what, half) in enumerate(units(h)):
                        bank = claim(g, ("proj", h), u)
                        hi, lo = (wq_hi, wq_lo) if what == "q" else (wk_hi, wk_lo)
                        s = (h % (GROUP if what == "q" else KH)) * DH
                        cols = slice(half * HALF, (half + 1) * HALF)
                        for k in range(KC):
                            last = mm3(nc, bank[:], hi[:, k, s:s + DH], lo[:, k, s:s + DH], c.xt_hi[:, k, cols], c.xt_lo[:, k, cols], k == 0, k == KC - 1)
                        last.then_inc(s_proj, 1)

                def values(g):
                    pe.wait_ge(s_split_v, g + 2)
                    per = NT // VU
                    for u in range(VU):
                        bank = claim(g, "v", u)
                        for i in range(per):
                            t = u * per + i
                            cols = slice(t * P, (t + 1) * P)
                            for k in range(KC):
                                last = mm3(nc, bank[:, i * KVC:(i + 1) * KVC], c.xt_hi[:, k, cols], c.xt_lo[:, k, cols], wv_hi[:, k], wv_lo[:, k],
                                           k == 0, k == KC - 1)
                        last.then_inc(s_v, 1)

                def scores(g, h):
                    if rope:
                        pe.wait_ge(s_rope, proj_index(g, h, len(units(h))))
                    elif h:
                        pe.wait_ge(s_free, number(g, ("proj", h), len(units(h)) - 1) + (RING + 1))
                    else:
                        pe.wait_ge(s_free, number(g, ("proj", GROUP), len(units(0)) - 1) + (RING + 1 - U))
                    pe.wait_ge(s_exp, g * (GROUP * NT) + (h + 1) * NT)
                    for q in range(2):
                        for b in range(B):
                            i, at, width = scores_bank(b, q)
                            out = c.banks[i][:, at:at + width]
                            rows = slice(b * T + q * P, b * T + (q + 1) * P)
                            cols = slice(b * T, b * T + width)
                            mm3(nc, out, q_hi[:, rows], q_lo[:, rows], k_hi[:, cols], k_lo[:, cols], True, False)
                            last = nc.tensor.matmul(out[:, width - P:], c.ident_bf[:], c.causal[:], start=False, stop=True)
                            if at + width == BANK:
                                last.then_inc(s_scores, 1)

                def transposes(g, h):
                    for slot in range(3 * B):
                        b, j = slot // 3, slot % 3
                        bank = 3 + (3 * h + slot // 4) % 2
                        if slot % 4 == 0:
                            pe.wait_ge(s_pt_free, g * (3 * GROUP) + (3 * h + slot // 4 + 1))
                        if j == 0:
                            pe.wait_ge(s_norm, g * (GROUP * B) + (h * B + b + 1))
                        i, at, width = scores_bank(b, min(j, 1))
                        at += P if j == 2 else 0
                        last = nc.tensor.transpose(c.banks[bank][:, slot % 4 * P:(slot % 4 + 1) * P], probs[:, i, at:at + P], c.ident[:])
                        if slot % 4 == 3:
                            last.then_inc(s_pt, 1)

                def pv(g, h):
                    pe.wait_ge(s_free, number(g, "v", VU - 1) + (RING + 1 - U))
                    for half in range(2):
                        bank = claim(g, ("pv", h), half)
                        for i in range(2):
                            b = 2 * half + i
                            pe.wait_ge(s_pt_free, g * (3 * GROUP) + (3 * h + (3 * b + 2) // 4 + 1 + 2))
                            at = 3 * b * P
                            s = slice((h % KH) * DH, (h % KH + 1) * DH)
                            out = bank[:, i * T:(i + 1) * T]
                            mm3(nc, out, v_hi[:, 2 * b, s], v_lo[:, 2 * b, s], pt_hi[:, at:at + T], pt_lo[:, at:at + T], True, False)
                            last = mm3(nc, out[:, P:], v_hi[:, 2 * b + 1, s], v_lo[:, 2 * b + 1, s], pt_hi[:, at + T:at + T + P], pt_lo[:, at + T:at + T + P],
                                       False, True)
                        last.then_inc(s_pv, 1)

                def output(g):
                    pe.wait_ge(s_split_o, g + 1)
                    pe.wait_ge(s_free, number(g, ("pv", GROUP - 1), 1) + (RING + 1))
                    for u in range(OU):
                        bank = claim(g, "o", u)
                        for i in range(2):
                            cols = slice((2 * u + i) * P, (2 * u + i + 1) * P)
                            for h in range(GROUP):
                                last = mm3(nc, bank[:, i * D:(i + 1) * D], ot_hi[:, h, cols], ot_lo[:, h, cols], wo_hi[:, h], wo_lo[:, h],
                                           h == 0, h == GROUP - 1)
                        last.then_inc(s_o, 1)

                def turn(g, more):
                    for h in range(GROUP):
                        scores(g, h)
                        if h:
                            pv(g, h - 1)
                        if more or h + 1 < GROUP:
                            proj(g, h + 1)
                        transposes(g, h)
                    pv(g, GROUP - 1)
                    if more:
                        values(g)
                    output(g)

                proj(-1, GROUP)
                values(-1)
                with pe.Fori(0, GROUPS - 1) as g:
                    turn(g, True)
                turn(GROUPS - 1, False)

            @block.scalar
            def _(act):
                act.sem_inc(s_exp, NT)

                def proj(g, h, u):
                    n = proj_index(g, h, u)
                    what, half = units(h)[u]
                    cols = slice(half * HALF, (half + 1) * HALF)
                    dst = (q_hi if what == "q" else k_hi)[:, cols]
                    if rope:
                        act.wait_ge(s_sum, n + 1)
                        nc.scalar.activation(dst, turned[:, u % 2], ACT.Copy).then_inc(s_proj_hi, 1)
                    else:
                        act.wait_ge(s_proj, n + (PROJ + 1))
                        act.sem_inc(s_seen, 1)
                        head = g * GROUP + (h + (0 if what == "q" else HEADS))
                        nc.scalar.activation(dst, ring_bank(("proj", h), u)[:], ACT.Identity,
                                             bias=c.bias_t[:, bass.ds(head, 1)]).then_inc(s_proj_hi, 1)

                def values(g):
                    per = NT // VU
                    for u in range(VU):
                        act.wait_ge(s_v, (g + 1) * VU + (VU + u + 1))
                        nc.scalar.activation(v_hi[:, u * per:(u + 1) * per].rearrange("p t n -> p (t n)"), ring_bank("v", u)[:], ACT.Copy).then_inc(s_v_hi, 1)

                def exps(g, h):
                    for q in range(2):
                        for b in range(B):
                            i, at, width = scores_bank(b, q)
                            if at == 0:
                                act.wait_ge(s_peak, g * (3 * GROUP) + (3 * h + i + 1))
                            n = q * B + b
                            nc.scalar.activation(probs[:, i, at:at + width], c.banks[i][:, at:at + width], ACT.Exp, bias=neg_peak[:, n:n + 1],
                                                 scale=SCALE, accum_out=row_sum[:, n:n + 1]).then_inc(s_exp, 1)

                def pt(g, h):
                    for i in range(3):
                        act.wait_ge(s_pt, g * (3 * GROUP) + (3 * h + i + 1))
                        nc.scalar.activation(pt_hi[:, i * BANK:(i + 1) * BANK], c.banks[3 + (3 * h + i) % 2][:], ACT.Copy).then_inc(s_pt_hi, 1)

                def pv(g, h):
                    for half in range(2):
                        act.wait_ge(s_pv, g * (2 * GROUP) + (2 * h + half + 1))
                        act.sem_inc(s_seen, 1)
                        dst, src = ot_hi[:, h, half * HALF:(half + 1) * HALF], ring_bank(("pv", h), half)[:]
                        if rope:
                            last = nc.scalar.activation(dst, src, ACT.Copy, scale=scale_row[:, bass.ds(g * GROUP + h, 1)])
                        else:
                            last = nc.scalar.activation(dst, src, ACT.Identity, bias=c.bias_t[:, bass.ds(g * GROUP + (h + 2 * HEADS), 1)])
                        last.then_inc(s_pv_hi, 1)

                def turn(g, more):
                    for h in range(GROUP):
                        exps(g, h)
                        if h:
                            pv(g, h - 1)
                        if more or h + 1 < GROUP:
                            for u in range(len(units(h + 1))):
                                proj(g, h + 1, u)
                        pt(g, h)
                    pv(g, GROUP - 1)
                    if more:
                        values(g)

                if rope:
                    act.wait_ge(s_table, 48)
                for u in range(NEXT):
                    proj(-1, GROUP, u)
                values(-1)
                with act.Fori(0, GROUPS - 1) as g:
                    turn(g, True)
                turn(GROUPS - 1, False)

            @block.vector
            def _(dve):
                own = Count(s_dve)
                dve.sem_inc(s_free, RING)
                dve.sem_inc(s_pt_free, 2)

                def proj(g, h, u):
                    n = proj_index(g, h, u)
                    what, half = units(h)[u]
                    cols = slice(half * HALF, (half + 1) * HALF)
                    bank = ring_bank(("proj", h), u)
                    if rope:
                        dve.wait_ge(s_proj, n + (PROJ + 1))
                        two = lambda ap: ap.rearrange("p (b t) -> p b t", b=2)
                        many = lambda ap, size: ap.unsqueeze(1).broadcast_to([size, 2, T])
                        if not (isinstance(g, int) and g < 0 and u < 2):
                            dve.wait_ge(s_sum, n - 1)
                        nc.vector.tensor_tensor(two(along[:, u % 2]), two(bank[:]), many(cos[:], P), ALU.mult)
                        for to, at in ((0, HALF_BLOCK), (HALF_BLOCK, 0)):
                            last = nc.vector.tensor_tensor(two(across[to:to + HALF_BLOCK, u % 2]), two(bank[at:at + HALF_BLOCK]),
                                                           many(sin[at:at + HALF_BLOCK], HALF_BLOCK), ALU.mult)
                        last.then_inc(s_free, 1)
                    else:
                        dve.wait_ge(s_proj_hi, n + 1)
                        hi, lo = (q_hi, q_lo) if what == "q" else (k_hi, k_lo)
                        head = g * GROUP + (h + (0 if what == "q" else HEADS))
                        nc.vector.scalar_tensor_tensor(lo[:, cols], bank[:], c.bias_t[:, bass.ds(head, 1)], f32(hi[:, cols]),
                                                       ALU.add, ALU.subtract).then_inc(s_free, 1)

                def values(g):
                    per = NT // VU
                    for u in range(VU):
                        dve.wait_ge(s_v_hi, (g + 1) * VU + (u + 1))
                        flat = lambda v: v[:, u * per:(u + 1) * per].rearrange("p t n -> p (t n)")
                        nc.vector.tensor_tensor(flat(v_lo), ring_bank("v", u)[:], f32(flat(v_hi)), ALU.subtract).then_inc(s_free, 1)

                def peaks(g, h):
                    for i in range(3):
                        dve.wait_ge(s_scores, g * (3 * GROUP) + (3 * h + i + 1))
                        n, rows = (0, B) if i == 0 else (B + 2 * (i - 1), 2)
                        done = own.inc(nc.vector.tensor_reduce(peak[:, n:n + rows], c.banks[i][:].rearrange("p (r k) -> p r k", r=rows), AX.X, ALU.max))
                        dve.wait_ge(s_dve, done)
                        nc.vector.tensor_scalar(neg_peak[:, n:n + rows], peak[:, n:n + rows], -SCALE, None, ALU.mult).then_inc(s_peak, 1)

                def norm(g, h):
                    dve.wait_ge(s_exp, g * (GROUP * NT) + ((h + 2) * NT))
                    done = own.inc(nc.vector.reciprocal(row_inv[:], row_sum[:]))
                    dve.wait_ge(s_dve, done)
                    for b in range(B):
                        for q in range(2):
                            i, at, width = scores_bank(b, q)
                            part = probs[:, i, at:at + width]
                            last = nc.vector.tensor_scalar(part, part, row_inv[:, q * B + b:q * B + b + 1], None, ALU.mult)
                        last.then_inc(s_norm, 1)

                def pt(g, h):
                    for i in range(3):
                        dve.wait_ge(s_pt_hi, g * (3 * GROUP) + (3 * h + i + 1))
                        cols = slice(i * BANK, (i + 1) * BANK)
                        nc.vector.tensor_tensor(pt_lo[:, cols], c.banks[3 + (3 * h + i) % 2][:], f32(pt_hi[:, cols]), ALU.subtract).then_inc(s_pt_free, 1)

                def pv(g, h):
                    for half in range(2):
                        dve.wait_ge(s_pv_hi, g * (2 * GROUP) + (2 * h + half + 1))
                        cols = slice(half * HALF, (half + 1) * HALF)
                        if rope:
                            factor, op = scale_row[:, bass.ds(g * GROUP + h, 1)], ALU.mult
                        else:
                            factor, op = c.bias_t[:, bass.ds(g * GROUP + (h + 2 * HEADS), 1)], ALU.add
                        nc.vector.scalar_tensor_tensor(ot_lo[:, h, cols], ring_bank(("pv", h), half)[:], factor, f32(ot_hi[:, h, cols]),
                                                       op, ALU.subtract).then_inc(s_free, 1)

                def output(g):
                    for u in range(OU):
                        dve.wait_ge(s_o, g * OU + (OU + u + 1))
                        rows = c.x[:, 2 * u:2 * u + 2].rearrange("p t n -> p (t n)")
                        nc.vector.tensor_tensor(rows, rows, ring_bank("o", u)[:], ALU.add).then_inc(s_free, 1)

                def skip(g, step, count):
                    dve.wait_ge(s_free, number(g, step, 0) + RING)
                    dve.sem_inc(s_free, count)

                def threshold(g, h):
                    tile = g * 2 + h // 2
                    rounds = -(-KEEP // 8)
                    if h % 2 == 0:
                        nc.vector.tensor_copy(work[0][:], c.sim[:, bass.ds(tile, 1)].rearrange("p t n -> p (t n)"))
                        dve.drain()
                    for r in range(h % 2 * rounds // 2, (h % 2 + 1) * rounds // 2):
                        nc.vector.max(top8[:], work[r % 2][:])
                        dve.drain()
                        if r < rounds - 1:
                            nc.vector.match_replace(work[1 - r % 2][:], top8[:], work[r % 2][:], -3e38)
                        else:
                            nc.vector.tensor_copy(c.thr[:, bass.ds(tile, 1)], top8[:, (KEEP - 1) % 8:(KEEP - 1) % 8 + 1])
                        dve.drain()

                def turn(g, more):
                    for h in range(GROUP):
                        peaks(g, h)
                        if not rope:
                            threshold(g, h)
                        if h:
                            pv(g, h - 1)
                        if more or h + 1 < GROUP:
                            count = len(units(h + 1))
                            for u in range(count):
                                proj(g, h + 1, u)
                                if u == count // 2 - 1:
                                    norm(g, h)
                        else:
                            norm(g, h)
                            skip(g, ("proj", h + 1), NEXT)
                        pt(g, h)
                    pv(g, GROUP - 1)
                    if more:
                        values(g)
                    else:
                        skip(g, "v", VU)
                    output(g)

                if rope:
                    dve.wait_ge(s_table, 48)
                for u in range(NEXT):
                    proj(-1, GROUP, u)
                skip(-1, ("pv", GROUP - 1), 2)
                values(-1)
                skip(-1, "o", OU)
                per_turn = GROUP * 4
                with dve.Fori(0, GROUPS - 1) as g:
                    own.enter(g, per_turn)
                    turn(g, True)
                own.leave(GROUPS - 1)
                turn(GROUPS - 1, False)


class Norm:

    def __init__(self, c, name, sb):
        self.c, self.nc = c, c.nc
        self.stats, self.mv = sb(f"{name}_stats", [P, NT, 6]), sb(f"{name}_mv", [P, NT, 2])
        self.shifted, self.rstd = sb(f"{name}_shifted", [P, NT]), sb(f"{name}_rstd", [P, NT])
        self.s_var, self.s_eps, self.s_rstd = (c.sem(f"{name}_{n}") for n in ("var", "eps", "rstd"))

    def moments(self, dve, tiles):
        for t in range(NT):
            self.nc.vector.bn_stats(self.stats[:, t], tiles(t))
        dve.drain()
        for t in range(NT):
            last = self.nc.vector.bn_aggr(self.mv[:, t], self.stats[:, t])
        last.then_inc(self.s_var, 1)

    def root(self, pool, factor=1.0, eps=EPS):
        pool.wait_ge(self.s_var, 1)
        self.nc.gpsimd.tensor_scalar(self.shifted[:], self.mv[:, :, 1], factor, eps, ALU.mult, ALU.add).then_inc(self.s_eps, 1)
        pool.wait_ge(self.s_eps, 1)
        self.nc.gpsimd.tensor_tensor(self.rstd[:], self.shifted[:], self.c.half_neg[:], ALU.pow).then_inc(self.s_rstd, 1)

    def apply(self, dve, t, dst, src):
        if t == 0:
            dve.wait_ge(self.s_rstd, 1)
        return self.nc.vector.tensor_scalar(dst, src, self.mv[:, t, 0:1], self.rstd[:, t:t + 1], ALU.subtract, ALU.mult)


class Transposed:

    def __init__(self, c, name):
        self.c, self.nc = c, c.nc
        self.s_tr, self.s_hi, self.s_lo = (c.sem(f"{name}_{n}") for n in ("tr", "hi", "lo"))
        self.order = [(h, k) for h in range(2) for k in range(KC)]

    def pe(self, pe, s_ready, per_half):
        for n, (h, k) in enumerate(self.order):
            pe.wait_ge(s_ready, per_half * (h + 1))
            for t in range(4):
                last = self.nc.tensor.transpose(self.c.banks[4 + n][:, t * P:(t + 1) * P], self.c.x[:, 4 * h + t, k * P:(k + 1) * P], self.c.ident[:])
            last.then_inc(self.s_tr, 1)

    def act(self, act):
        for n, (h, k) in enumerate(self.order):
            act.wait_ge(self.s_tr, n + 1)
            self.nc.scalar.activation(self.c.xt_hi[:, k, h * HALF:(h + 1) * HALF], self.c.banks[4 + n][:], ACT.Copy).then_inc(self.s_hi, 1)

    def dve(self, dve):
        for n, (h, k) in enumerate(self.order):
            dve.wait_ge(self.s_hi, n + 1)
            cols = slice(h * HALF, (h + 1) * HALF)
            self.nc.vector.tensor_tensor(self.c.xt_lo[:, k, cols], self.c.banks[4 + n][:], f32(self.c.xt_hi[:, k, cols]), ALU.subtract).then_inc(self.s_lo, 1)

    def wait(self, pe, half=1):
        pe.wait_ge(self.s_lo, KC * (half + 1))


def route(c, out, w_hi, w_lo, experts):
    for t in range(NT):
        cols = slice(t * P, (t + 1) * P)
        for k in range(KC):
            last = mm3(c.nc, out[:, t * experts:(t + 1) * experts], c.xt_hi[:, k, cols], c.xt_lo[:, k, cols], w_hi[:, k], w_lo[:, k], k == 0, k == KC - 1)
    return last


def graph_and_masked_experts(c, upto):
    nc, a = c.nc, c.a
    PAIRS = EXPERTS0 // 2
    RING = 4
    with ExitStack() as ctx:
        sb = lambda name, shape, dt=F32: ctx.enter_context(nc.sbuf_tensor(f"b_{name}", shape, dt))
        norm1, norm2, norm3 = (Norm(c, f"b_norm{i}", sb) for i in (1, 2, 3))
        turned2, turned3 = Transposed(c, "b_turned2"), Transposed(c, "b_turned3")
        gate_in = sb("gate_in", [P, NT, T])
        kept, mixed = sb("kept", [P, NT, T]), sb("mixed", [P, NT, T])
        quarter = sb("quarter", [P, 1])
        top, above, likely = sb("top", [P, NT]), sb("above", [P, NT, EXPERTS0]), sb("likely", [P, NT, EXPERTS0])
        total, weight = sb("total", [P, NT]), sb("weight", [P, NT])
        numbers, found, first = sb("numbers", [P, NT, EXPERTS0]), sb("found", [P, NT, EXPERTS0]), sb("first", [P, NT])
        chosen, gate = sb("chosen", [P, NT, EXPERTS0]), sb("gate", [P, NT, EXPERTS0])
        raw = [sb(f"raw{i}", [P, 2, KC, D]) for i in range(2)]
        masked = [sb(f"masked{i}", [P, 2, KC, D], BF16) for i in range(2)]
        w = [sb(f"w{i}", [P, KC, 2 * D], F32R) for i in range(2)]
        acc = [sb(f"acc{i}", [P, NT, D]) for i in range(2)]

        S = lambda name: c.sem(f"b_{name}")
        s_numbers, s_raw = S("numbers"), [S(f"raw{i}") for i in range(2)]
        s_tanh, s_kept, s_kept_t = S("tanh"), S("kept"), S("kept_t")
        s_mixed, s_norm1, s_norm2, s_norm3 = S("mixed"), S("norm1"), S("norm2"), S("norm3")
        s_logits, s_above, s_likely, s_acc0 = S("logits"), S("above"), S("likely"), S("acc0")
        s_masked, s_turned, s_w = S("masked"), S("turned"), S("w")
        s_out, s_used = S("out"), S("used")

        def raw_of(pair):
            masks = a["L0_ffn_expert_masks"].rearrange("(n e) (k p) i -> n p e k i", e=2, p=P)
            return masks[bass.ds(pair, 1)].rearrange("n p e k i -> p (n e) k i")

        with nc.Block() as block:
            @block.sync
            def _(sp):
                sp.dma_start(numbers[:], a["numbers"]).then_inc(s_numbers, 16)

                def load(i, j):
                    pair = i * 2 + j
                    sp.wait_ge(s_masked, pair + 1)
                    for e in range(2):
                        sp.dma_start(raw[j][:, e], a["L0_ffn_expert_masks"][bass.ds(pair * 2 + e, 1)].rearrange("n (k p) i -> p (n k) i", p=P)).then_inc(s_raw[j], 16)

                with sp.Fori(0, PAIRS // 2) as i:
                    load(i, 0)
                    load(i, 1)

            @block.gpsimd
            def _(pool):
                pool.sem_inc(s_masked, 2)
                for x in acc:
                    last = nc.gpsimd.memset(x[:], 0.0)
                last.then_inc(s_acc0, 1)
                norm1.root(pool)
                norm2.root(pool)

                def mask(i, j):
                    pair = i * 2 + j
                    pool.wait_ge(s_raw[j], i * 32 + 32)
                    pool.wait_ge(s_turned, pair + 1)
                    wide = c.tern[:].unsqueeze(1).broadcast_to([P, 2, KC, D])
                    nc.gpsimd.tensor_tensor(masked[j][:], raw[j][:], wide, ALU.mult).then_inc(s_masked, 1)

                with pool.Fori(0, PAIRS // 2) as i:
                    mask(i, 0)
                    mask(i, 1)
                norm3.root(pool)

            @block.tensor
            def _(pe):
                pe.sem_inc(s_turned, 2)
                pe.sem_inc(s_out, 2 * NT)
                for b in range(B):
                    pe.wait_ge(s_kept, b + 1)
                    for i in range(2):
                        for j in range(2):
                            last = nc.tensor.transpose(c.banks[b][:, i * T + j * P:i * T + (j + 1) * P], kept[:, 2 * b + j, i * P:(i + 1) * P], c.ident[:])
                    last.then_inc(s_kept_t, 1)
                turned2.pe(pe, s_norm2, 4)
                turned2.wait(pe)
                pe.wait_ge(s_mixed, 1)
                route(c, c.banks[0], c.rt_hi, c.rt_lo, EXPERTS0).then_inc(s_logits, 1)

                def turn(i, j):
                    pair = i * 2 + j
                    pe.wait_ge(s_masked, pair + 3)
                    pe.wait_ge(s_w, pair + 1)
                    bank = c.banks[6 + j][:].bitcast(BF16)
                    for k in range(KC):
                        for e in range(2):
                            for o in range(KC):
                                at = k * 2 * D + e * D + o * P
                                last = nc.tensor.transpose(bank[:, at:at + P], masked[j][:, e, o, k * P:(k + 1) * P], c.ident_bf[:])
                    last.then_inc(s_turned, 1)

                def products(i, j):
                    pair = i * 2 + j
                    pe.wait_ge(s_w, pair + 3)
                    for t in range(NT):
                        pe.wait_ge(s_used, i * (2 * NT) + (j * NT + t + 1))
                        out = c.banks[t % RING][:]
                        cols = slice(t * P, (t + 1) * P)
                        for k in range(KC):
                            nc.tensor.matmul(out, c.xt_hi[:, k, cols], w[j][:, k], start=k == 0, stop=False)
                            last = nc.tensor.matmul(out, c.xt_lo[:, k, cols], w[j][:, k], start=False, stop=k == KC - 1)
                        last.then_inc(s_out, 1)

                turned2.wait(pe)
                turn(0, 0)
                pe.wait_ge(s_above, 1)
                with pe.Fori(0, PAIRS // 2 - 1) as i:
                    turn(i, 1)
                    products(i, 0)
                    turn(i + 1, 0)
                    products(i, 1)
                turn(PAIRS // 2 - 1, 1)
                products(PAIRS // 2 - 1, 0)
                products(PAIRS // 2 - 1, 1)
                turned3.pe(pe, s_norm3, 4)

            @block.scalar
            def _(act):
                act.sem_inc(s_w, 2)
                nc.scalar.activation(gate_in[:], c.sim[:], ACT.Tanh, scale=0.5).then_inc(s_tanh, 1)
                turned2.act(act)
                act.wait_ge(s_above, 1)
                nc.scalar.activation(likely[:], above[:], ACT.Exp).then_inc(s_likely, 1)

                def weights(i, j):
                    pair = i * 2 + j
                    act.wait_ge(s_turned, pair + 3)
                    act.wait_ge(s_out, i * (2 * NT) + (j * NT + NT))
                    nc.scalar.activation(w[j][:].rearrange("p k n -> p (k n)"), c.banks[6 + j][:].bitcast(BF16), ACT.Copy).then_inc(s_w, 1)

                with act.Fori(0, PAIRS // 2) as i:
                    weights(i, 0)
                    weights(i, 1)
                turned3.act(act)

            @block.vector
            def _(dve):
                dve.sem_inc(s_used, RING)
                nc.vector.tensor_scalar(quarter[:], c.gamma[:], 0.25, None, ALU.mult)
                dve.wait_ge(s_tanh, 1)
                nc.vector.tensor_scalar(gate_in[:], gate_in[:], 1.0, None, ALU.add)
                dve.drain()
                for t in range(NT):
                    last = nc.vector.scalar_tensor_tensor(kept[:, t], c.sim[:, t], c.thr[:, t:t + 1], gate_in[:, t], ALU.is_ge, ALU.mult)
                    if t % 2:
                        last.then_inc(s_kept, 1)
                norm1.moments(dve, lambda t: c.x[:, t])
                for b in range(B):
                    dve.wait_ge(s_kept_t, b + 1)
                    rows = lambda v: v[:, 2 * b:2 * b + 2].rearrange("p t n -> p (t n)")
                    nc.vector.tensor_tensor(rows(mixed), rows(kept), c.banks[b][:], ALU.add)
                dve.drain()
                nc.vector.tensor_scalar(mixed[:], mixed[:], quarter[:], None, ALU.mult).then_inc(s_mixed, 1)
                for t in range(NT):
                    norm1.apply(dve, t, c.x[:, t], c.x[:, t])
                dve.drain()
                for t in range(NT):
                    nc.vector.scalar_tensor_tensor(c.x[:, t], c.x[:, t], c.one_less[:], mixed[:, t], ALU.mult, ALU.add)
                dve.drain()
                norm2.moments(dve, lambda t: c.x[:, t])
                for t in range(NT):
                    norm2.apply(dve, t, c.x[:, t], c.x[:, t]).then_inc(s_norm2, 1)
                turned2.dve(dve)

                dve.wait_ge(s_logits, 1)
                logits = c.banks[0][:, 0:NT * EXPERTS0].rearrange("p (t e) -> p t e", t=NT)
                wide = lambda v: v[:].unsqueeze(2).broadcast_to([P, NT, EXPERTS0])
                nc.vector.tensor_reduce(top[:], logits, AX.X, ALU.max)
                dve.drain()
                nc.vector.tensor_tensor(above[:], logits, wide(top), ALU.subtract).then_inc(s_above, 1)
                dve.drain()
                nc.vector.tensor_scalar(found[:], above[:], 0.0, -float(EXPERTS0), ALU.is_ge, ALU.mult)
                dve.wait_ge(s_numbers, 16)
                dve.drain()
                nc.vector.tensor_tensor(found[:], found[:], numbers[:], ALU.add)
                dve.drain()
                nc.vector.tensor_reduce(first[:], found[:], AX.X, ALU.min)
                dve.drain()
                nc.vector.tensor_scalar(first[:], first[:], float(EXPERTS0), None, ALU.add)
                dve.drain()
                nc.vector.tensor_tensor(chosen[:], numbers[:], wide(first), ALU.is_equal)
                dve.wait_ge(s_likely, 1)
                nc.vector.tensor_reduce(total[:], likely[:], AX.X, ALU.add)
                dve.drain()
                nc.vector.reciprocal(weight[:], total[:])
                dve.drain()
                nc.vector.tensor_tensor(gate[:], chosen[:], wide(weight), ALU.mult)
                dve.wait_ge(s_acc0, 1)
                dve.drain()
                flat = gate[:].rearrange("p t e -> p (t e)")

                def add(i, j):
                    for t in range(NT):
                        dve.wait_ge(s_out, i * (2 * NT) + (2 * NT + j * NT + t + 1))
                        for e in range(2):
                            g = flat[:, bass.ds(i * 4 + (t * EXPERTS0 + 2 * j + e), 1)]
                            last = nc.vector.scalar_tensor_tensor(acc[e][:, t], c.banks[t % RING][:, e * D:(e + 1) * D], g, acc[e][:, t], ALU.mult, ALU.add)
                        last.then_inc(s_used, 1)

                with dve.Fori(0, PAIRS // 2) as i:
                    add(i, 0)
                    add(i, 1)
                dve.drain()
                nc.vector.tensor_tensor(acc[0][:], acc[0][:], acc[1][:], ALU.add)
                dve.drain()
                nc.vector.tensor_tensor(acc[0][:], acc[0][:], c.rows[:, ROW_SCALE].unsqueeze(1).broadcast_to([P, NT, D]), ALU.mult)
                dve.drain()
                nc.vector.tensor_tensor(c.x[:], c.x[:], acc[0][:], ALU.add)
                dve.drain()
                norm3.moments(dve, lambda t: c.x[:, t])
                for t in range(NT):
                    norm3.apply(dve, t, c.x[:, t], c.x[:, t]).then_inc(s_norm3, 1)
                turned3.dve(dve)


def cross_and_experts(c, upto):
    nc, a = c.nc, c.a
    PIECES = EXPERTS1 + SHARED
    OUT = NT // 2
    with ExitStack() as ctx:
        sb = lambda name, shape, dt=F32: ctx.enter_context(nc.sbuf_tensor(f"d_{name}", shape, dt))
        norm4, norm_s, norm5, norm6 = (Norm(c, f"d_norm{i}", sb) for i in "4s56")
        turned4, turned5 = Transposed(c, "d_turned4"), Transposed(c, "d_turned5")
        ot_hi, ot_lo = sb("ot_hi", [DC, NTOK], F32R), sb("ot_lo", [DC, NTOK], F32R)
        rstd16 = sb("rstd16", [P, NT])
        scores, probs = sb("scores", [P, NT, T]), sb("probs", [P, NT, T])
        peak, row_sum, row_inv = sb("peak", [P, NT]), sb("row_sum", [P, NT]), sb("row_inv", [P, NT])
        wr, wr_hi, wr_lo = sb("wr", [P, KC, EXPERTS1]), sb("wr_hi", [P, KC, EXPERTS1], F32R), sb("wr_lo", [P, KC, EXPERTS1], F32R)
        logits = sb("logits", [P, NT, EXPERTS1])
        best, more, same, room = sb("best", [P, NT, 8]), sb("more", [P, NT, EXPERTS1]), sb("same", [P, NT, EXPERTS1]), sb("room", [P, NT])
        rank = [sb(f"rank{i}", [P, NT, EXPERTS1]) for i in range(2)]
        above, likely = sb("above", [P, NT, EXPERTS1]), sb("likely", [P, NT, EXPERTS1])
        total, weight = sb("total", [P, NT]), sb("weight", [P, NT])
        gate = sb("gate", [P, NT, PIECES])
        raw = [sb(f"raw{i}", [P, 3, D]) for i in range(2)]
        w_hi, w_lo = ([sb(f"w_{n}{i}", [P, 3, D], F32R) for i in range(2)] for n in ("hi", "lo"))
        silu, act_full = sb("silu", [P, 2, HALF]), [sb(f"h{i}", [HID, NTOK]) for i in range(2)]
        h_hi, h_lo = ([sb(f"h_{n}{i}", [HID, NTOK], F32R) for i in range(2)] for n in ("hi", "lo"))

        S = lambda name: c.sem(f"d_{name}")
        s_wr, s_wr_hi, s_wr_lo = S("wr"), S("wr_hi"), S("wr_lo")
        s_norm4, s_ot, s_ot_hi, s_ot_lo = S("norm4"), S("ot"), S("ot_hi"), S("ot_lo")
        s_sim, s_peak, s_exp, s_norm5, s_rstd16 = S("sim"), S("peak"), S("exp"), S("norm5"), S("rstd16")
        s_scored = S("scored")
        s_logits, s_above, s_likely = S("logits"), S("above"), S("likely")
        s_raw, s_split, s_pool = [S(f"raw{i}") for i in range(2)], S("split"), S("pool")
        s_up, s_silu, s_h, s_h_hi, s_h_lo = S("up"), S("silu"), S("h"), S("h_hi"), S("h_lo")
        s_out, s_used, s_norm6, s_store = S("out"), S("used"), S("norm6"), S("store")

        with nc.Block() as block:
            @block.sync
            def _(sp):
                sp.dma_start(wr[:], a["L1_ffn_w_router"].rearrange("(k p) e -> p k e", p=P)).then_inc(s_wr, 16)

                def load(j, up, gate_, down):
                    sp.dma_start(raw[j][:, 0].rearrange("p (k n) -> p k n", k=KC), up).then_inc(s_raw[j], 16)
                    sp.dma_start(raw[j][:, 1].rearrange("p (k n) -> p k n", k=KC), gate_).then_inc(s_raw[j], 16)
                    sp.dma_start(raw[j][:, 2], down).then_inc(s_raw[j], 16)

                with sp.Fori(0, EXPERTS1 // 2) as i:
                    for j in range(2):
                        sp.wait_ge(s_split, i * 2 + (j + 1))
                        one = bass.ds(i * 2 + j, 1)
                        load(j, *(a[f"L1_ffn_we{n}"][one].rearrange("n (k p) h -> p (n k) h", p=P) for n in (1, 3)),
                             a["L1_ffn_we2"][one].rearrange("n h d -> h (n d)"))
                for e in range(EXPERTS1, PIECES):
                    sp.wait_ge(s_split, e + 1)
                    cols = slice((e - EXPERTS1) * HID, (e - EXPERTS1 + 1) * HID)
                    load(e % 2, *(a[f"L1_ffn_ws{n}"][:, cols].rearrange("(k p) h -> p k h", p=P) for n in (1, 3)), a["L1_ffn_ws2"][cols, :])
                for b in range(B):
                    sp.wait_ge(s_norm6, 2 * b + 2)
                    sp.dma_start(c.out[b].rearrange("(t p) d -> p t d", p=P), c.x[:, 2 * b:2 * b + 2]).then_inc(s_store, 16)
                sp.wait_ge(s_store, 16 * B)

            @block.gpsimd
            def _(pool):
                own = Count(s_pool)
                pool.sem_inc(s_split, 2)
                norm4.root(pool)
                norm_s.root(pool, 1.0 / 256, 1e-6)
                pool.wait_ge(norm_s.s_rstd, 1)
                nc.gpsimd.tensor_scalar(rstd16[:], norm_s.rstd[:], 1.0 / 16, None, ALU.mult).then_inc(s_rstd16, 1)
                norm5.root(pool)

                def split(i, j):
                    pool.wait_ge(s_raw[j], i * 48 + 48)
                    pool.wait_ge(s_out, i * (2 * OUT) + (j + 1) * OUT)
                    n = own.inc(nc.gpsimd.tensor_tensor(w_hi[j][:], raw[j][:], c.one[:].unsqueeze(1).broadcast_to([P, 3, D]), ALU.mult))
                    pool.wait_ge(s_pool, n)
                    nc.gpsimd.tensor_tensor(w_lo[j][:], raw[j][:], f32(w_hi[j][:]), ALU.subtract).then_inc(s_split, 1)

                def low(i, j):
                    for half in range(2):
                        pool.wait_ge(s_h_hi, i * 4 + (2 * j + half + 1))
                        cols = slice(half * HALF, (half + 1) * HALF)
                        nc.gpsimd.tensor_tensor(h_lo[j][:, cols], act_full[j][:, cols], f32(h_hi[j][:, cols]), ALU.subtract).then_inc(s_h_lo, 1)

                split(0, 0)
                with pool.Fori(0, PIECES // 2 - 1) as i:
                    own.enter(i, 2)
                    split(i, 1)
                    low(i, 0)
                    split(i + 1, 0)
                    low(i, 1)
                own.leave(PIECES // 2 - 1)
                split(PIECES // 2 - 1, 1)
                low(PIECES // 2 - 1, 0)
                low(PIECES // 2 - 1, 1)
                norm6.root(pool)

            @block.tensor
            def _(pe):
                pe.sem_inc(s_out, 2 * OUT)
                turned4.pe(pe, s_norm4, 4)
                turned4.wait(pe)
                for b in range(B):
                    rows = slice(b * T, (b + 1) * T)
                    for k in range(KC):
                        last = mm3(nc, c.banks[b // 2][:, (b % 2) * T:(b % 2 + 1) * T], c.kv_hi[:, 2 * b + k], c.kv_lo[:, 2 * b + k],
                                   c.xt_hi[:, k, rows], c.xt_lo[:, k, rows], k == 0, k == KC - 1)
                    if b % 2:
                        last.then_inc(s_ot, 1)
                for b in range(B):
                    pe.wait_ge(s_ot_lo, b // 2 + 1)
                    if b == 2:
                        pe.wait_ge(s_ot_lo, 2)
                    bank = c.banks[(2, 3, 0, 1)[b]]
                    keys = slice(b * T, (b + 1) * T)
                    for i in range(2):
                        rows = slice(b * T + i * P, b * T + (i + 1) * P)
                        last = mm3(nc, bank[:, i * T:(i + 1) * T], ot_hi[:, rows], ot_lo[:, rows], c.kvt_hi[:, keys], c.kvt_lo[:, keys], True, True)
                    last.then_inc(s_sim, 1)
                turned5.pe(pe, s_norm5, 4)
                turned5.wait(pe)
                pe.wait_ge(s_wr_lo, 1)
                pe.wait_ge(s_scored, 1)
                route(c, c.banks[4], wr_hi, wr_lo, EXPERTS1).then_inc(s_logits, 1)

                def up(i, j):
                    piece = i * 2 + j
                    pe.wait_ge(s_split, piece + 3)
                    pe.wait_ge(s_h, piece * 2 + 2)
                    for half in range(2):
                        cols = slice(half * HALF, (half + 1) * HALF)
                        for n in range(2):
                            for k in range(KC):
                                s = slice(k * HID, (k + 1) * HID)
                                last = mm3(nc, c.banks[2 * half + n][:], w_hi[j][:, n, s], w_lo[j][:, n, s], c.xt_hi[:, k, cols], c.xt_lo[:, k, cols],
                                           k == 0, k == KC - 1)
                            last.then_inc(s_up, 1)

                def down(i, j):
                    pe.wait_ge(s_h_lo, i * 4 + (2 * j + 2))
                    for u in range(OUT):
                        pe.wait_ge(s_used, i * (2 * OUT) + (j * OUT + u + 1))
                        for t in range(2):
                            cols = slice((2 * u + t) * P, (2 * u + t + 1) * P)
                            last = mm3(nc, c.banks[4 + u][:, t * D:(t + 1) * D], h_hi[j][:, cols], h_lo[j][:, cols], w_hi[j][:, 2], w_lo[j][:, 2], True, True)
                        last.then_inc(s_out, 1)

                up(0, 0)
                pe.wait_ge(s_above, 1)
                with pe.Fori(0, PIECES // 2 - 1) as i:
                    up(i, 1)
                    down(i, 0)
                    up(i + 1, 0)
                    down(i, 1)
                up(PIECES // 2 - 1, 1)
                down(PIECES // 2 - 1, 0)
                down(PIECES // 2 - 1, 1)

            @block.scalar
            def _(act):
                act.wait_ge(s_wr, 16)
                nc.scalar.activation(wr_hi[:], wr[:], ACT.Copy).then_inc(s_wr_hi, 1)
                turned4.act(act)
                for h in range(2):
                    act.wait_ge(s_ot, h + 1)
                    nc.scalar.activation(ot_hi[:, h * HALF:(h + 1) * HALF], c.banks[h][0:DC], ACT.Copy).then_inc(s_ot_hi, 1)
                for t in range(NT):
                    act.wait_ge(s_peak, 1)
                    nc.scalar.activation(probs[:, t], scores[:, t], ACT.Exp, bias=peak[:, t:t + 1], accum_out=row_sum[:, t:t + 1]).then_inc(s_exp, 1)
                turned5.act(act)
                act.wait_ge(s_above, 1)
                nc.scalar.activation(likely[:], above[:], ACT.Exp).then_inc(s_likely, 1)

                def hidden(i, j):
                    for half in range(2):
                        act.wait_ge(s_up, i * 8 + (4 * j + 2 * half + 1))
                        act.wait_ge(s_h, i * 4 + (2 * j + half + 1))
                        nc.scalar.activation(silu[:, half], c.banks[2 * half][:], ACT.Silu).then_inc(s_silu, 1)
                        act.wait_ge(s_h, i * 4 + (2 * j + half + 3))
                        cols = slice(half * HALF, (half + 1) * HALF)
                        nc.scalar.activation(h_hi[j][:, cols], act_full[j][:, cols], ACT.Copy).then_inc(s_h_hi, 1)

                with act.Fori(0, PIECES // 2) as i:
                    hidden(i, 0)
                    hidden(i, 1)

            @block.vector
            def _(dve):
                dve.sem_inc(s_h, 2)
                dve.sem_inc(s_used, OUT)
                norm4.moments(dve, lambda t: c.x[:, t])
                dve.wait_ge(s_wr_hi, 1)
                nc.vector.tensor_tensor(wr_lo[:], wr[:], f32(wr_hi[:]), ALU.subtract).then_inc(s_wr_lo, 1)
                for t in range(NT):
                    norm4.apply(dve, t, c.x[:, t], c.x[:, t]).then_inc(s_norm4, 1)
                turned4.dve(dve)
                for h in range(2):
                    dve.wait_ge(s_ot_hi, h + 1)
                    cols = slice(h * HALF, (h + 1) * HALF)
                    nc.vector.tensor_tensor(ot_lo[:, cols], c.banks[h][0:DC], f32(ot_hi[:, cols]), ALU.subtract).then_inc(s_ot_lo, 1)

                tile = lambda t: c.banks[(2, 3, 0, 1)[t // 2]][:, (t % 2) * T:(t % 2 + 1) * T]
                dve.wait_ge(s_sim, B)
                norm_s.moments(dve, tile)
                dve.wait_ge(s_rstd16, 1)
                for t in range(NT):
                    last = nc.vector.tensor_scalar(scores[:, t], tile(t), norm_s.mv[:, t, 0:1], rstd16[:, t:t + 1], ALU.subtract, ALU.mult)
                last.then_inc(s_scored, 1)
                dve.drain()
                row = lambda r: c.rows[:, r].unsqueeze(1).broadcast_to([P, NT, T])
                nc.vector.tensor_tensor(scores[:], scores[:], row(ROW_GAMMA), ALU.mult)
                dve.drain()
                nc.vector.tensor_tensor(scores[:], scores[:], row(ROW_BETA), ALU.add)
                dve.drain()
                nc.vector.tensor_reduce(peak[:], scores[:], AX.X, ALU.max)
                dve.drain()
                nc.vector.tensor_scalar(peak[:], peak[:], -1.0, None, ALU.mult).then_inc(s_peak, 1)
                dve.wait_ge(s_exp, NT)
                nc.vector.reciprocal(row_inv[:], row_sum[:])
                dve.drain()
                for t in range(NT):
                    nc.vector.scalar_tensor_tensor(c.x[:, t], probs[:, t], row_inv[:, t:t + 1], c.x[:, t], ALU.mult, ALU.add)
                dve.drain()
                norm5.moments(dve, lambda t: c.x[:, t])
                for t in range(NT):
                    norm5.apply(dve, t, c.x[:, t], c.x[:, t]).then_inc(s_norm5, 1)
                turned5.dve(dve)

                wide = lambda v: v.broadcast_to([P, NT, EXPERTS1])
                dve.wait_ge(s_logits, 1)
                nc.vector.tensor_copy(logits[:], c.banks[4][:, 0:NT * EXPERTS1].rearrange("p (t e) -> p t e", t=NT))
                dve.drain()
                for t in range(NT):
                    nc.vector.max(best[:, t], logits[:, t])
                dve.drain()
                nc.vector.tensor_tensor(above[:], logits[:], wide(best[:, :, 0:1]), ALU.subtract).then_inc(s_above, 1)
                nc.vector.tensor_tensor(more[:], logits[:], wide(best[:, :, TOPK - 1:TOPK]), ALU.is_gt)
                nc.vector.tensor_tensor(same[:], logits[:], wide(best[:, :, TOPK - 1:TOPK]), ALU.is_equal)
                dve.drain()
                nc.vector.tensor_reduce(room[:], more[:], AX.X, ALU.add)
                nc.vector.tensor_copy(rank[0][:], same[:])
                dve.drain()
                nc.vector.tensor_scalar(room[:], room[:], -1.0, float(TOPK), ALU.mult, ALU.add)
                step = 1
                at = 0
                while step < EXPERTS1:
                    nc.vector.tensor_tensor(rank[1 - at][:, :, step:], rank[at][:, :, step:], rank[at][:, :, :-step], ALU.add)
                    nc.vector.tensor_copy(rank[1 - at][:, :, 0:step], rank[at][:, :, 0:step])
                    dve.drain()
                    step, at = 2 * step, 1 - at
                nc.vector.tensor_tensor(rank[1 - at][:], rank[at][:], wide(room[:].unsqueeze(2)), ALU.is_le)
                dve.drain()
                nc.vector.tensor_tensor(same[:], same[:], rank[1 - at][:], ALU.mult)
                dve.drain()
                nc.vector.tensor_tensor(more[:], more[:], same[:], ALU.add)
                dve.wait_ge(s_likely, 1)
                dve.drain()
                nc.vector.tensor_tensor(likely[:], likely[:], more[:], ALU.mult)
                dve.drain()
                nc.vector.tensor_reduce(total[:], likely[:], AX.X, ALU.add)
                nc.vector.memset(gate[:, :, EXPERTS1:], 1.0 / (TOPK + 1))
                dve.drain()
                nc.vector.reciprocal(weight[:], total[:])
                dve.drain()
                nc.vector.tensor_scalar(weight[:], weight[:], TOPK / (TOPK + 1), None, ALU.mult)
                dve.drain()
                nc.vector.tensor_tensor(gate[:, :, 0:EXPERTS1], likely[:], wide(weight[:].unsqueeze(2)), ALU.mult)
                dve.drain()
                flat = gate[:].rearrange("p t e -> p (t e)")

                def hidden(i, j):
                    for half in range(2):
                        dve.wait_ge(s_silu, i * 4 + (2 * j + half + 1))
                        dve.wait_ge(s_up, i * 8 + (4 * j + 2 * half + 2))
                        cols = slice(half * HALF, (half + 1) * HALF)
                        nc.vector.tensor_tensor(act_full[j][:, cols], silu[:, half], c.banks[2 * half + 1][:], ALU.mult).then_inc(s_h, 1)

                def add(i, j):
                    for u in range(OUT):
                        dve.wait_ge(s_out, i * (2 * OUT) + (2 * OUT + j * OUT + u + 1))
                        for t in range(2 * u, 2 * u + 2):
                            g = flat[:, bass.ds(i * 2 + (t * PIECES + j), 1)]
                            last = nc.vector.scalar_tensor_tensor(c.x[:, t], c.banks[4 + u][:, (t % 2) * D:(t % 2 + 1) * D], g, c.x[:, t], ALU.mult, ALU.add)
                        last.then_inc(s_used, 1)

                hidden(0, 0)
                with dve.Fori(0, PIECES // 2 - 1) as i:
                    hidden(i, 1)
                    add(i, 0)
                    hidden(i + 1, 0)
                    add(i, 1)
                hidden(PIECES // 2 - 1, 1)
                add(PIECES // 2 - 1, 0)
                add(PIECES // 2 - 1, 1)
                dve.drain()
                norm6.moments(dve, lambda t: c.x[:, t])
                for t in range(NT):
                    norm6.apply(dve, t, c.x[:, t], c.x[:, t]).then_inc(s_norm6, 1)


_INS = ['x', 'ctx_512', 'L0_attn_w_q', 'L0_attn_b_q', 'L0_attn_w_k', 'L0_attn_b_k', 'L0_attn_w_v', 'L0_attn_b_v',
        'L0_attn_w_o', 'L0_attn_b_o', 'L0_xattn_Wq', 'L0_xattn_Wk', 'L0_xattn_gamma_raw', 'L0_ffn_weight', 'L0_ffn_scale',
        'L0_ffn_expert_masks', 'L0_ffn_router_w', 'L1_attn_Wq', 'L1_attn_Wk', 'L1_attn_Wv', 'L1_attn_Wo',
        'L1_attn_head_scale', 'L1_xattn_W_k', 'L1_xattn_b_k', 'L1_xattn_ln_gamma', 'L1_xattn_ln_beta', 'L1_ffn_w_router',
        'L1_ffn_we1', 'L1_ffn_we3', 'L1_ffn_we2', 'L1_ffn_ws1', 'L1_ffn_ws3', 'L1_ffn_ws2']


def constants():
    import numpy as np
    freq = (1.0 / np.float32(10000.0) ** (np.arange(0, DH, 2, dtype=np.float32) / np.float32(DH))).astype(np.float32)
    angle = np.arange(T, dtype=np.float32)[None, :] * freq[:, None]
    cos, sin = np.cos(angle).astype(np.float32), np.sin(angle).astype(np.float32)
    return {
        "ident": np.eye(P, dtype=np.float32),
        "causal": np.triu(np.full((P, P), -1e30, np.float32), 1),
        "numbers": np.tile(np.arange(EXPERTS0, dtype=np.float32), (P, NT, 1)),
        "cos": np.concatenate([cos, cos]),
        "sin": np.concatenate([sin, -sin]),
    }


UPTO = 99


def kernel(**inputs):
    import numpy as _np
    import concourse.bacc as _bacc
    from concourse.bass_utils import run_bass_kernel_spmd as _run

    nc = _bacc.Bacc("TRN2", target_bir_lowering=False, num_devices=1)
    arrays, args = {}, {}
    for name, value in [(n, inputs[n]) for n in _INS] + list(constants().items()):
        v = _np.ascontiguousarray(value)
        if v.ndim == 0:
            v = v.reshape(1)
        arrays[f"in_{name}_dram"] = v
        args[name] = nc.dram_tensor(f"in_{name}_dram", v.shape, mybir.dt.from_np(v.dtype), kind="ExternalInput").ap()
    out = nc.dram_tensor("out_0_dram", (B, T, D), F32, kind="ExternalOutput").ap()
    decoder(nc, args, out, UPTO)
    r = _run(nc, [arrays], core_ids=[0])
    return r.results[0]["out_0_dram"]
```

```python
import concourse.bass as bass
from concourse import mybir
from contextlib import ExitStack

F32 = mybir.dt.float32
F32R = mybir.dt.float32r
BF16 = mybir.dt.bfloat16
ALU = mybir.AluOpType
ACT = mybir.ActivationFunctionType
AX = mybir.AxisListType

P = 128
B, T, D = 4, 256, 256
NT = B * T // P
KC = D // P
NTOK = B * T
HALF = NTOK // 2
BANK = 512
HEADS, DH = 16, 128
GROUP = 4
GROUPS = HEADS // GROUP
SCALE = DH ** -0.5
DC = 64
EPS = 1e-5
EXPERTS0 = 32
EXPERTS1, HID, TOPK = 16, 128, 4
SHARED = 512 // HID
KEEP = int(T * 0.3)
HALF_BLOCK = DH // 2


class Count:

    def __init__(self, sem):
        self.sem, self.base, self.n = sem, 0, 0

    def inc(self, instruction):
        instruction.then_inc(self.sem, 1)
        self.n += 1
        return self.base + self.n

    def enter(self, i, per_turn):
        self.entry, self.per_turn = self.base + self.n, per_turn
        self.base, self.n = self.entry + i * per_turn, 0

    def leave(self, turns):
        assert self.n == self.per_turn, (self.n, self.per_turn)
        self.base, self.n = self.entry + turns * self.per_turn, 0

    @property
    def now(self):
        return self.base + self.n


def f32(ap):
    return ap.bitcast(F32)


class Chip:
    pass


def decoder(nc, a, out, upto=99):
    with ExitStack() as ctx:
        c = Chip()
        c.nc, c.a, c.out = nc, a, out
        c.sem = lambda name: ctx.enter_context(nc.semaphore(name))
        sb = lambda name, shape, dt=F32: ctx.enter_context(nc.sbuf_tensor(name, shape, dt))
        c.banks = [ctx.enter_context(nc.psum_tensor(f"bank{i}", [P, BANK], F32)) for i in range(8)]
        c.x = sb("x", [P, NT, D])
        c.xt_hi, c.xt_lo = sb("xt_hi", [P, KC, NTOK], F32R), sb("xt_lo", [P, KC, NTOK], F32R)
        c.ident = sb("ident", [P, P])
        c.ident_bf = sb("ident_bf", [P, P], BF16)
        c.causal = sb("causal", [P, P], BF16)
        c.sim = sb("sim", [P, NT, T])
        c.thr = sb("thr", [P, NT])
        c.kv_hi, c.kv_lo = sb("kv_hi", [P, NT, P], F32R), sb("kv_lo", [P, NT, P], F32R)
        c.kvt_hi, c.kvt_lo = sb("kvt_hi", [DC, NTOK], F32R), sb("kvt_lo", [DC, NTOK], F32R)
        c.bias_t = sb("bias_t", [P, 3 * HEADS])
        c.rt_hi, c.rt_lo = sb("rt_hi", [P, KC, EXPERTS0], F32R), sb("rt_lo", [P, KC, EXPERTS0], F32R)
        c.tern = sb("tern", [P, KC, D], BF16)
        c.rows = sb("rows", [P, 5, D])
        c.gamma, c.one_less = sb("gamma", [P, 1]), sb("one_less", [P, 1])
        c.zero = sb("zero", [P, 1], BF16)
        c.half_neg, c.one = sb("half_neg", [P, NT]), sb("one", [P, 1])
        setup(c)
        if upto >= 1:
            attention(c, 0)
        if upto >= 2:
            graph_and_masked_experts(c, upto)
        if upto >= 5:
            attention(c, 1)
        if upto >= 6:
            cross_and_experts(c, upto)
        if upto < 99:
            dump(c)


def dump(c):
    nc = c.nc
    s = c.sem("s_dump")
    with nc.Block() as block:
        @block.sync
        def _(sp):
            sp.dma_start(c.out.rearrange("b (t p) d -> p (b t) d", p=P), c.x[:]).then_inc(s, 16)
            sp.wait_ge(s, 16)


def mm3(nc, out, l_hi, l_lo, r_hi, r_lo, start, stop):
    nc.tensor.matmul(out, l_hi, r_hi, start=start, stop=False)
    nc.tensor.matmul(out, l_hi, r_lo, start=False, stop=False)
    return nc.tensor.matmul(out, l_lo, r_hi, start=False, stop=stop)


ROW_BO, ROW_SCALE, ROW_GAMMA, ROW_BETA, ROW_BK = range(5)


def setup(c):
    nc, a = c.nc, c.a
    with ExitStack() as ctx:
        sb = lambda name, shape, dt=F32: ctx.enter_context(nc.sbuf_tensor(name, shape, dt))
        ctx_nat = sb("ctx_nat", [P, NT, DC])
        ctxt_hi, ctxt_lo = sb("ctxt_hi", [DC, NTOK], F32R), sb("ctxt_lo", [DC, NTOK], F32R)
        w_nat = sb("w_nat", [DC, 3, DC])
        wt_hi, wt_lo = sb("wt_hi", [DC, 3, 2, DC], F32R), sb("wt_lo", [DC, 3, 2, DC], F32R)
        qt_hi, qt_lo = sb("qt_hi", [DC, NTOK], F32R), sb("qt_lo", [DC, NTOK], F32R)
        kt_hi, kt_lo = sb("kt_hi", [DC, NTOK], F32R), sb("kt_lo", [DC, NTOK], F32R)
        kv = sb("kv", [P, NT, P])
        bias_nat = sb("bias_nat", [3 * HEADS, DH])
        bk_col = sb("bk_col", [DC, 1])
        r_nat = sb("r_nat", [EXPERTS0, D])
        w0 = sb("w0", [P, KC, D])
        w0b = sb("w0b", [P, KC, D])
        causal_f = sb("causal_f", [P, P])
        g_raw, g_exp, g_den = sb("g_raw", [P, 1]), sb("g_exp", [P, 1]), sb("g_den", [P, 1])

        s_x, s_ctx, s_w, s_const, s_bias, s_rows = (c.sem(f"su_{n}") for n in ("x", "ctx", "w", "const", "bias", "rows"))
        s_tr = c.sem("su_tr")
        s_hi = c.sem("su_hi")
        s_lo = c.sem("su_lo")
        s_pool = c.sem("su_pool")

        bank = c.banks
        with nc.Block() as block:
            @block.sync
            def _(sp):
                sp.dma_start(c.ident[:], a["ident"]).then_inc(s_const, 16)
                sp.dma_start(ctx_nat[:], a["ctx_512"].rearrange("b (t p) d -> p (b t) d", p=P)).then_inc(s_ctx, 16)
                sp.dma_start(w_nat[:, 0], a["L0_xattn_Wq"]).then_inc(s_w, 16)
                sp.dma_start(w_nat[:, 1], a["L0_xattn_Wk"]).then_inc(s_w, 16)
                sp.dma_start(w_nat[:, 2], a["L1_xattn_W_k"]).then_inc(s_w, 16)
                sp.dma_start(r_nat[:], a["L0_ffn_router_w"]).then_inc(s_w, 16)
                for i, n in enumerate(("b_q", "b_k", "b_v")):
                    sp.dma_start(bias_nat[i * HEADS:(i + 1) * HEADS], a[f"L0_attn_{n}"].rearrange("(h d) -> h d", d=DH)).then_inc(s_w, 16)
                sp.dma_start(c.x[:], a["x"].rearrange("b (t p) d -> p (b t) d", p=P)).then_inc(s_x, 16)
                sp.dma_start(causal_f[:], a["causal"]).then_inc(s_bias, 16)
                sp.dma_start(w0[:], a["L0_ffn_weight"].rearrange("(c p) i -> p c i", p=P)).then_inc(s_bias, 16)
                sp.dma_start(bk_col[:], a["L1_xattn_b_k"].rearrange("(d o) -> d o", o=1)).then_inc(s_bias, 16)
                sp.dma_start(g_raw[:], a["L0_xattn_gamma_raw"].partition_broadcast(P)).then_inc(s_bias, 16)
                sp.dma_start(c.rows[:, ROW_BK, 0:DC], a["L1_xattn_b_k"].partition_broadcast(P)).then_inc(s_rows, 16)
                sp.dma_start(c.rows[:, ROW_BK, DC:P], a["L1_xattn_b_k"].partition_broadcast(P)).then_inc(s_rows, 16)
                for r, n in ((ROW_BO, "L0_attn_b_o"), (ROW_SCALE, "L0_ffn_scale"), (ROW_GAMMA, "L1_xattn_ln_gamma"), (ROW_BETA, "L1_xattn_ln_beta")):
                    sp.dma_start(c.rows[:, r], a[n].partition_broadcast(P)).then_inc(s_rows, 16)

            @block.tensor
            def _(pe):
                pe.wait_ge(s_const, 16)
                pe.wait_ge(s_ctx, 16)
                for h in range(2):
                    for t in range(4):
                        last = nc.tensor.transpose(bank[h][0:DC, t * P:(t + 1) * P], ctx_nat[:, 4 * h + t], c.ident[:])
                    last.then_inc(s_tr, 1)
                pe.wait_ge(s_w, 7 * 16)
                for i in range(3):
                    nc.tensor.transpose(bank[2][0:DC, i * DC:(i + 1) * DC], w_nat[:, i], c.ident[0:DC, 0:DC])
                nc.tensor.transpose(bank[2][:, 192:192 + 3 * HEADS], bias_nat[:], c.ident[0:3 * HEADS, 0:3 * HEADS])
                for k in range(KC):
                    last = nc.tensor.transpose(bank[2][:, 256 + k * EXPERTS0:256 + (k + 1) * EXPERTS0], r_nat[:, k * P:(k + 1) * P],
                                               c.ident[0:EXPERTS0, 0:EXPERTS0])
                last.then_inc(s_tr, 1)
                pe.wait_ge(s_x, 16)
                for k in range(KC):
                    for h in range(2):
                        for t in range(4):
                            last = nc.tensor.transpose(bank[3 + 2 * k + h][:, t * P:(t + 1) * P], c.x[:, 4 * h + t, k * P:(k + 1) * P], c.ident[:])
                        last.then_inc(s_tr, 1)
                pe.wait_ge(s_lo, 4)
                for i in range(3):
                    for h in range(2):
                        n = 2 * i + h
                        b = bank[(7, 0, 1, 2, 3, 4)[n]]
                        pe.wait_ge(s_lo, (4, 4, 4, 4, 5, 6)[n])
                        cols = slice(h * HALF, (h + 1) * HALF)
                        w_hi, w_lo = (w[:, i].rearrange("k a n -> k (a n)") for w in (wt_hi, wt_lo))
                        mm3(nc, b[:], w_hi, w_lo, ctxt_hi[:, cols], ctxt_lo[:, cols], True, True).then_inc(s_tr, 1)
                for h in range(2):
                    pe.wait_ge(s_lo, 7 + h)
                    w_hi, w_lo = (w[:, 2].rearrange("k a n -> k (a n)") for w in (wt_hi, wt_lo))
                    for t in range(4):
                        cols = slice((4 * h + t) * P, (4 * h + t + 1) * P)
                        last = mm3(nc, bank[5 + h][:, t * P:(t + 1) * P], ctxt_hi[:, cols], ctxt_lo[:, cols], w_hi, w_lo, True, True)
                    last.then_inc(s_tr, 1)
                pe.wait_ge(s_lo, 14)
                for b in range(B):
                    for h in range(2):
                        cols = slice(b * T + h * P, b * T + (h + 1) * P)
                        keys = slice(b * T, (b + 1) * T)
                        last = mm3(nc, bank[(7, 0, 1, 2)[b]][:, h * T:(h + 1) * T], qt_hi[:, cols], qt_lo[:, cols], kt_hi[:, keys], kt_lo[:, keys], True, True)
                    last.then_inc(s_tr, 1)

            @block.scalar
            def _(act):
                hi = Count(s_hi)
                for h in range(2):
                    act.wait_ge(s_tr, h + 1)
                    hi.inc(nc.scalar.activation(ctxt_hi[:, h * HALF:(h + 1) * HALF], bank[h][0:DC], ACT.Copy))
                act.wait_ge(s_tr, 3)
                small = bank[2][0:DC, 0:3 * DC].rearrange("k (i n) -> k i n", i=3)
                nc.scalar.activation(wt_hi[:, :, 0], small, ACT.Copy)
                nc.scalar.activation(wt_hi[:, :, 1], small, ACT.Copy)
                nc.scalar.activation(c.bias_t[:], bank[2][:, 192:192 + 3 * HEADS], ACT.Copy)
                hi.inc(nc.scalar.activation(c.rt_hi[:], bank[2][:, 256:256 + KC * EXPERTS0].rearrange("p (k e) -> p k e", k=KC), ACT.Copy))
                for n in range(4):
                    act.wait_ge(s_tr, 4 + n)
                    hi.inc(nc.scalar.activation(c.xt_hi[:, n // 2, (n % 2) * HALF:(n % 2 + 1) * HALF], bank[3 + n][:], ACT.Copy))
                act.wait_ge(s_const, 16)
                nc.scalar.activation(c.ident_bf[:], c.ident[:], ACT.Copy)
                act.wait_ge(s_bias, 64)
                nc.scalar.activation(c.causal[:], causal_f[:], ACT.Copy)
                g = nc.scalar.activation(g_exp[:], g_raw[:], ACT.Exp, scale=-1.0)
                hi.inc(g)
                for i in range(3):
                    for h in range(2):
                        n = 2 * i + h
                        act.wait_ge(s_tr, 8 + n)
                        b = bank[(7, 0, 1, 2, 3, 4)[n]]
                        dst = (qt_hi, kt_hi, c.kvt_hi)[i][:, h * HALF:(h + 1) * HALF]
                        if i < 2:
                            hi.inc(nc.scalar.activation(dst, b[0:DC], ACT.Copy))
                        else:
                            hi.inc(nc.scalar.activation(dst, b[0:DC], ACT.Identity, bias=bk_col[:]))
                for h in range(2):
                    act.wait_ge(s_lo, 15 + h)
                    hi.inc(nc.scalar.activation(c.kv_hi[:, 4 * h:4 * h + 4], kv[:, 4 * h:4 * h + 4], ACT.Copy))
                for b in range(B):
                    act.wait_ge(s_tr, 16 + b)
                    src = bank[(7, 0, 1, 2)[b]][:].rearrange("p (h n) -> p h n", h=2)
                    nc.scalar.activation(c.sim[:, 2 * b:2 * b + 2], src, ACT.Copy, scale=1.0 / 16)

            @block.vector
            def _(dve):
                lo = Count(s_lo)
                nc.vector.memset(c.half_neg[:], -0.5)
                nc.vector.memset(c.one[:], 1.0)
                nc.vector.memset(c.zero[:], 0.0)
                for h in range(2):
                    dve.wait_ge(s_hi, h + 1)
                    cols = slice(h * HALF, (h + 1) * HALF)
                    lo.inc(nc.vector.tensor_tensor(ctxt_lo[:, cols], bank[h][0:DC], f32(ctxt_hi[:, cols]), ALU.subtract))
                dve.wait_ge(s_hi, 3)
                small = bank[2][0:DC, 0:3 * DC].rearrange("k (i n) -> k i n", i=3)
                nc.vector.tensor_tensor(wt_lo[:, :, 0], small, f32(wt_hi[:, :, 0]), ALU.subtract)
                lo.inc(nc.vector.tensor_tensor(wt_lo[:, :, 1], small, f32(wt_hi[:, :, 1]), ALU.subtract))
                lo.inc(nc.vector.tensor_tensor(c.rt_lo[:], bank[2][:, 256:256 + KC * EXPERTS0].rearrange("p (k e) -> p k e", k=KC),
                                               f32(c.rt_hi[:]), ALU.subtract))
                for n in range(4):
                    dve.wait_ge(s_hi, 4 + n)
                    cols = slice((n % 2) * HALF, (n % 2 + 1) * HALF)
                    lo.inc(nc.vector.tensor_tensor(c.xt_lo[:, n // 2, cols], bank[3 + n][:], f32(c.xt_hi[:, n // 2, cols]), ALU.subtract))
                for i in range(3):
                    for h in range(2):
                        n = 2 * i + h
                        dve.wait_ge(s_hi, 9 + n)
                        b = bank[(7, 0, 1, 2, 3, 4)[n]]
                        cols = slice(h * HALF, (h + 1) * HALF)
                        if i < 2:
                            lo.inc(nc.vector.tensor_tensor((qt_lo, kt_lo)[i][:, cols], b[0:DC], f32((qt_hi, kt_hi)[i][:, cols]), ALU.subtract))
                        else:
                            lo.inc(nc.vector.scalar_tensor_tensor(c.kvt_lo[:, cols], b[0:DC], bk_col[:], f32(c.kvt_hi[:, cols]), ALU.add, ALU.subtract))
                dve.wait_ge(s_rows, 6 * 16)
                for h in range(2):
                    dve.wait_ge(s_tr, 14 + h)
                    lo.inc(nc.vector.tensor_tensor(kv[:, 4 * h:4 * h + 4], bank[5 + h][:].rearrange("p (t n) -> p t n", t=4),
                                                   c.rows[:, ROW_BK, 0:P].unsqueeze(1).broadcast_to([P, 4, P]), ALU.add))
                for h in range(2):
                    dve.wait_ge(s_hi, 15 + h)
                    lo.inc(nc.vector.tensor_tensor(c.kv_lo[:, 4 * h:4 * h + 4], kv[:, 4 * h:4 * h + 4], f32(c.kv_hi[:, 4 * h:4 * h + 4]), ALU.subtract))
                dve.wait_ge(s_hi, 8)
                n = lo.inc(nc.vector.tensor_scalar(g_den[:], g_exp[:], 1.0, None, ALU.add))
                dve.wait_ge(s_lo, n)
                n = lo.inc(nc.vector.reciprocal(c.gamma[:], g_den[:]))
                dve.wait_ge(s_lo, n)
                lo.inc(nc.vector.tensor_scalar(c.one_less[:], c.gamma[:], -1.0, 2.0, ALU.mult, ALU.add))

            @block.gpsimd
            def _(pool):
                own = Count(s_pool)
                pool.wait_ge(s_bias, 64)
                n = own.inc(nc.gpsimd.tensor_scalar(w0b[:], w0[:], 2.0, 1.0, ALU.mult, ALU.min))
                pool.wait_ge(s_pool, n)
                n = own.inc(nc.gpsimd.tensor_scalar(w0[:], w0b[:], -1.0, 12582912.0, ALU.max, ALU.add))
                pool.wait_ge(s_pool, n)
                nc.gpsimd.tensor_scalar(c.tern[:], w0[:], -12582912.0, None, ALU.add)
                pool.wait_ge(s_rows, 6 * 16)
                pool.wait_ge(s_tr, 7)
                nc.gpsimd.tensor_tensor(c.x[:], c.x[:], c.rows[:, ROW_BO].unsqueeze(1).broadcast_to([P, NT, D]), ALU.add)


def attention(c, layer):
    nc, a = c.nc, c.a
    rope = layer == 1
    names = [f"L0_attn_w_{n}" for n in "qkvo"] if not rope else [f"L1_attn_W{n}" for n in "qkvo"]
    w_q, w_k, w_v = (a[n].rearrange("(k p) n -> p k n", p=P) for n in names[:3])
    w_o = a[names[3]].rearrange("(h d) n -> d h n", d=DH)
    KVC = DH if rope else GROUP * DH
    KH = KVC // DH

    def units(h):
        if rope and h % GROUP:
            return [("q", 0), ("q", 1)]
        return [("k", 0), ("k", 1), ("q", 0), ("q", 1)]

    PROJ_TO = [sum(len(units(i)) for i in range(h)) for h in range(GROUP + 1)]
    PROJ = PROJ_TO[-1]
    VU = 2 if rope else NT
    OU = NT // 2
    RING = 3

    first, n = {}, 0
    for h in range(1, GROUP + 1):
        first["proj", h + 1] = n
        n += len(units(h + 1))
        first["pv", h - 1] = n
        n += 2
    first["v"], first["o"] = n, n + VU
    U = n + VU + OU
    assert U % RING == 0
    BEFORE = U - first["proj", GROUP]

    def number(g, step, u):
        return g * U + (BEFORE + first[step] + u)

    def ring_bank(step, u):
        return c.banks[5 + (BEFORE + first[step] + u) % RING]

    def taken(g, step, u):
        return number(g, step, u) + (RING + 1)

    with ExitStack() as ctx:
        sb = lambda name, shape, dt=F32: ctx.enter_context(nc.sbuf_tensor(f"a{layer}_{name}", shape, dt))
        raw_q, raw_k, raw_v = sb("raw_q", [P, KC, GROUP * DH]), sb("raw_k", [P, KC, KVC]), sb("raw_v", [P, KC, KVC])
        raw_o = sb("raw_o", [DH, GROUP, D])
        wq_hi, wq_lo = sb("wq_hi", [P, KC, GROUP * DH], F32R), sb("wq_lo", [P, KC, GROUP * DH], F32R)
        wk_hi, wk_lo = sb("wk_hi", [P, KC, KVC], F32R), sb("wk_lo", [P, KC, KVC], F32R)
        wv_hi, wv_lo = sb("wv_hi", [P, KC, KVC], F32R), sb("wv_lo", [P, KC, KVC], F32R)
        wo_hi, wo_lo = sb("wo_hi", [DH, GROUP, D], F32R), sb("wo_lo", [DH, GROUP, D], F32R)
        queries, keys, vals = sb("queries", [DH, NTOK]), sb("keys", [DH, NTOK]), sb("vals", [P, NT, KVC])
        probs = [sb(f"probs{i}", [P, 3, BANK]) for i in range(2)]
        probs_t = sb("probs_t", [P, 3 * BANK])
        attended = sb("attended", [DH, NTOK])
        ot_hi, ot_lo = sb("ot_hi", [DH, GROUP, NTOK], F32R), sb("ot_lo", [DH, GROUP, NTOK], F32R)
        peak, neg_peak = sb("peak", [P, NT]), sb("neg_peak", [P, NT])
        row_sum, row_inv = sb("row_sum", [P, 2, NT]), sb("row_inv", [P, 2, NT])
        if rope:
            cos, sin = sb("cos", [P, T]), sb("sin", [P, T])
            scale_row = sb("scale_row", [P, HEADS])
            along, across = (sb(n, [P, 2, HALF]) for n in ("along", "across"))
        else:
            work = [sb(f"work{i}", [P, T]) for i in range(2)]
            top8 = sb("top8", [P, 8])

        S = lambda name: c.sem(f"a{layer}_{name}")
        s_raw = {n: S(f"raw_{n}") for n in "qkvo"}
        s_table = S("table")
        s_split_proj, s_split_v, s_split_o = S("split_proj"), S("split_v"), S("split_o")
        s_pool = S("pool")
        s_proj, s_v, s_pv, s_o = S("proj"), S("v"), S("pv"), S("o")
        s_taken = S("taken")
        s_attended = S("attended")
        s_ot_hi, s_ot_lo = S("ot_hi"), S("ot_lo")
        s_seen = S("seen")
        s_rope = S("rope")
        s_scores, s_peak, s_exp, s_norm = S("scores"), S("peak"), S("exp"), S("norm")
        s_pt, s_pt_free = S("pt"), S("pt_free")
        s_dve = S("dve")

        def scores_bank(b, q):
            return (0, b * P, P) if q == 0 else (1 + b // 2, (b % 2) * T, T)

        def proj_index(g, h, u):
            return (g + h // GROUP) * PROJ + (PROJ_TO[h % GROUP] + u)

        with nc.Block() as block:
            @block.sync
            def _(sp):
                def load(n, dst, src, g):
                    width = {"q": GROUP * DH, "k": KVC, "v": KVC, "o": GROUP}[n]
                    part = src[:, bass.ds(g * GROUP, GROUP)] if n == "o" else src[:, :, bass.ds(g * width, width)]
                    sp.dma_start(dst[:], part).then_inc(s_raw[n], 16)

                for n, dst, src in (("q", raw_q, w_q), ("k", raw_k, w_k), ("v", raw_v, w_v), ("o", raw_o, w_o)):
                    load(n, dst, src, 0)
                if rope:
                    sp.dma_start(cos[:], a["cos"]).then_inc(s_table, 16)
                    sp.dma_start(sin[:], a["sin"]).then_inc(s_table, 16)
                    sp.dma_start(scale_row[:], a["L1_attn_head_scale"].rearrange("a h b c -> (a h b c)").partition_broadcast(P)).then_inc(s_table, 16)
                with sp.Fori(0, GROUPS - 1) as g:
                    sp.wait_ge(s_split_v, g + 1)
                    load("v", raw_v, w_v, g + 1)
                    sp.wait_ge(s_split_proj, g * GROUP + GROUP)
                    load("q", raw_q, w_q, g + 1)
                    load("k", raw_k, w_k, g + 1)
                    sp.wait_ge(s_split_o, g + 1)
                    load("o", raw_o, w_o, g + 1)

            @block.gpsimd
            def _(pool):
                own = Count(s_pool)
                pool.sem_inc(s_ot_lo, 2)

                def split(parts, done):
                    for hi, lo, raw in parts:
                        n = own.inc(nc.gpsimd.tensor_tensor(hi, raw, c.one[:].unsqueeze(1).broadcast_to(list(raw.shape)), ALU.mult))
                    pool.wait_ge(s_pool, n)
                    for hi, lo, raw in parts:
                        last = nc.gpsimd.tensor_tensor(lo, raw, f32(hi), ALU.subtract)
                    last.then_inc(done, 1)

                def split_proj(g, h):
                    pool.wait_ge(s_raw["q"], (g + h // GROUP) * 16 + 16)
                    pool.wait_ge(s_proj, proj_index(g, h, len(units(h))))
                    s = slice((h % GROUP) * DH, (h % GROUP + 1) * DH)
                    parts = [(wq_hi[:, :, s], wq_lo[:, :, s], raw_q[:, :, s])]
                    if ("k", 0) in units(h):
                        pool.wait_ge(s_raw["k"], (g + h // GROUP) * 16 + 16)
                        s = slice((h % KH) * DH, (h % KH + 1) * DH)
                        parts.append((wk_hi[:, :, s], wk_lo[:, :, s], raw_k[:, :, s]))
                    split(parts, s_split_proj)

                def split_v(g):
                    pool.wait_ge(s_raw["v"], g * 16 + 16)
                    pool.wait_ge(s_v, g * VU + VU)
                    split([(wv_hi[:], wv_lo[:], raw_v[:])], s_split_v)

                def split_o(g):
                    pool.wait_ge(s_raw["o"], g * 16 + 16)
                    pool.wait_ge(s_o, g * OU + OU)
                    split([(wo_hi[:], wo_lo[:], raw_o[:])], s_split_o)

                def rotate(g, h):
                    for u, (what, half) in enumerate(units(h) if rope else ()):
                        dst = (queries if what == "q" else keys)[:, half * HALF:(half + 1) * HALF]
                        pool.wait_ge(s_taken, taken(g, ("proj", h), u))
                        nc.gpsimd.tensor_tensor(dst, along[:, u % 2], across[:, u % 2], ALU.add).then_inc(s_rope, 1)

                def low(g, h):
                    for half in range(2):
                        pool.wait_ge(s_ot_hi, g * (2 * GROUP) + (2 * h + half + 1))
                        cols = slice(half * HALF, (half + 1) * HALF)
                        nc.gpsimd.tensor_tensor(ot_lo[:, h, cols], attended[:, cols], f32(ot_hi[:, h, cols]), ALU.subtract).then_inc(s_ot_lo, 1)

                def turn(g, more):
                    split_proj(g, 3)
                    rotate(g, 2)
                    if not more:
                        split_o(g)
                    low(g, 0)
                    if more:
                        split_proj(g, 4)
                    rotate(g, 3)
                    low(g, 1)
                    if more:
                        split_v(g + 1)
                        split_proj(g, 5)
                        rotate(g, 4)
                    low(g, 2)
                    if more:
                        split_o(g)
                        rotate(g, 5)
                    low(g, 3)
                    if more:
                        split_proj(g, 6)

                split_proj(-1, 4)
                split_proj(-1, 5)
                rotate(-1, 4)
                split_v(0)
                rotate(-1, 5)
                split_proj(-1, 6)
                with pool.Fori(0, GROUPS - 1) as g:
                    own.enter(g, GROUP + KH + 2)
                    turn(g, True)
                own.leave(GROUPS - 1)
                turn(GROUPS - 1, False)

            @block.tensor
            def _(pe):
                pe.sem_inc(s_proj, PROJ)
                pe.sem_inc(s_v, VU)
                pe.sem_inc(s_o, OU)

                def claim(g, step, u):
                    pe.wait_ge(s_taken, number(g, step, u) + 1)
                    return ring_bank(step, u)

                def proj(g, h):
                    pe.wait_ge(s_split_proj, g * GROUP + (h + 1))
                    for u, (what, half) in enumerate(units(h)):
                        bank = claim(g, ("proj", h), u)
                        hi, lo = (wq_hi, wq_lo) if what == "q" else (wk_hi, wk_lo)
                        s = (h % (GROUP if what == "q" else KH)) * DH
                        cols = slice(half * HALF, (half + 1) * HALF)
                        for k in range(KC):
                            last = mm3(nc, bank[:], hi[:, k, s:s + DH], lo[:, k, s:s + DH], c.xt_hi[:, k, cols], c.xt_lo[:, k, cols], k == 0, k == KC - 1)
                        last.then_inc(s_proj, 1)

                def values(g):
                    pe.wait_ge(s_split_v, g + 2)
                    per = NT // VU
                    for u in range(VU):
                        bank = claim(g, "v", u)
                        for i in range(per):
                            t = u * per + i
                            cols = slice(t * P, (t + 1) * P)
                            for k in range(KC):
                                last = mm3(nc, bank[:, i * KVC:(i + 1) * KVC], c.xt_hi[:, k, cols], c.xt_lo[:, k, cols], wv_hi[:, k], wv_lo[:, k],
                                           k == 0, k == KC - 1)
                        last.then_inc(s_v, 1)

                def scores(g, h):
                    if rope:
                        pe.wait_ge(s_rope, proj_index(g, h, len(units(h))))
                    elif h > 1:
                        pe.wait_ge(s_taken, taken(g, ("proj", h), len(units(h)) - 1))
                    else:
                        pe.wait_ge(s_taken, taken(g, ("proj", GROUP + 1), len(units(h)) - 1) - U)
                    pe.wait_ge(s_exp, g * (GROUP * NT) + (h + 1) * NT)
                    for q in range(2):
                        for b in range(B):
                            i, at, width = scores_bank(b, q)
                            out = c.banks[i][:, at:at + width]
                            rows = slice(b * T + q * P, b * T + (q + 1) * P)
                            nc.tensor.matmul(out, queries[:, rows], keys[:, b * T:b * T + width], start=True, stop=False)
                            last = nc.tensor.matmul(out[:, width - P:], c.ident_bf[:], c.causal[:], start=False, stop=True)
                            if at + width == BANK:
                                last.then_inc(s_scores, 1)

                def transposes(g, h):
                    for slot in range(3 * B):
                        b, j = slot // 3, slot % 3
                        bank = 3 + (3 * h + slot // 4) % 2
                        if slot % 4 == 0:
                            pe.wait_ge(s_pt_free, g * (3 * GROUP) + (3 * h + slot // 4 + 1))
                        if slot % 6 == 0:
                            pe.wait_ge(s_norm, g * (GROUP * 3) + (h * 3 + b // 2 + 2))
                        i, at, width = scores_bank(b, min(j, 1))
                        at += P if j == 2 else 0
                        last = nc.tensor.transpose(c.banks[bank][:, slot % 4 * P:(slot % 4 + 1) * P], probs[h % 2][:, i, at:at + P], c.ident[:])
                        if slot % 4 == 3:
                            last.then_inc(s_pt, 1)

                def pv(g, h):
                    if h == 0:
                        pe.wait_ge(s_taken, taken(g, "v", VU - 1) - U)
                    for half in range(2):
                        bank = claim(g, ("pv", h), half)
                        for i in range(2):
                            b = 2 * half + i
                            pe.wait_ge(s_pt_free, g * (3 * GROUP) + (3 * h + (3 * b + 2) // 4 + 1 + 2))
                            at = 3 * b * P
                            s = slice((h % KH) * DH, (h % KH + 1) * DH)
                            out = bank[:, i * T:(i + 1) * T]
                            nc.tensor.matmul(out, vals[:, 2 * b, s], probs_t[:, at:at + T], start=True, stop=False)
                            last = nc.tensor.matmul(out[:, P:], vals[:, 2 * b + 1, s], probs_t[:, at + T:at + T + P], start=False, stop=True)
                        last.then_inc(s_pv, 1)

                def output(g):
                    pe.wait_ge(s_split_o, g + 1)
                    pe.wait_ge(s_ot_lo, g * (2 * GROUP) + (2 * GROUP + 2))
                    for u in range(OU):
                        bank = claim(g, "o", u)
                        for i in range(2):
                            cols = slice((2 * u + i) * P, (2 * u + i + 1) * P)
                            for h in range(GROUP):
                                last = mm3(nc, bank[:, i * D:(i + 1) * D], ot_hi[:, h, cols], ot_lo[:, h, cols], wo_hi[:, h], wo_lo[:, h],
                                           h == 0, h == GROUP - 1)
                        last.then_inc(s_o, 1)

                def last_output(g, units, heads):
                    pe.wait_ge(s_split_o, g + 1)
                    pe.wait_ge(s_ot_lo, g * (2 * GROUP) + (2 * heads.stop + 2))
                    pe.wait_ge(s_exp, (g + 1) * (GROUP * NT) + NT)
                    if 3 in units:
                        pe.wait_ge(s_pt_free, (g + 1) * (GROUP * 3) + 2)
                    for u in units:
                        if 0 in heads:
                            nc.tensor.matmul(c.banks[u][:], c.ident_bf[:], c.zero[:].broadcast_to([P, BANK]), start=True, stop=False)
                        for i in range(2):
                            cols = slice((2 * u + i) * P, (2 * u + i + 1) * P)
                            for h in heads:
                                last = mm3(nc, c.banks[u][:, i * D:(i + 1) * D], ot_hi[:, h, cols], ot_lo[:, h, cols], wo_hi[:, h], wo_lo[:, h],
                                           False, i == 1 and h == GROUP - 1)
                        if GROUP - 1 in heads:
                            last.then_inc(s_o, 1)

                def turn(g, more):
                    for h in range(1, GROUP + 1):
                        if more or h < GROUP:
                            scores(g, h)
                        if more or h + 1 < GROUP:
                            proj(g, h + 1)
                        if not more and h == GROUP:
                            last_output(g, range(0, 3), range(0, 2))
                        transposes(g, h - 1)
                        pv(g, h - 1)
                    if more:
                        values(g)
                        output(g)
                    else:
                        last_output(g, range(0, 3), range(2, 3))
                        last_output(g, range(3, 4), range(0, 3))
                        last_output(g, range(0, 4), range(3, 4))

                proj(-1, GROUP)
                scores(-1, GROUP)
                proj(-1, GROUP + 1)
                values(-1)
                with pe.Fori(0, GROUPS - 1) as g:
                    turn(g, True)
                turn(GROUPS - 1, False)

            @block.scalar
            def _(act):
                act.sem_inc(s_exp, NT)
                act.sem_inc(s_pt_free, 2)

                def exps(g, h):
                    for q in range(2):
                        for b in range(B):
                            i, at, width = scores_bank(b, q)
                            if at == 0:
                                act.wait_ge(s_peak, g * (3 * GROUP) + (3 * h + i + 1))
                            n = q * B + b
                            nc.scalar.activation(probs[h % 2][:, i, at:at + width], c.banks[i][:, at:at + width], ACT.Exp, bias=neg_peak[:, n:n + 1],
                                                 scale=SCALE, accum_out=row_sum[:, h % 2, n:n + 1]).then_inc(s_exp, 1)

                def pt(g, h):
                    for i in range(3):
                        act.wait_ge(s_pt, g * (3 * GROUP) + (3 * h + i + 1))
                        nc.scalar.activation(probs_t[:, i * BANK:(i + 1) * BANK], c.banks[3 + (3 * h + i) % 2][:], ACT.Copy).then_inc(s_pt_free, 1)

                def pv(g, h):
                    for half in range(2):
                        n = g * (2 * GROUP) + (2 * h + half)
                        act.wait_ge(s_pv, n + 1)
                        act.wait_ge(s_ot_lo, n + 1)
                        act.sem_inc(s_seen, 1)
                        dst, src = attended[:, half * HALF:(half + 1) * HALF], ring_bank(("pv", h), half)[:]
                        if rope:
                            last = nc.scalar.activation(dst, src, ACT.Copy, scale=scale_row[:, bass.ds(g * GROUP + h, 1)])
                        else:
                            last = nc.scalar.activation(dst, src, ACT.Identity, bias=c.bias_t[:, bass.ds(g * GROUP + (h + 2 * HEADS), 1)])
                        last.then_inc(s_attended, 1)
                    for half in range(2):
                        act.wait_ge(s_attended, g * (2 * GROUP) + (2 * h + half + 1))
                        cols = slice(half * HALF, (half + 1) * HALF)
                        nc.scalar.activation(ot_hi[:, h, cols], attended[:, cols], ACT.Copy).then_inc(s_ot_hi, 1)

                def turn(g, more):
                    for h in range(1, GROUP + 1):
                        if more or h < GROUP - 1:
                            exps(g, h)
                        pt(g, h - 1)
                        if not more and h == GROUP - 1:
                            exps(g, h)
                        pv(g, h - 1)

                if rope:
                    act.wait_ge(s_table, 48)
                exps(-1, GROUP)
                with act.Fori(0, GROUPS - 1) as g:
                    turn(g, True)
                turn(GROUPS - 1, False)

            @block.vector
            def _(dve):
                own = Count(s_dve)
                dve.sem_inc(s_taken, RING)

                def proj(g, h, u):
                    n = proj_index(g, h, u)
                    what, half = units(h)[u]
                    cols = slice(half * HALF, (half + 1) * HALF)
                    bank = ring_bank(("proj", h), u)
                    dve.wait_ge(s_proj, n + (PROJ + 1))
                    if rope:
                        two = lambda ap: ap.rearrange("p (b t) -> p b t", b=2)
                        many = lambda ap, size: ap.unsqueeze(1).broadcast_to([size, 2, T])
                        if not (isinstance(n, int) and n < 2):
                            dve.wait_ge(s_rope, n - 1)
                        nc.vector.tensor_tensor(two(along[:, u % 2]), two(bank[:]), many(cos[:], P), ALU.mult)
                        for to, at in ((0, HALF_BLOCK), (HALF_BLOCK, 0)):
                            last = nc.vector.tensor_tensor(two(across[to:to + HALF_BLOCK, u % 2]), two(bank[at:at + HALF_BLOCK]),
                                                           many(sin[at:at + HALF_BLOCK], HALF_BLOCK), ALU.mult)
                        last.then_inc(s_taken, 1)
                    else:
                        head = g * GROUP + (h + (0 if what == "q" else HEADS))
                        nc.vector.tensor_scalar((queries if what == "q" else keys)[:, cols], bank[:], c.bias_t[:, bass.ds(head, 1)], None,
                                                ALU.add).then_inc(s_taken, 1)

                def values(g, u):
                    per = NT // VU
                    dve.wait_ge(s_v, g * VU + (2 * VU + u + 1))
                    nc.vector.tensor_copy(vals[:, u * per:(u + 1) * per].rearrange("p t n -> p (t n)"), ring_bank("v", u)[:]).then_inc(s_taken, 1)

                def rows_of(i):
                    return (0, B) if i == 0 else (B + 2 * (i - 1), 2)

                def peaks(g, h):
                    for i in range(3):
                        dve.wait_ge(s_scores, g * (3 * GROUP) + (3 * h + i + 1))
                        n, rows = rows_of(i)
                        done = own.inc(nc.vector.tensor_reduce(peak[:, n:n + rows], c.banks[i][:].rearrange("p (r k) -> p r k", r=rows), AX.X, ALU.max))
                        dve.wait_ge(s_dve, done)
                        nc.vector.tensor_scalar(neg_peak[:, n:n + rows], peak[:, n:n + rows], -SCALE, None, ALU.mult).then_inc(s_peak, 1)

                def norm(g, h, i):
                    n, rows = rows_of(i)
                    dve.wait_ge(s_exp, g * (GROUP * NT) + ((h + 1) * NT + n + rows))
                    done = own.inc(nc.vector.reciprocal(row_inv[:, h % 2, n:n + rows], row_sum[:, h % 2, n:n + rows]))
                    dve.wait_ge(s_dve, done)
                    width = BANK // rows
                    for r in range(rows):
                        part = probs[h % 2][:, i, r * width:(r + 1) * width]
                        last = nc.vector.tensor_scalar(part, part, row_inv[:, h % 2, n + r:n + r + 1], None, ALU.mult)
                    last.then_inc(s_norm, 1)

                def pv(g, h):
                    dve.wait_ge(s_taken, number(g, ("pv", h), 0) + RING)
                    for half in range(2):
                        dve.wait_ge(s_attended, g * (2 * GROUP) + (2 * h + half + 1))
                        dve.sem_inc(s_taken, 1)

                def output(g, u, bank):
                    dve.wait_ge(s_o, g * OU + (OU + u + 1))
                    rows = c.x[:, 2 * u:2 * u + 2].rearrange("p t n -> p (t n)")
                    nc.vector.tensor_tensor(rows, rows, bank[:], ALU.add).then_inc(s_taken, 1)

                def skip(g, step, count):
                    dve.wait_ge(s_taken, number(g, step, 0) + RING)
                    dve.sem_inc(s_taken, count)

                ROUNDS = -(-KEEP // 8)

                def threshold(tile, begin, end):
                    if rope:
                        return
                    if begin == 0:
                        nc.vector.tensor_copy(work[0][:], c.sim[:, bass.ds(tile, 1)].rearrange("p t n -> p (t n)"))
                    for op in range(begin, end):
                        r = op // 2
                        dve.drain()
                        if op % 2 == 0:
                            nc.vector.max(top8[:], work[r % 2][:])
                        elif r < ROUNDS - 1:
                            nc.vector.match_replace(work[1 - r % 2][:], top8[:], work[r % 2][:], -3e38)
                        else:
                            nc.vector.tensor_copy(c.thr[:, bass.ds(tile, 1)], top8[:, (KEEP - 1) % 8:(KEEP - 1) % 8 + 1])

                PART = 2 * ROUNDS // GROUP

                def turn(g, more):
                    for h in range(1, GROUP + 1):
                        if more or h < GROUP:
                            peaks(g, h)
                        count = len(units(h + 1))
                        search = (h - 1) * PART
                        if more or h + 1 < GROUP:
                            for u in range(count):
                                proj(g, h + 1, u)
                                if u < 2:
                                    threshold(g * 2, search + 2 * u, search + 2 * u + 2)
                            threshold(g * 2, search + 4, search + PART)
                        else:
                            skip(g, ("proj", h + 1), count)
                            threshold(g * 2, search, search + PART)
                        if more or h < GROUP:
                            for i in range(3):
                                norm(g, h, i)
                        pv(g, h - 1)
                    if more:
                        for u in range(VU):
                            values(g, u)
                            threshold(g * 2 + 1, u, u + 1)
                    for u in range(OU):
                        output(g, u, ring_bank("o", u) if more else c.banks[u])
                        if more:
                            threshold(g * 2 + 1, VU + u * 3, VU + u * 3 + 3)

                if rope:
                    dve.wait_ge(s_table, 48)
                for u in range(len(units(GROUP))):
                    proj(-1, GROUP, u)
                peaks(-1, GROUP)
                skip(-1, ("pv", GROUP - 2), 2)
                for u in range(len(units(GROUP + 1))):
                    proj(-1, GROUP + 1, u)
                for i in range(3):
                    norm(-1, GROUP, i)
                skip(-1, ("pv", GROUP - 1), 2)
                for u in range(VU):
                    values(-1, u)
                    threshold(NT - 1, u, u + 1)
                threshold(NT - 1, VU, 2 * ROUNDS)
                skip(-1, "o", OU)
                per_turn = GROUP * 6
                with dve.Fori(0, GROUPS - 1) as g:
                    own.enter(g, per_turn)
                    turn(g, True)
                own.leave(GROUPS - 1)
                turn(GROUPS - 1, False)


class Norm:

    def __init__(self, c, name, sb):
        self.c, self.nc = c, c.nc
        self.stats, self.mv = sb(f"{name}_stats", [P, NT, 6]), sb(f"{name}_mv", [P, NT, 2])
        self.shifted, self.rstd = sb(f"{name}_shifted", [P, NT]), sb(f"{name}_rstd", [P, NT])
        self.s_var, self.s_eps, self.s_rstd = (c.sem(f"{name}_{n}") for n in ("var", "eps", "rstd"))

    def moments(self, dve, tiles):
        for t in range(NT):
            self.nc.vector.bn_stats(self.stats[:, t], tiles(t))
        dve.drain()
        for t in range(NT):
            last = self.nc.vector.bn_aggr(self.mv[:, t], self.stats[:, t])
        last.then_inc(self.s_var, 1)

    def root(self, pool, factor=1.0, eps=EPS):
        pool.wait_ge(self.s_var, 1)
        self.nc.gpsimd.tensor_scalar(self.shifted[:], self.mv[:, :, 1], factor, eps, ALU.mult, ALU.add).then_inc(self.s_eps, 1)
        pool.wait_ge(self.s_eps, 1)
        self.nc.gpsimd.tensor_tensor(self.rstd[:], self.shifted[:], self.c.half_neg[:], ALU.pow).then_inc(self.s_rstd, 1)

    def apply(self, dve, t, dst, src):
        if t == 0:
            dve.wait_ge(self.s_rstd, 1)
        return self.nc.vector.tensor_scalar(dst, src, self.mv[:, t, 0:1], self.rstd[:, t:t + 1], ALU.subtract, ALU.mult)


class Transposed:

    def __init__(self, c, name):
        self.c, self.nc = c, c.nc
        self.s_tr, self.s_hi, self.s_lo = (c.sem(f"{name}_{n}") for n in ("tr", "hi", "lo"))
        self.order = [(h, k) for h in range(2) for k in range(KC)]

    def pe(self, pe, s_ready, per_half):
        for n, (h, k) in enumerate(self.order):
            pe.wait_ge(s_ready, per_half * (h + 1))
            for t in range(4):
                last = self.nc.tensor.transpose(self.c.banks[4 + n][:, t * P:(t + 1) * P], self.c.x[:, 4 * h + t, k * P:(k + 1) * P], self.c.ident[:])
            last.then_inc(self.s_tr, 1)

    def act(self, act):
        for n, (h, k) in enumerate(self.order):
            act.wait_ge(self.s_tr, n + 1)
            self.nc.scalar.activation(self.c.xt_hi[:, k, h * HALF:(h + 1) * HALF], self.c.banks[4 + n][:], ACT.Copy).then_inc(self.s_hi, 1)

    def dve(self, dve):
        for n, (h, k) in enumerate(self.order):
            dve.wait_ge(self.s_hi, n + 1)
            cols = slice(h * HALF, (h + 1) * HALF)
            self.nc.vector.tensor_tensor(self.c.xt_lo[:, k, cols], self.c.banks[4 + n][:], f32(self.c.xt_hi[:, k, cols]), ALU.subtract).then_inc(self.s_lo, 1)

    def wait(self, pe, half=1):
        pe.wait_ge(self.s_lo, KC * (half + 1))


def route(c, out, w_hi, w_lo, experts):
    for t in range(NT):
        cols = slice(t * P, (t + 1) * P)
        for k in range(KC):
            last = mm3(c.nc, out[:, t * experts:(t + 1) * experts], c.xt_hi[:, k, cols], c.xt_lo[:, k, cols], w_hi[:, k], w_lo[:, k], k == 0, k == KC - 1)
    return last


def graph_and_masked_experts(c, upto):
    nc, a = c.nc, c.a
    PAIRS = EXPERTS0 // 2
    RING = 4
    with ExitStack() as ctx:
        sb = lambda name, shape, dt=F32: ctx.enter_context(nc.sbuf_tensor(f"b_{name}", shape, dt))
        norm1, norm2, norm3 = (Norm(c, f"b_norm{i}", sb) for i in (1, 2, 3))
        turned2, turned3 = Transposed(c, "b_turned2"), Transposed(c, "b_turned3")
        gate_in = sb("gate_in", [P, NT, T])
        kept, mixed = sb("kept", [P, NT, T]), sb("mixed", [P, NT, T])
        quarter = sb("quarter", [P, 1])
        top, above, likely = sb("top", [P, NT]), sb("above", [P, NT, EXPERTS0]), sb("likely", [P, NT, EXPERTS0])
        total, weight = sb("total", [P, NT]), sb("weight", [P, NT])
        numbers, found, first = sb("numbers", [P, NT, EXPERTS0]), sb("found", [P, NT, EXPERTS0]), sb("first", [P, NT])
        chosen, gate = sb("chosen", [P, NT, EXPERTS0]), sb("gate", [P, NT, EXPERTS0])
        raw = [sb(f"raw{i}", [P, 2, KC, D]) for i in range(2)]
        masked = [sb(f"masked{i}", [P, 2, KC, D], BF16) for i in range(2)]
        w = [sb(f"w{i}", [P, KC, 2 * D], F32R) for i in range(2)]
        acc = [sb(f"acc{i}", [P, NT, D]) for i in range(2)]

        S = lambda name: c.sem(f"b_{name}")
        s_numbers, s_raw = S("numbers"), [S(f"raw{i}") for i in range(2)]
        s_tanh, s_kept, s_kept_t = S("tanh"), S("kept"), S("kept_t")
        s_mixed, s_norm1, s_norm2, s_norm3 = S("mixed"), S("norm1"), S("norm2"), S("norm3")
        s_logits, s_above, s_likely, s_acc0 = S("logits"), S("above"), S("likely"), S("acc0")
        s_masked, s_turned, s_w = S("masked"), S("turned"), S("w")
        s_out, s_used = S("out"), S("used")

        def raw_of(pair):
            masks = a["L0_ffn_expert_masks"].rearrange("(n e) (k p) i -> n p e k i", e=2, p=P)
            return masks[bass.ds(pair, 1)].rearrange("n p e k i -> p (n e) k i")

        with nc.Block() as block:
            @block.sync
            def _(sp):
                sp.dma_start(numbers[:], a["numbers"]).then_inc(s_numbers, 16)

                def load(i, j):
                    pair = i * 2 + j
                    sp.wait_ge(s_masked, pair + 1)
                    for e in range(2):
                        sp.dma_start(raw[j][:, e], a["L0_ffn_expert_masks"][bass.ds(pair * 2 + e, 1)].rearrange("n (k p) i -> p (n k) i", p=P)).then_inc(s_raw[j], 16)

                with sp.Fori(0, PAIRS // 2) as i:
                    load(i, 0)
                    load(i, 1)

            @block.gpsimd
            def _(pool):
                pool.sem_inc(s_masked, 2)
                for x in acc:
                    last = nc.gpsimd.memset(x[:], 0.0)
                last.then_inc(s_acc0, 1)
                norm1.root(pool)
                norm2.root(pool)

                def mask(i, j):
                    pair = i * 2 + j
                    pool.wait_ge(s_raw[j], i * 32 + 32)
                    pool.wait_ge(s_turned, pair + 1)
                    wide = c.tern[:].unsqueeze(1).broadcast_to([P, 2, KC, D])
                    nc.gpsimd.tensor_tensor(masked[j][:], raw[j][:], wide, ALU.mult).then_inc(s_masked, 1)

                with pool.Fori(0, PAIRS // 2) as i:
                    mask(i, 0)
                    mask(i, 1)
                norm3.root(pool)

            @block.tensor
            def _(pe):
                pe.sem_inc(s_turned, 2)
                pe.sem_inc(s_out, 2 * NT)
                for b in range(B):
                    pe.wait_ge(s_kept, b + 1)
                    for i in range(2):
                        for j in range(2):
                            last = nc.tensor.transpose(c.banks[b][:, i * T + j * P:i * T + (j + 1) * P], kept[:, 2 * b + j, i * P:(i + 1) * P], c.ident[:])
                    last.then_inc(s_kept_t, 1)
                turned2.pe(pe, s_norm2, 4)
                turned2.wait(pe)
                pe.wait_ge(s_mixed, 1)
                route(c, c.banks[0], c.rt_hi, c.rt_lo, EXPERTS0).then_inc(s_logits, 1)

                def turn(i, j):
                    pair = i * 2 + j
                    pe.wait_ge(s_masked, pair + 3)
                    pe.wait_ge(s_w, pair + 1)
                    bank = c.banks[6 + j][:].bitcast(BF16)
                    for k in range(KC):
                        for e in range(2):
                            for o in range(KC):
                                at = k * 2 * D + e * D + o * P
                                last = nc.tensor.transpose(bank[:, at:at + P], masked[j][:, e, o, k * P:(k + 1) * P], c.ident_bf[:])
                    last.then_inc(s_turned, 1)

                def products(i, j):
                    pair = i * 2 + j
                    pe.wait_ge(s_w, pair + 3)
                    for t in range(NT):
                        pe.wait_ge(s_used, i * (2 * NT) + (j * NT + t + 1))
                        out = c.banks[t % RING][:]
                        cols = slice(t * P, (t + 1) * P)
                        for k in range(KC):
                            nc.tensor.matmul(out, c.xt_hi[:, k, cols], w[j][:, k], start=k == 0, stop=False)
                            last = nc.tensor.matmul(out, c.xt_lo[:, k, cols], w[j][:, k], start=False, stop=k == KC - 1)
                        last.then_inc(s_out, 1)

                turned2.wait(pe)
                turn(0, 0)
                pe.wait_ge(s_above, 1)
                with pe.Fori(0, PAIRS // 2 - 1) as i:
                    turn(i, 1)
                    products(i, 0)
                    turn(i + 1, 0)
                    products(i, 1)
                turn(PAIRS // 2 - 1, 1)
                products(PAIRS // 2 - 1, 0)
                products(PAIRS // 2 - 1, 1)
                turned3.pe(pe, s_norm3, 4)

            @block.scalar
            def _(act):
                act.sem_inc(s_w, 2)
                nc.scalar.activation(gate_in[:], c.sim[:], ACT.Tanh, scale=0.5).then_inc(s_tanh, 1)
                turned2.act(act)
                act.wait_ge(s_above, 1)
                nc.scalar.activation(likely[:], above[:], ACT.Exp).then_inc(s_likely, 1)

                def weights(i, j):
                    pair = i * 2 + j
                    act.wait_ge(s_turned, pair + 3)
                    act.wait_ge(s_out, i * (2 * NT) + (j * NT + NT))
                    nc.scalar.activation(w[j][:].rearrange("p k n -> p (k n)"), c.banks[6 + j][:].bitcast(BF16), ACT.Copy).then_inc(s_w, 1)

                with act.Fori(0, PAIRS // 2) as i:
                    weights(i, 0)
                    weights(i, 1)
                turned3.act(act)

            @block.vector
            def _(dve):
                dve.sem_inc(s_used, RING)
                nc.vector.tensor_scalar(quarter[:], c.gamma[:], 0.25, None, ALU.mult)
                dve.wait_ge(s_tanh, 1)
                nc.vector.tensor_scalar(gate_in[:], gate_in[:], 1.0, None, ALU.add)
                dve.drain()
                for t in range(NT):
                    last = nc.vector.scalar_tensor_tensor(kept[:, t], c.sim[:, t], c.thr[:, t:t + 1], gate_in[:, t], ALU.is_ge, ALU.mult)
                    if t % 2:
                        last.then_inc(s_kept, 1)
                norm1.moments(dve, lambda t: c.x[:, t])
                for b in range(B):
                    dve.wait_ge(s_kept_t, b + 1)
                    rows = lambda v: v[:, 2 * b:2 * b + 2].rearrange("p t n -> p (t n)")
                    nc.vector.tensor_tensor(rows(mixed), rows(kept), c.banks[b][:], ALU.add)
                dve.drain()
                nc.vector.tensor_scalar(mixed[:], mixed[:], quarter[:], None, ALU.mult).then_inc(s_mixed, 1)
                for t in range(NT):
                    norm1.apply(dve, t, c.x[:, t], c.x[:, t])
                dve.drain()
                for t in range(NT):
                    nc.vector.scalar_tensor_tensor(c.x[:, t], c.x[:, t], c.one_less[:], mixed[:, t], ALU.mult, ALU.add)
                dve.drain()
                norm2.moments(dve, lambda t: c.x[:, t])
                for t in range(NT):
                    norm2.apply(dve, t, c.x[:, t], c.x[:, t]).then_inc(s_norm2, 1)
                turned2.dve(dve)

                dve.wait_ge(s_logits, 1)
                logits = c.banks[0][:, 0:NT * EXPERTS0].rearrange("p (t e) -> p t e", t=NT)
                wide = lambda v: v[:].unsqueeze(2).broadcast_to([P, NT, EXPERTS0])
                nc.vector.tensor_reduce(top[:], logits, AX.X, ALU.max)
                dve.drain()
                nc.vector.tensor_tensor(above[:], logits, wide(top), ALU.subtract).then_inc(s_above, 1)
                dve.drain()
                nc.vector.tensor_scalar(found[:], above[:], 0.0, -float(EXPERTS0), ALU.is_ge, ALU.mult)
                dve.wait_ge(s_numbers, 16)
                dve.drain()
                nc.vector.tensor_tensor(found[:], found[:], numbers[:], ALU.add)
                dve.drain()
                nc.vector.tensor_reduce(first[:], found[:], AX.X, ALU.min)
                dve.drain()
                nc.vector.tensor_scalar(first[:], first[:], float(EXPERTS0), None, ALU.add)
                dve.drain()
                nc.vector.tensor_tensor(chosen[:], numbers[:], wide(first), ALU.is_equal)
                dve.wait_ge(s_likely, 1)
                nc.vector.tensor_reduce(total[:], likely[:], AX.X, ALU.add)
                dve.drain()
                nc.vector.reciprocal(weight[:], total[:])
                dve.drain()
                nc.vector.tensor_tensor(gate[:], chosen[:], wide(weight), ALU.mult)
                dve.wait_ge(s_acc0, 1)
                dve.drain()
                flat = gate[:].rearrange("p t e -> p (t e)")

                def add(i, j):
                    for t in range(NT):
                        dve.wait_ge(s_out, i * (2 * NT) + (2 * NT + j * NT + t + 1))
                        for e in range(2):
                            g = flat[:, bass.ds(i * 4 + (t * EXPERTS0 + 2 * j + e), 1)]
                            last = nc.vector.scalar_tensor_tensor(acc[e][:, t], c.banks[t % RING][:, e * D:(e + 1) * D], g, acc[e][:, t], ALU.mult, ALU.add)
                        last.then_inc(s_used, 1)

                with dve.Fori(0, PAIRS // 2) as i:
                    add(i, 0)
                    add(i, 1)
                dve.drain()
                nc.vector.tensor_tensor(acc[0][:], acc[0][:], acc[1][:], ALU.add)
                dve.drain()
                nc.vector.tensor_tensor(acc[0][:], acc[0][:], c.rows[:, ROW_SCALE].unsqueeze(1).broadcast_to([P, NT, D]), ALU.mult)
                dve.drain()
                nc.vector.tensor_tensor(c.x[:], c.x[:], acc[0][:], ALU.add)
                dve.drain()
                norm3.moments(dve, lambda t: c.x[:, t])
                for t in range(NT):
                    norm3.apply(dve, t, c.x[:, t], c.x[:, t]).then_inc(s_norm3, 1)
                turned3.dve(dve)


def cross_and_experts(c, upto):
    nc, a = c.nc, c.a
    PIECES = EXPERTS1 + SHARED
    OUT = NT // 2
    with ExitStack() as ctx:
        sb = lambda name, shape, dt=F32: ctx.enter_context(nc.sbuf_tensor(f"d_{name}", shape, dt))
        norm4, norm_s, norm5, norm6 = (Norm(c, f"d_norm{i}", sb) for i in "4s56")
        turned4, turned5 = Transposed(c, "d_turned4"), Transposed(c, "d_turned5")
        ot_hi, ot_lo = sb("ot_hi", [DC, NTOK], F32R), sb("ot_lo", [DC, NTOK], F32R)
        rstd16 = sb("rstd16", [P, NT])
        scores, probs = sb("scores", [P, NT, T]), sb("probs", [P, NT, T])
        peak, row_sum, row_inv = sb("peak", [P, NT]), sb("row_sum", [P, NT]), sb("row_inv", [P, NT])
        wr, wr_hi, wr_lo = sb("wr", [P, KC, EXPERTS1]), sb("wr_hi", [P, KC, EXPERTS1], F32R), sb("wr_lo", [P, KC, EXPERTS1], F32R)
        logits = sb("logits", [P, NT, EXPERTS1])
        best, more, same, room = sb("best", [P, NT, 8]), sb("more", [P, NT, EXPERTS1]), sb("same", [P, NT, EXPERTS1]), sb("room", [P, NT])
        rank = [sb(f"rank{i}", [P, NT, EXPERTS1]) for i in range(2)]
        above, likely = sb("above", [P, NT, EXPERTS1]), sb("likely", [P, NT, EXPERTS1])
        total, weight = sb("total", [P, NT]), sb("weight", [P, NT])
        gate, primed = sb("gate", [P, NT, PIECES]), sb("primed", [P, 1])
        raw = [sb(f"raw{i}", [P, 3, D]) for i in range(2)]
        w_hi, w_lo = ([sb(f"w_{n}{i}", [P, 3, D], F32R) for i in range(2)] for n in ("hi", "lo"))
        silu, act_full = sb("silu", [P, 2, HALF]), [sb(f"h{i}", [HID, NTOK]) for i in range(2)]
        h_hi, h_lo = ([sb(f"h_{n}{i}", [HID, NTOK], F32R) for i in range(2)] for n in ("hi", "lo"))

        S = lambda name: c.sem(f"d_{name}")
        s_wr, s_wr_hi, s_wr_lo = S("wr"), S("wr_hi"), S("wr_lo")
        s_norm4, s_ot, s_ot_hi, s_ot_lo = S("norm4"), S("ot"), S("ot_hi"), S("ot_lo")
        s_sim, s_peak, s_exp, s_norm5, s_rstd16 = S("sim"), S("peak"), S("exp"), S("norm5"), S("rstd16")
        s_scored = S("scored")
        s_logits, s_above, s_likely = S("logits"), S("above"), S("likely")
        s_raw_up, s_raw_down = ([S(f"raw_{n}{i}") for i in range(2)] for n in ("up", "down"))
        s_split_up, s_split_down, s_pool = S("split_up"), S("split_down"), S("pool")
        s_up, s_silu, s_h, s_h_hi, s_h_lo = S("up"), S("silu"), S("h"), S("h_hi"), S("h_lo")
        s_out, s_used, s_norm6, s_store = S("out"), S("used"), S("norm6"), S("store")

        with nc.Block() as block:
            @block.sync
            def _(sp):
                sp.dma_start(wr[:], a["L1_ffn_w_router"].rearrange("(k p) e -> p k e", p=P)).then_inc(s_wr, 16)

                def load(j, done, first, third, second):
                    sp.wait_ge(s_split_up, done)
                    sp.dma_start(raw[j][:, 0].rearrange("p (k n) -> p k n", k=KC), first).then_inc(s_raw_up[j], 16)
                    sp.dma_start(raw[j][:, 1].rearrange("p (k n) -> p k n", k=KC), third).then_inc(s_raw_up[j], 16)
                    sp.wait_ge(s_split_down, done)
                    sp.dma_start(raw[j][:, 2], second).then_inc(s_raw_down[j], 16)

                with sp.Fori(0, EXPERTS1 // 2) as i:
                    for j in range(2):
                        one = bass.ds(i * 2 + j, 1)
                        load(j, i * 2 + (j + 1), *(a[f"L1_ffn_we{n}"][one].rearrange("n (k p) h -> p (n k) h", p=P) for n in (1, 3)),
                             a["L1_ffn_we2"][one].rearrange("n h d -> h (n d)"))
                for e in range(EXPERTS1, PIECES):
                    cols = slice((e - EXPERTS1) * HID, (e - EXPERTS1 + 1) * HID)
                    load(e % 2, e + 1, *(a[f"L1_ffn_ws{n}"][:, cols].rearrange("(k p) h -> p k h", p=P) for n in (1, 3)), a["L1_ffn_ws2"][cols, :])
                for b in range(B):
                    sp.wait_ge(s_norm6, 2 * b + 2)
                    sp.dma_start(c.out[b].rearrange("(t p) d -> p t d", p=P), c.x[:, 2 * b:2 * b + 2]).then_inc(s_store, 16)
                sp.wait_ge(s_store, 16 * B)

            @block.gpsimd
            def _(pool):
                own = Count(s_pool)
                pool.sem_inc(s_split_up, 2)
                pool.sem_inc(s_split_down, 2)
                norm4.root(pool)
                norm_s.root(pool, 1.0 / 256, 1e-6)
                pool.wait_ge(norm_s.s_rstd, 1)
                nc.gpsimd.tensor_scalar(rstd16[:], norm_s.rstd[:], 1.0 / 16, None, ALU.mult).then_inc(s_rstd16, 1)
                norm5.root(pool)

                def split(j, part, done):
                    width = part.stop - part.start
                    n = own.inc(nc.gpsimd.tensor_tensor(w_hi[j][:, part], raw[j][:, part], c.one[:].unsqueeze(1).broadcast_to([P, width, D]), ALU.mult))
                    pool.wait_ge(s_pool, n)
                    nc.gpsimd.tensor_tensor(w_lo[j][:, part], raw[j][:, part], f32(w_hi[j][:, part]), ALU.subtract).then_inc(done, 1)

                def split_up(i, j):
                    pool.wait_ge(s_raw_up[j], i * 32 + 32)
                    pool.wait_ge(s_up, i * 8 + (4 * j + 4))
                    split(j, slice(0, 2), s_split_up)

                def split_down(i, j):
                    pool.wait_ge(s_raw_down[j], i * 16 + 16)
                    pool.wait_ge(s_out, i * (2 * OUT) + (j + 1) * OUT)
                    split(j, slice(2, 3), s_split_down)

                def low(i, j):
                    for half in range(2):
                        pool.wait_ge(s_h_hi, i * 4 + (2 * j + half + 1))
                        cols = slice(half * HALF, (half + 1) * HALF)
                        nc.gpsimd.tensor_tensor(h_lo[j][:, cols], act_full[j][:, cols], f32(h_hi[j][:, cols]), ALU.subtract).then_inc(s_h_lo, 1)

                def turn(i, more):
                    split_up(i, 1)
                    low(i, 0)
                    split_down(i, 0)
                    if more:
                        split_up(i + 1, 0)
                    low(i, 1)
                    split_down(i, 1)

                split_up(0, 0)
                with pool.Fori(0, PIECES // 2 - 1) as i:
                    own.enter(i, 4)
                    turn(i, True)
                own.leave(PIECES // 2 - 1)
                turn(PIECES // 2 - 1, False)
                norm6.root(pool)

            @block.tensor
            def _(pe):
                pe.sem_inc(s_out, 2 * OUT)
                pe.sem_inc(s_up, 8)
                turned4.pe(pe, s_norm4, 4)
                turned4.wait(pe)
                for b in range(B):
                    rows = slice(b * T, (b + 1) * T)
                    for k in range(KC):
                        last = mm3(nc, c.banks[b // 2][:, (b % 2) * T:(b % 2 + 1) * T], c.kv_hi[:, 2 * b + k], c.kv_lo[:, 2 * b + k],
                                   c.xt_hi[:, k, rows], c.xt_lo[:, k, rows], k == 0, k == KC - 1)
                    if b % 2:
                        last.then_inc(s_ot, 1)
                for b in range(B):
                    pe.wait_ge(s_ot_lo, b // 2 + 1)
                    if b == 2:
                        pe.wait_ge(s_ot_lo, 2)
                    bank = c.banks[(2, 3, 0, 1)[b]]
                    keys = slice(b * T, (b + 1) * T)
                    for i in range(2):
                        rows = slice(b * T + i * P, b * T + (i + 1) * P)
                        last = mm3(nc, bank[:, i * T:(i + 1) * T], ot_hi[:, rows], ot_lo[:, rows], c.kvt_hi[:, keys], c.kvt_lo[:, keys], True, True)
                    last.then_inc(s_sim, 1)
                turned5.pe(pe, s_norm5, 4)
                turned5.wait(pe)
                pe.wait_ge(s_wr_lo, 1)
                pe.wait_ge(s_scored, 1)
                route(c, c.banks[4], wr_hi, wr_lo, EXPERTS1).then_inc(s_logits, 1)

                def up(i, j):
                    piece = i * 2 + j
                    pe.wait_ge(s_split_up, piece + 3)
                    for half in range(2):
                        pe.wait_ge(s_h, piece * 2 + (half + 1))
                        cols = slice(half * HALF, (half + 1) * HALF)
                        for n in range(2):
                            for k in range(KC):
                                s = slice(k * HID, (k + 1) * HID)
                                last = mm3(nc, c.banks[2 * half + n][:], w_hi[j][:, n, s], w_lo[j][:, n, s], c.xt_hi[:, k, cols], c.xt_lo[:, k, cols],
                                           k == 0, k == KC - 1)
                            last.then_inc(s_up, 1)

                def down(i, j):
                    pe.wait_ge(s_h_lo, i * 4 + (2 * j + 2))
                    pe.wait_ge(s_split_down, i * 2 + (j + 3))
                    for u in range(OUT):
                        pe.wait_ge(s_used, i * (2 * OUT) + (j * OUT + u + 1))
                        for t in range(2):
                            cols = slice((2 * u + t) * P, (2 * u + t + 1) * P)
                            last = mm3(nc, c.banks[4 + u][:, t * D:(t + 1) * D], h_hi[j][:, cols], h_lo[j][:, cols], w_hi[j][:, 2], w_lo[j][:, 2], True, True)
                        last.then_inc(s_out, 1)

                up(0, 0)
                pe.wait_ge(s_above, 1)
                with pe.Fori(0, PIECES // 2 - 1) as i:
                    up(i, 1)
                    down(i, 0)
                    up(i + 1, 0)
                    down(i, 1)
                up(PIECES // 2 - 1, 1)
                down(PIECES // 2 - 1, 0)
                down(PIECES // 2 - 1, 1)

            @block.scalar
            def _(act):
                act.wait_ge(s_wr, 16)
                nc.scalar.activation(wr_hi[:], wr[:], ACT.Copy).then_inc(s_wr_hi, 1)
                turned4.act(act)
                for h in range(2):
                    act.wait_ge(s_ot, h + 1)
                    nc.scalar.activation(ot_hi[:, h * HALF:(h + 1) * HALF], c.banks[h][0:DC], ACT.Copy).then_inc(s_ot_hi, 1)
                for t in range(NT):
                    act.wait_ge(s_peak, 1)
                    nc.scalar.activation(probs[:, t], scores[:, t], ACT.Exp, bias=peak[:, t:t + 1], accum_out=row_sum[:, t:t + 1]).then_inc(s_exp, 1)
                turned5.act(act)
                act.wait_ge(s_above, 1)
                nc.scalar.activation(likely[:], above[:], ACT.Exp).then_inc(s_likely, 1)

                def hidden(i, j):
                    for half in range(2):
                        act.wait_ge(s_up, i * 8 + (8 + 4 * j + 2 * half + 1))
                        act.wait_ge(s_h, i * 4 + (2 * j + half + 1))
                        nc.scalar.activation(silu[:, half], c.banks[2 * half][:], ACT.Silu).then_inc(s_silu, 1)
                        act.wait_ge(s_h, i * 4 + (2 * j + half + 3))
                        cols = slice(half * HALF, (half + 1) * HALF)
                        nc.scalar.activation(h_hi[j][:, cols], act_full[j][:, cols], ACT.Copy).then_inc(s_h_hi, 1)

                nc.scalar.activation(primed[:], c.one[:], ACT.Silu)
                with act.Fori(0, PIECES // 2) as i:
                    hidden(i, 0)
                    hidden(i, 1)

            @block.vector
            def _(dve):
                dve.sem_inc(s_h, 2)
                dve.sem_inc(s_used, OUT)
                norm4.moments(dve, lambda t: c.x[:, t])
                dve.wait_ge(s_wr_hi, 1)
                nc.vector.tensor_tensor(wr_lo[:], wr[:], f32(wr_hi[:]), ALU.subtract).then_inc(s_wr_lo, 1)
                for t in range(NT):
                    norm4.apply(dve, t, c.x[:, t], c.x[:, t]).then_inc(s_norm4, 1)
                turned4.dve(dve)
                for h in range(2):
                    dve.wait_ge(s_ot_hi, h + 1)
                    cols = slice(h * HALF, (h + 1) * HALF)
                    nc.vector.tensor_tensor(ot_lo[:, cols], c.banks[h][0:DC], f32(ot_hi[:, cols]), ALU.subtract).then_inc(s_ot_lo, 1)

                tile = lambda t: c.banks[(2, 3, 0, 1)[t // 2]][:, (t % 2) * T:(t % 2 + 1) * T]
                dve.wait_ge(s_sim, B)
                norm_s.moments(dve, tile)
                dve.wait_ge(s_rstd16, 1)
                for t in range(NT):
                    last = nc.vector.tensor_scalar(scores[:, t], tile(t), norm_s.mv[:, t, 0:1], rstd16[:, t:t + 1], ALU.subtract, ALU.mult)
                last.then_inc(s_scored, 1)
                dve.drain()
                row = lambda r: c.rows[:, r].unsqueeze(1).broadcast_to([P, NT, T])
                nc.vector.tensor_tensor(scores[:], scores[:], row(ROW_GAMMA), ALU.mult)
                dve.drain()
                nc.vector.tensor_tensor(scores[:], scores[:], row(ROW_BETA), ALU.add)
                dve.drain()
                nc.vector.tensor_reduce(peak[:], scores[:], AX.X, ALU.max)
                dve.drain()
                nc.vector.tensor_scalar(peak[:], peak[:], -1.0, None, ALU.mult).then_inc(s_peak, 1)
                dve.wait_ge(s_exp, NT)
                nc.vector.reciprocal(row_inv[:], row_sum[:])
                dve.drain()
                for t in range(NT):
                    nc.vector.scalar_tensor_tensor(c.x[:, t], probs[:, t], row_inv[:, t:t + 1], c.x[:, t], ALU.mult, ALU.add)
                dve.drain()
                norm5.moments(dve, lambda t: c.x[:, t])
                for t in range(NT):
                    norm5.apply(dve, t, c.x[:, t], c.x[:, t]).then_inc(s_norm5, 1)
                turned5.dve(dve)

                wide = lambda v: v.broadcast_to([P, NT, EXPERTS1])
                dve.wait_ge(s_logits, 1)
                nc.vector.tensor_copy(logits[:], c.banks[4][:, 0:NT * EXPERTS1].rearrange("p (t e) -> p t e", t=NT))
                dve.drain()
                for t in range(NT):
                    nc.vector.max(best[:, t], logits[:, t])
                dve.drain()
                nc.vector.tensor_tensor(above[:], logits[:], wide(best[:, :, 0:1]), ALU.subtract).then_inc(s_above, 1)
                nc.vector.tensor_tensor(more[:], logits[:], wide(best[:, :, TOPK - 1:TOPK]), ALU.is_gt)
                nc.vector.tensor_tensor(same[:], logits[:], wide(best[:, :, TOPK - 1:TOPK]), ALU.is_equal)
                dve.drain()
                nc.vector.tensor_reduce(room[:], more[:], AX.X, ALU.add)
                nc.vector.tensor_copy(rank[0][:], same[:])
                dve.drain()
                nc.vector.tensor_scalar(room[:], room[:], -1.0, float(TOPK), ALU.mult, ALU.add)
                step = 1
                at = 0
                while step < EXPERTS1:
                    nc.vector.tensor_tensor(rank[1 - at][:, :, step:], rank[at][:, :, step:], rank[at][:, :, :-step], ALU.add)
                    nc.vector.tensor_copy(rank[1 - at][:, :, 0:step], rank[at][:, :, 0:step])
                    dve.drain()
                    step, at = 2 * step, 1 - at
                nc.vector.tensor_tensor(rank[1 - at][:], rank[at][:], wide(room[:].unsqueeze(2)), ALU.is_le)
                dve.drain()
                nc.vector.tensor_tensor(same[:], same[:], rank[1 - at][:], ALU.mult)
                dve.drain()
                nc.vector.tensor_tensor(more[:], more[:], same[:], ALU.add)
                dve.wait_ge(s_likely, 1)
                dve.drain()
                nc.vector.tensor_tensor(likely[:], likely[:], more[:], ALU.mult)
                dve.drain()
                nc.vector.tensor_reduce(total[:], likely[:], AX.X, ALU.add)
                nc.vector.memset(gate[:, :, EXPERTS1:], 1.0 / (TOPK + 1))
                dve.drain()
                nc.vector.reciprocal(weight[:], total[:])
                dve.drain()
                nc.vector.tensor_scalar(weight[:], weight[:], TOPK / (TOPK + 1), None, ALU.mult)
                dve.drain()
                nc.vector.tensor_tensor(gate[:, :, 0:EXPERTS1], likely[:], wide(weight[:].unsqueeze(2)), ALU.mult)
                dve.drain()
                flat = gate[:].rearrange("p t e -> p (t e)")

                def hidden(i, j):
                    for half in range(2):
                        dve.wait_ge(s_silu, i * 4 + (2 * j + half + 1))
                        dve.wait_ge(s_up, i * 8 + (8 + 4 * j + 2 * half + 2))
                        cols = slice(half * HALF, (half + 1) * HALF)
                        nc.vector.tensor_tensor(act_full[j][:, cols], silu[:, half], c.banks[2 * half + 1][:], ALU.mult).then_inc(s_h, 1)

                def add(i, j):
                    for u in range(OUT):
                        dve.wait_ge(s_out, i * (2 * OUT) + (2 * OUT + j * OUT + u + 1))
                        for t in range(2 * u, 2 * u + 2):
                            g = flat[:, bass.ds(i * 2 + (t * PIECES + j), 1)]
                            last = nc.vector.scalar_tensor_tensor(c.x[:, t], c.banks[4 + u][:, (t % 2) * D:(t % 2 + 1) * D], g, c.x[:, t], ALU.mult, ALU.add)
                        last.then_inc(s_used, 1)

                hidden(0, 0)
                with dve.Fori(0, PIECES // 2 - 1) as i:
                    hidden(i, 1)
                    add(i, 0)
                    hidden(i + 1, 0)
                    add(i, 1)
                hidden(PIECES // 2 - 1, 1)
                add(PIECES // 2 - 1, 0)
                add(PIECES // 2 - 1, 1)
                dve.drain()
                norm6.moments(dve, lambda t: c.x[:, t])
                for t in range(NT):
                    norm6.apply(dve, t, c.x[:, t], c.x[:, t]).then_inc(s_norm6, 1)


_INS = ['x', 'ctx_512', 'L0_attn_w_q', 'L0_attn_b_q', 'L0_attn_w_k', 'L0_attn_b_k', 'L0_attn_w_v', 'L0_attn_b_v',
        'L0_attn_w_o', 'L0_attn_b_o', 'L0_xattn_Wq', 'L0_xattn_Wk', 'L0_xattn_gamma_raw', 'L0_ffn_weight', 'L0_ffn_scale',
        'L0_ffn_expert_masks', 'L0_ffn_router_w', 'L1_attn_Wq', 'L1_attn_Wk', 'L1_attn_Wv', 'L1_attn_Wo',
        'L1_attn_head_scale', 'L1_xattn_W_k', 'L1_xattn_b_k', 'L1_xattn_ln_gamma', 'L1_xattn_ln_beta', 'L1_ffn_w_router',
        'L1_ffn_we1', 'L1_ffn_we3', 'L1_ffn_we2', 'L1_ffn_ws1', 'L1_ffn_ws3', 'L1_ffn_ws2']


def constants():
    import numpy as np
    freq = (1.0 / np.float32(10000.0) ** (np.arange(0, DH, 2, dtype=np.float32) / np.float32(DH))).astype(np.float32)
    angle = np.arange(T, dtype=np.float32)[None, :] * freq[:, None]
    cos, sin = np.cos(angle).astype(np.float32), np.sin(angle).astype(np.float32)
    return {
        "ident": np.eye(P, dtype=np.float32),
        "causal": np.triu(np.full((P, P), -1e30, np.float32), 1),
        "numbers": np.tile(np.arange(EXPERTS0, dtype=np.float32), (P, NT, 1)),
        "cos": np.concatenate([cos, cos]),
        "sin": np.concatenate([sin, -sin]),
    }


UPTO = 99


def kernel(**inputs):
    import numpy as _np
    import concourse.bacc as _bacc
    from concourse.bass_utils import run_bass_kernel_spmd as _run

    nc = _bacc.Bacc("TRN2", target_bir_lowering=False, num_devices=1)
    arrays, args = {}, {}
    for name, value in [(n, inputs[n]) for n in _INS] + list(constants().items()):
        v = _np.ascontiguousarray(value)
        if v.ndim == 0:
            v = v.reshape(1)
        arrays[f"in_{name}_dram"] = v
        args[name] = nc.dram_tensor(f"in_{name}_dram", v.shape, mybir.dt.from_np(v.dtype), kind="ExternalInput").ap()
    out = nc.dram_tensor("out_0_dram", (B, T, D), F32, kind="ExternalOutput").ap()
    decoder(nc, args, out, UPTO)
    r = _run(nc, [arrays], core_ids=[0])
    return r.results[0]["out_0_dram"]
```

```python
import concourse.bass as bass
from concourse import mybir
from contextlib import ExitStack

F32 = mybir.dt.float32
F32R = mybir.dt.float32r
BF16 = mybir.dt.bfloat16
ALU = mybir.AluOpType
ACT = mybir.ActivationFunctionType
AX = mybir.AxisListType

P = 128
B, T, D = 4, 256, 256
NT = B * T // P
KC = D // P
NTOK = B * T
HALF = NTOK // 2
BANK = 512
HEADS, DH = 16, 128
GROUP = 4
GROUPS = HEADS // GROUP
SCALE = DH ** -0.5
DC = 64
EPS = 1e-5
EXPERTS0 = 32
EXPERTS1, HID, TOPK = 16, 128, 4
SHARED = 512 // HID
KEEP = int(T * 0.3)
HALF_BLOCK = DH // 2
HALF_TILES = (range(0, NT // 2), range(NT // 2, NT))


class Count:

    def __init__(self, sem):
        self.sem, self.base, self.n = sem, 0, 0

    def inc(self, instruction):
        instruction.then_inc(self.sem, 1)
        self.n += 1
        return self.base + self.n

    def enter(self, i, per_turn):
        self.entry, self.per_turn = self.base + self.n, per_turn
        self.base, self.n = self.entry + i * per_turn, 0

    def leave(self, turns):
        assert self.n == self.per_turn, (self.n, self.per_turn)
        self.base, self.n = self.entry + turns * self.per_turn, 0

    @property
    def now(self):
        return self.base + self.n


def f32(ap):
    return ap.bitcast(F32)


class Chip:
    pass


def decoder(nc, a, out):
    with ExitStack() as ctx:
        c = Chip()
        c.nc, c.a, c.out = nc, a, out
        c.sem = lambda name: ctx.enter_context(nc.semaphore(name))
        sb = lambda name, shape, dt=F32: ctx.enter_context(nc.sbuf_tensor(name, shape, dt))
        c.banks = [ctx.enter_context(nc.psum_tensor(f"bank{i}", [P, BANK], F32)) for i in range(8)]
        c.x = sb("x", [P, NT, D])
        c.xt_hi, c.xt_lo = sb("xt_hi", [P, KC, NTOK], F32R), sb("xt_lo", [P, KC, NTOK], F32R)
        c.ident = sb("ident", [P, P])
        c.ident_bf = sb("ident_bf", [P, P], BF16)
        c.causal = sb("causal", [P, B, P], BF16)
        c.sim = sb("sim", [P, NT, T])
        c.thr = sb("thr", [P, NT])
        c.kv = sb("kv", [P, NT, P])
        c.kv_hi, c.kv_lo = sb("kv_hi", [P, NT, P], F32R), sb("kv_lo", [P, NT, P], F32R)
        c.kvt_hi, c.kvt_lo = sb("kvt_hi", [P, NTOK], F32R), sb("kvt_lo", [P, NTOK], F32R)
        c.kvg_hi, c.kvg_lo = sb("kvg_hi", [P, NTOK], F32R), sb("kvg_lo", [P, NTOK], F32R)
        c.kvt = sb("kvt", [P, NTOK])
        c.kvt_sum, c.kvt_mean = sb("kvt_sum", [P, B]), sb("kvt_mean", [P, B])
        c.bias_t = sb("bias_t", [P, 3 * HEADS])
        c.rt = sb("rt", [P, KC, P // (2 * EXPERTS0), 2, EXPERTS0], F32R)
        c.pick = {n: sb(f"pick{n}", [2 * n, n]) for n in (EXPERTS0, EXPERTS1)}
        c.rows = sb("rows", [P, 5, D])
        c.ffn_weight, c.clipped, c.tern = sb("ffn_weight", [P, KC, D]), sb("clipped", [P, KC, D]), sb("tern", [P, KC, D], BF16)
        c.s_ffn_weight = c.sem("ffn_weight")
        c.gamma, c.one_less = sb("gamma", [P, 1]), sb("one_less", [P, 1])
        c.zero, c.idle = sb("zero", [P, 1], BF16), sb("idle", [P, BANK], BF16)
        c.half_neg, c.one = sb("half_neg", [P, NT]), sb("one", [P, 1])
        c.quarter = sb("quarter", [P, 1])
        with AttentionWeights(c, 0) as weights:
            setup(c, weights)
            attention(c, 0, weights)
        with AttentionWeights(c, 1) as weights:
            graph_and_masked_experts(c, weights)
            attention(c, 1, weights)
        cross_and_experts(c)


def mm3(nc, out, l_hi, l_lo, r_hi, r_lo, start, stop):
    nc.tensor.matmul(out, l_hi, r_hi, start=start, stop=False)
    nc.tensor.matmul(out, l_hi, r_lo, start=False, stop=False)
    return nc.tensor.matmul(out, l_lo, r_hi, start=False, stop=stop)


LOW = slice(DC, 2 * DC)


def mm_stacked(nc, out, stacked, hi, lo, moving):
    for twice, start in ((hi, True), (lo, False)):
        l, r = (twice, stacked) if moving else (stacked, twice)
        last = nc.tensor.matmul(out, l, r, start=start, stop=not start)
    return last


def keep_warm(c, count):
    for _ in range(count):
        c.nc.tensor.matmul(c.banks[3][:], c.idle[:, 0:P], c.idle[:], start=True, stop=True)


ROW_BO, ROW_SCALE, ROW_GAMMA, ROW_BETA, ROW_BK = range(5)


def setup(c, weights):
    nc, a = c.nc, c.a
    with ExitStack() as ctx:
        sb = lambda name, shape, dt=F32: ctx.enter_context(nc.sbuf_tensor(name, shape, dt))
        ctx_nat = sb("ctx_nat", [P, NT, 2, DC])
        ctxt_hi, ctxt_lo = sb("ctxt_hi", [P, NTOK], F32R), sb("ctxt_lo", [P, NTOK], F32R)
        w_nat = sb("w_nat", [DC, 3, 2, DC])
        wt, qt = sb("wt", [P, 3, 2, DC], F32R), sb("qt", [P, NTOK], F32R)
        kt_hi, kt_lo = sb("kt_hi", [P, NTOK], F32R), sb("kt_lo", [P, NTOK], F32R)
        bias_nat = sb("bias_nat", [3 * HEADS, DH])
        r_nat = sb("r_nat", [EXPERTS0, D])
        causal_f = sb("causal_f", [P, P])
        g_raw, g_exp, g_den = sb("g_raw", [P, 1]), sb("g_exp", [P, 1]), sb("g_den", [P, 1])

        s_x = [c.sem(f"su_x{h}") for h in range(2)]
        s_ctx, s_w, s_const, s_bias, s_rows = (c.sem(f"su_{n}") for n in ("ctx", "w", "const", "bias", "rows"))
        s_idle = c.sem("su_idle")
        s_twice = c.sem("su_twice")
        s_tr = c.sem("su_tr")
        s_hi = c.sem("su_hi")
        s_lo = c.sem("su_lo")

        bank = c.banks
        with nc.Block() as block:
            @block.sync
            def _(sp):
                sp.dma_start(c.ident[:], a["ident"]).then_inc(s_const, 16)
                for h in range(2):
                    sp.dma_start(c.x[:, 4 * h:4 * h + 4], a["x"][2 * h:2 * h + 2].rearrange("b (t p) d -> p (b t) d", p=P)).then_inc(s_x[h], 16)
                    if h == 0:
                        sp.dma_start(ctx_nat[:, :, 0], a["ctx_512"].rearrange("b (t p) d -> p (b t) d", p=P)).then_inc(s_ctx, 16)
                for i, n in enumerate(("L0_xattn_Wq", "L0_xattn_Wk", "L1_xattn_W_k")):
                    sp.dma_start(w_nat[:, i, 0], a[n]).then_inc(s_w, 16)
                sp.dma_start(r_nat[:], a["L0_ffn_router_w"]).then_inc(s_w, 16)
                for i, n in enumerate(("b_q", "b_k", "b_v")):
                    sp.dma_start(bias_nat[i * HEADS:(i + 1) * HEADS], a[f"L0_attn_{n}"].rearrange("(h d) -> h d", d=DH)).then_inc(s_w, 16)
                weights.first_loads(sp)
                sp.dma_start(causal_f[:], a["causal"]).then_inc(s_bias, 16)
                sp.dma_start(c.ffn_weight[:], a["L0_ffn_weight"].rearrange("(k p) i -> p k i", p=P)).then_inc(c.s_ffn_weight, 16)
                sp.dma_start(g_raw[:], a["L0_xattn_gamma_raw"].partition_broadcast(P)).then_inc(s_bias, 16)
                sp.dma_start(c.rows[:, ROW_BK, 0:DC], a["L1_xattn_b_k"].partition_broadcast(P)).then_inc(s_rows, 16)
                sp.dma_start(c.rows[:, ROW_BK, DC:P], a["L1_xattn_b_k"].partition_broadcast(P)).then_inc(s_rows, 16)
                for r, n in ((ROW_BO, "L0_attn_b_o"), (ROW_SCALE, "L0_ffn_scale"), (ROW_GAMMA, "L1_xattn_ln_gamma"), (ROW_BETA, "L1_xattn_ln_beta")):
                    sp.dma_start(c.rows[:, r], a[n].partition_broadcast(P)).then_inc(s_rows, 16)

            @block.tensor
            def _(pe):
                pe.wait_ge(s_idle, 1)
                keep_warm(c, 9)
                pe.wait_ge(s_const, 16)
                for h in range(2):
                    pe.wait_ge(s_x[h], 16)
                    for k in range(KC):
                        for t in range(4):
                            last = nc.tensor.transpose(bank[3 + 2 * k + h][:, t * P:(t + 1) * P], c.x[:, 4 * h + t, k * P:(k + 1) * P], c.ident[:])
                        last.then_inc(s_tr, 1)
                pe.wait_ge(s_twice, 1)
                for h in range(2):
                    for t in range(4):
                        last = nc.tensor.transpose(bank[h][:, t * P:(t + 1) * P], ctx_nat[:, 4 * h + t].rearrange("p a d -> p (a d)"), c.ident[:])
                    last.then_inc(s_tr, 1)
                pe.wait_ge(s_twice, 2)
                for i in range(3):
                    nc.tensor.transpose(bank[2][:, i * DC:(i + 1) * DC], w_nat[:, i].rearrange("p a d -> p (a d)"), c.ident[0:DC, 0:DC])
                pe.wait_ge(s_w, 7 * 16)
                nc.tensor.transpose(bank[2][:, 192:192 + 3 * HEADS], bias_nat[:], c.ident[0:3 * HEADS, 0:3 * HEADS])
                for k in range(KC):
                    last = nc.tensor.transpose(bank[2][:, 256 + k * EXPERTS0:256 + (k + 1) * EXPERTS0], r_nat[:, k * P:(k + 1) * P],
                                               c.ident[0:EXPERTS0, 0:EXPERTS0])
                last.then_inc(s_tr, 1)
                pe.wait_ge(s_lo, 8)
                for i in range(3):
                    for h in range(2):
                        n = 2 * i + h
                        b = bank[(7, 0, 1, 2, 3, 4)[n]]
                        cols = slice(h * HALF, (h + 1) * HALF)
                        mm_stacked(nc, b[:], wt[:, i].rearrange("k a n -> k (a n)"), ctxt_hi[:, cols], ctxt_lo[:, cols], False).then_inc(s_tr, 1)
                for h in range(2):
                    for t in range(4):
                        cols = slice((4 * h + t) * P, (4 * h + t + 1) * P)
                        last = mm_stacked(nc, bank[5 + h][:, t * P:(t + 1) * P], wt[:, 2].rearrange("k a n -> k (a n)"), ctxt_hi[:, cols], ctxt_lo[:, cols], True)
                    last.then_inc(s_tr, 1)
                pe.wait_ge(s_lo, 12)
                for b in range(B):
                    for h in range(2):
                        cols = slice(b * T + h * P, b * T + (h + 1) * P)
                        keys = slice(b * T, (b + 1) * T)
                        last = mm_stacked(nc, bank[(7, 0, 1, 2)[b]][:, h * T:(h + 1) * T], qt[:, cols], kt_hi[:, keys], kt_lo[:, keys], False)
                    last.then_inc(s_tr, 1)

            @block.scalar
            def _(act):
                hi = Count(s_hi)
                for n in range(4):
                    act.wait_ge(s_tr, 1 + n)
                    k, h = n % 2, n // 2
                    hi.inc(nc.scalar.activation(c.xt_hi[:, k, h * HALF:(h + 1) * HALF], bank[3 + 2 * k + h][:], ACT.Copy))
                for h in range(2):
                    act.wait_ge(s_tr, h + 5)
                    hi.inc(nc.scalar.activation(ctxt_hi[:, h * HALF:(h + 1) * HALF], bank[h][:], ACT.Copy))
                act.wait_ge(s_tr, 7)
                small = bank[2][:, 0:3 * DC].rearrange("k (i n) -> k i n", i=3)
                nc.scalar.activation(wt[:, :, 0], small, ACT.Copy)
                nc.scalar.activation(wt[:, :, 1], small, ACT.Copy)
                nc.scalar.activation(c.bias_t[:], bank[2][:, 192:192 + 3 * HEADS], ACT.Copy)
                hi.inc(nc.scalar.activation(c.rt[:, :, :, 0], again(bank[2][:, 256:256 + KC * EXPERTS0].rearrange("p (k e) -> p k e", k=KC), EXPERTS0), ACT.Copy))
                for i in range(3):
                    for h in range(2):
                        n = 2 * i + h
                        act.wait_ge(s_tr, 8 + n)
                        b = bank[(7, 0, 1, 2, 3, 4)[n]]
                        if i < 2:
                            hi.inc(nc.scalar.activation((qt, kt_hi)[i][:, h * HALF:(h + 1) * HALF], b[:], ACT.Copy))
                        else:
                            for j in range(2):
                                batch = slice((2 * h + j) * T, (2 * h + j + 1) * T)
                                last = nc.scalar.activation(c.kvt[:, batch], b[:, j * T:(j + 1) * T], ACT.Copy, accum_out=c.kvt_sum[:, 2 * h + j:2 * h + j + 1])
                            hi.inc(last)
                act.wait_ge(s_const, 16)
                nc.scalar.activation(c.ident_bf[:], c.ident[:], ACT.Copy)
                act.wait_ge(s_bias, 32)
                nc.scalar.activation(c.causal[:], causal_f[:].unsqueeze(1).broadcast_to([P, B, P]), ACT.Copy)
                g = nc.scalar.activation(g_exp[:], g_raw[:], ACT.Exp, scale=-1.0)
                hi.inc(g)
                for b in range(B):
                    act.wait_ge(s_tr, 16 + b)
                    src = bank[(7, 0, 1, 2)[b]][:].rearrange("p (h n) -> p h n", h=2)
                    nc.scalar.activation(c.sim[:, 2 * b:2 * b + 2], src, ACT.Copy, scale=1.0 / 16)

            @block.vector
            def _(dve):
                lo = Count(s_lo)
                nc.vector.memset(c.idle[:], 0.0).then_inc(s_idle, 1)
                nc.vector.memset(c.zero[:], 0.0)
                dve.wait_ge(s_const, 16)
                for n, pick in c.pick.items():
                    nc.vector.tensor_tensor(pick[:], c.ident[0:2 * n, 0:n], c.ident[0:2 * n, n:2 * n], ALU.add)
                for n in range(4):
                    dve.wait_ge(s_hi, 1 + n)
                    k, h = n % 2, n // 2
                    cols = slice(h * HALF, (h + 1) * HALF)
                    lo.inc(nc.vector.tensor_tensor(c.xt_lo[:, k, cols], bank[3 + 2 * k + h][:], f32(c.xt_hi[:, k, cols]), ALU.subtract))
                for h in range(2):
                    dve.wait_ge(s_hi, h + 5)
                    cols = slice(h * HALF, (h + 1) * HALF)
                    lo.inc(nc.vector.tensor_tensor(ctxt_lo[:, cols], bank[h][:], f32(ctxt_hi[:, cols]), ALU.subtract))
                dve.wait_ge(s_hi, 7)
                small = bank[2][LOW, 0:3 * DC].rearrange("k (i n) -> k i n", i=3)
                nc.vector.tensor_tensor(wt[LOW, :, 0], small, f32(wt[LOW, :, 0]), ALU.subtract)
                lo.inc(nc.vector.tensor_tensor(wt[LOW, :, 1], small, f32(wt[LOW, :, 1]), ALU.subtract))
                lo.inc(nc.vector.tensor_tensor(c.rt[:, :, :, 1], again(bank[2][:, 256:256 + KC * EXPERTS0].rearrange("p (k e) -> p k e", k=KC), EXPERTS0),
                                               f32(c.rt[:, :, :, 0]), ALU.subtract))
                for i in range(2):
                    for h in range(2):
                        n = 2 * i + h
                        dve.wait_ge(s_hi, 8 + n)
                        b = bank[(7, 0, 1, 2)[n]]
                        cols = slice(h * HALF, (h + 1) * HALF)
                        if i == 0:
                            lo.inc(nc.vector.tensor_tensor(qt[LOW, cols], b[LOW], f32(qt[LOW, cols]), ALU.subtract))
                        else:
                            lo.inc(nc.vector.tensor_tensor(kt_lo[:, cols], b[:], f32(kt_hi[:, cols]), ALU.subtract))
                dve.wait_ge(s_rows, 6 * 16)
                for h in range(2):
                    dve.wait_ge(s_tr, 14 + h)
                    lo.inc(nc.vector.tensor_tensor(c.kv[:, 4 * h:4 * h + 4], bank[5 + h][:].rearrange("p (t n) -> p t n", t=4),
                                                   c.rows[:, ROW_BK, 0:P].unsqueeze(1).broadcast_to([P, 4, P]), ALU.add))
                dve.wait_ge(s_hi, 14)
                n = lo.inc(nc.vector.tensor_scalar(g_den[:], g_exp[:], 1.0, None, ALU.add))
                dve.wait_ge(s_lo, n)
                n = lo.inc(nc.vector.reciprocal(c.gamma[:], g_den[:]))
                dve.wait_ge(s_lo, n)
                lo.inc(nc.vector.tensor_scalar(c.one_less[:], c.gamma[:], -1.0, 2.0, ALU.mult, ALU.add))
                nc.vector.tensor_scalar(c.quarter[:], c.gamma[:], 0.25, None, ALU.mult)

            @block.gpsimd
            def _(pool):
                nc.gpsimd.memset(c.half_neg[:], -0.5)
                nc.gpsimd.memset(c.one[:], 1.0)
                pool.wait_ge(s_ctx, 16)
                nc.gpsimd.tensor_copy(ctx_nat[:, :, 1], ctx_nat[:, :, 0]).then_inc(s_twice, 1)
                pool.wait_ge(s_w, 7 * 16)
                nc.gpsimd.tensor_copy(w_nat[:, :, 1], w_nat[:, :, 0]).then_inc(s_twice, 1)
                pool.drain()
                weights.first_splits(pool)


class AttentionWeights:

    def __init__(self, c, layer):
        self.c, self.layer, self.rope = c, layer, layer == 1
        names = [f"L0_attn_w_{n}" for n in "qkvo"] if not self.rope else [f"L1_attn_W{n}" for n in "qkvo"]
        self.dram = {n: c.a[name].rearrange("(k p) n -> p k n", p=P) for n, name in zip("qkv", names)}
        self.dram["o"] = c.a[names[3]].rearrange("(h d) n -> d h n", d=DH)
        self.KH = 1 if self.rope else GROUP
        self.width = {"q": GROUP * DH, "k": self.KH * DH, "v": GROUP * DH, "o": GROUP}

    def __enter__(self):
        self.memory = ExitStack()
        sb = lambda name, shape, dt=F32: self.memory.enter_context(self.c.nc.sbuf_tensor(f"a{self.layer}_{name}", shape, dt))
        S = lambda name: self.c.sem(f"a{self.layer}_{name}")
        shape = {n: [P, KC, self.width[n]] for n in "qkv"} | {"o": [DH, GROUP, D]}
        self.raw = {n: sb(f"raw_{n}", shape[n]) for n in "qkvo"}
        self.hi = {n: sb(f"w{n}_hi", shape[n], F32R) for n in "qkvo"}
        self.lo = {n: sb(f"w{n}_lo", shape[n], F32R) for n in "qkvo"}
        self.s_raw = {n: S(f"raw_{n}") for n in "qkvo"}
        self.s_split_proj, self.s_split_v, self.s_split_o = S("split_proj"), S("split_v"), S("split_o")
        self.own = Count(S("pool"))
        if self.rope:
            self.cos, self.sin, self.scale_row = sb("cos", [P, T]), sb("sin", [P, T]), sb("scale_row", [P, HEADS])
            self.s_table = S("table")
        return self

    def __exit__(self, *error):
        self.memory.close()

    def units(self, h):
        if self.rope and h % GROUP:
            return [("q", 0), ("q", 1)]
        return [("k", 0), ("k", 1), ("q", 0), ("q", 1)]

    def load(self, sp, n, g):
        width = self.width[n]
        part = self.dram[n][:, bass.ds(g * width, width)] if n == "o" else self.dram[n][:, :, bass.ds(g * width, width)]
        sp.dma_start(self.raw[n][:], part).then_inc(self.s_raw[n], 16)

    def first_loads(self, sp):
        for n in "kqvo":
            self.load(sp, n, 0)
        if self.rope:
            a = self.c.a
            sp.dma_start(self.cos[:], a["cos"]).then_inc(self.s_table, 16)
            sp.dma_start(self.sin[:], a["sin"]).then_inc(self.s_table, 16)
            sp.dma_start(self.scale_row[:], a["L1_attn_head_scale"].rearrange("a h b c -> (a h b c)").partition_broadcast(P)).then_inc(self.s_table, 16)

    def split(self, pool, parts, done):
        nc = self.c.nc
        for hi, lo, raw in parts:
            n = self.own.inc(nc.gpsimd.tensor_tensor(hi, raw, self.c.one[:].unsqueeze(1).broadcast_to(list(raw.shape)), ALU.mult))
        pool.wait_ge(self.own.sem, n)
        for hi, lo, raw in parts:
            last = nc.gpsimd.tensor_tensor(lo, raw, f32(hi), ALU.subtract)
        last.then_inc(done, 1)

    def split_proj(self, pool, g, h):
        parts = []
        for n, heads in (("k", self.KH), ("q", GROUP)):
            if (n, 0) in self.units(h):
                pool.wait_ge(self.s_raw[n], (g + h // GROUP) * 16 + 16)
                s = slice((h % heads) * DH, (h % heads + 1) * DH)
                parts.append((self.hi[n][:, :, s], self.lo[n][:, :, s], self.raw[n][:, :, s]))
        self.split(pool, parts, self.s_split_proj)

    def split_all(self, pool, n, g, done):
        pool.wait_ge(self.s_raw[n], g * 16 + 16)
        self.split(pool, [(self.hi[n][:], self.lo[n][:], self.raw[n][:])], done)

    def first_splits(self, pool):
        for h in range(GROUP, GROUP + 2):
            self.split_proj(pool, -1, h)

    def second_splits(self, pool):
        self.split_all(pool, "v", 0, self.s_split_v)
        self.split_proj(pool, -1, GROUP + 2)


def attention(c, layer, weights):
    nc, a = c.nc, c.a
    rope = layer == 1
    KH, units = weights.KH, weights.units
    s_raw, s_split_proj, s_split_v, s_split_o = weights.s_raw, weights.s_split_proj, weights.s_split_v, weights.s_split_o

    PROJ_TO = [sum(len(units(i)) for i in range(h)) for h in range(GROUP + 1)]
    PROJ = PROJ_TO[-1]
    VU = 2 if rope else NT
    OU = NT // 2
    RING = 3

    first, n = {}, 0
    for h in range(1, GROUP + 1):
        parts = [("proj", h + 1, len(units(h + 1))), ("pv", h - 1, 2)]
        for name, head, count in reversed(parts) if rope and h == GROUP else parts:
            first[name, head] = n
            n += count
    first["v"], first["o"] = (n + OU, n) if rope else (n, n + VU)
    U = n + VU + OU
    assert U % RING == 0
    BEFORE = U - first["proj", GROUP]

    def number(g, step, u):
        return g * U + (BEFORE + first[step] + u)

    def ring_bank(step, u):
        return c.banks[5 + (BEFORE + first[step] + u) % RING]

    def taken(g, step, u):
        return number(g, step, u) + (RING + 1)

    with ExitStack() as ctx:
        sb = lambda name, shape, dt=F32: ctx.enter_context(nc.sbuf_tensor(f"a{layer}_{name}", shape, dt))
        queries, keys, vals = sb("queries", [DH, NTOK]), sb("keys", [DH, NTOK]), sb("vals", [P, NT, KH * DH])
        probs = [sb(f"probs{i}", [P, 3, BANK]) for i in range(2)]
        probs_t = sb("probs_t", [P, 3 * BANK])
        attended = sb("attended", [DH, NTOK])
        ot_hi, ot_lo = sb("ot_hi", [DH, GROUP, NTOK], F32R), sb("ot_lo", [DH, GROUP, NTOK], F32R)
        peak, neg_peak = sb("peak", [P, NT]), sb("neg_peak", [P, NT])
        row_sum, row_inv = sb("row_sum", [P, 2, NT]), sb("row_inv", [P, 2, NT])
        if rope:
            cos, sin, scale_row, s_table = weights.cos, weights.sin, weights.scale_row, weights.s_table
            all_vals = sb("all_vals", [P, NT, GROUPS * DH])
            along, across = (c.sim[:, 4 * i:4 * i + 4].rearrange("p (u t) n -> p u (t n)", u=2) for i in range(2))
        else:
            doubled = [weights.raw[n][:].rearrange("p k n -> p (k n)") for n in "qk"]
            similar = [c.sim[:, 4 * half:4 * half + 4].rearrange("p t n -> p (t n)") for half in range(2)]
            work = [sb(f"work{i}", [P, T]) for i in range(2)]
            top8 = sb("top8", [P, 8])

        S = lambda name: c.sem(f"a{layer}_{name}")
        s_proj, s_v, s_pv, s_o = S("proj"), S("v"), S("pv"), S("o")
        s_taken = S("taken")
        s_attended = S("attended")
        s_ot_hi, s_ot_lo = S("ot_hi"), S("ot_lo")
        s_vals = S("vals")
        s_group_vals = S("group_vals")
        s_seen = S("seen")
        s_rope = S("rope")
        s_scores, s_peak, s_exp, s_norm = S("scores"), S("peak"), S("exp"), S("norm")
        s_pt, s_pt_free = S("pt"), S("pt_free")
        if not rope:
            s_tanh, s_kept, s_kept_t = S("tanh"), S("kept"), S("kept_t")
        s_residual = S("residual")
        s_dve = S("dve")

        def scores_bank(b, q):
            return (0, b * P, P) if q == 0 else (1 + b // 2, (b % 2) * T, T)

        def proj_index(g, h, u):
            return (g + h // GROUP) * PROJ + (PROJ_TO[h % GROUP] + u)

        with nc.Block() as block:
            @block.sync
            def _(sp):
                with sp.Fori(0, GROUPS - 1) as g:
                    if not rope:
                        sp.wait_ge(s_split_v, g + 1)
                        weights.load(sp, "v", g + 1)
                    sp.wait_ge(s_split_proj, g * GROUP + GROUP)
                    weights.load(sp, "q", g + 1)
                    weights.load(sp, "k", g + 1)
                    sp.wait_ge(s_split_o, g + 1)
                    weights.load(sp, "o", g + 1)

            @block.gpsimd
            def _(pool):
                pool.sem_inc(s_ot_lo, 2)

                def split_proj(g, h):
                    pool.wait_ge(s_proj, proj_index(g, h, len(units(h))))
                    weights.split_proj(pool, g, h)

                def split_v(g):
                    pool.wait_ge(s_v, g * VU + VU)
                    weights.split_all(pool, "v", g, s_split_v)

                def split_o(g):
                    pool.wait_ge(s_o, g * OU + OU)
                    weights.split_all(pool, "o", g, s_split_o)

                def rotate(g, h):
                    for u, (what, half) in enumerate(units(h) if rope else ()):
                        dst = (queries if what == "q" else keys)[:, half * HALF:(half + 1) * HALF]
                        pool.wait_ge(s_taken, taken(g, ("proj", h), u))
                        nc.gpsimd.tensor_tensor(dst, along[:, u % 2], across[:, u % 2], ALU.add).then_inc(s_rope, 1)

                def low(g, h):
                    for half in range(2):
                        pool.wait_ge(s_ot_hi, g * (2 * GROUP) + (2 * h + half + 1))
                        cols = slice(half * HALF, (half + 1) * HALF)
                        nc.gpsimd.tensor_tensor(ot_lo[:, h, cols], attended[:, cols], f32(ot_hi[:, h, cols]), ALU.subtract).then_inc(s_ot_lo, 1)

                def turn(g, more):
                    split_proj(g, 3)
                    rotate(g, 2)
                    if not more:
                        split_o(g)
                    low(g, 0)
                    if more:
                        split_proj(g, 4)
                    rotate(g, 3)
                    low(g, 1)
                    if more:
                        if not rope:
                            split_v(g + 1)
                        split_proj(g, 5)
                        rotate(g, 4)
                    low(g, 2)
                    if more:
                        split_o(g)
                    low(g, 3)
                    if more:
                        rotate(g, 5)
                        split_proj(g, 6)

                def split_keys():
                    batches = lambda ap: ap[:].rearrange("p (b t) -> p b t", b=B)
                    whole = c.one[:].broadcast_to([P, NTOK])
                    values = c.kv[:].rearrange("p t n -> p (t n)")
                    nc.gpsimd.tensor_tensor(c.kv_hi[:].rearrange("p t n -> p (t n)"), values, whole, ALU.mult)
                    nc.gpsimd.tensor_scalar(c.kvt_mean[:], c.kvt_sum[:], -1.0 / T, None, ALU.mult)
                    pool.drain()
                    nc.gpsimd.tensor_tensor(c.kv_lo[:], c.kv[:], f32(c.kv_hi[:]), ALU.subtract)
                    nc.gpsimd.tensor_tensor(batches(c.kvt), batches(c.kvt), c.kvt_mean[:].unsqueeze(2).broadcast_to([P, B, T]), ALU.add)
                    pool.drain()
                    weighted = values
                    nc.gpsimd.tensor_tensor(weighted.rearrange("p (b t) -> p b t", b=B), batches(c.kvt), c.rows[:, ROW_GAMMA].unsqueeze(1).broadcast_to([P, B, T]), ALU.mult)
                    nc.gpsimd.tensor_tensor(c.kvt_hi[:], c.kvt[:], whole, ALU.mult)
                    pool.drain()
                    nc.gpsimd.tensor_tensor(c.kvt_lo[:], c.kvt[:], f32(c.kvt_hi[:]), ALU.subtract)
                    nc.gpsimd.tensor_tensor(c.kvg_hi[:], weighted, whole, ALU.mult)
                    pool.drain()
                    nc.gpsimd.tensor_tensor(c.kvg_lo[:], weighted, f32(c.kvg_hi[:]), ALU.subtract)

                if not rope:
                    weights.second_splits(pool)
                rotate(-1, 4)
                rotate(-1, 5)
                if not rope:
                    nc.gpsimd.tensor_tensor(c.x[:], c.x[:], c.rows[:, ROW_BO].unsqueeze(1).broadcast_to([P, NT, D]), ALU.add).then_inc(s_residual, 1)
                    pool.wait_ge(c.s_ffn_weight, 16)
                    nc.gpsimd.tensor_scalar(c.clipped[:], c.ffn_weight[:], 2.0, 1.0, ALU.mult, ALU.min)
                    pool.drain()
                    nc.gpsimd.tensor_scalar(c.ffn_weight[:], c.clipped[:], -1.0, 12582912.0, ALU.max, ALU.add)
                    pool.drain()
                    nc.gpsimd.tensor_scalar(c.tern[:], c.ffn_weight[:], -12582912.0, None, ALU.add)
                    split_keys()
                with pool.Fori(0, GROUPS - 1) as g:
                    weights.own.enter(g, GROUP + KH + (1 if rope else 2))
                    turn(g, True)
                weights.own.leave(GROUPS - 1)
                turn(GROUPS - 1, False)

            @block.tensor
            def _(pe):
                pe.sem_inc(s_proj, PROJ)
                if not rope:
                    pe.sem_inc(s_v, VU)
                pe.sem_inc(s_o, OU)

                def claim(g, step, u):
                    pe.wait_ge(s_taken, number(g, step, u) + 1)
                    return ring_bank(step, u)

                def proj(g, h, part):
                    if not part:
                        return
                    pe.wait_ge(s_split_proj, g * GROUP + (h + 1))
                    for u in part:
                        what, half = units(h)[u]
                        bank = claim(g, ("proj", h), u)
                        hi, lo = weights.hi[what], weights.lo[what]
                        s = (h % (GROUP if what == "q" else KH)) * DH
                        cols = slice(half * HALF, (half + 1) * HALF)
                        for k in range(KC):
                            last = mm3(nc, bank[:], hi[:, k, s:s + DH], lo[:, k, s:s + DH], c.xt_hi[:, k, cols], c.xt_lo[:, k, cols], k == 0, k == KC - 1)
                        last.then_inc(s_proj, 1)

                def values_tile(t, bank):
                    cols = slice(t * P, (t + 1) * P)
                    for k in range(KC):
                        last = mm3(nc, bank[:], c.xt_hi[:, k, cols], c.xt_lo[:, k, cols], weights.hi["v"][:, k], weights.lo["v"][:, k], k == 0, k == KC - 1)
                    last.then_inc(s_v, 1)

                def values(g):
                    pe.wait_ge(s_split_v, g + 2)
                    for t in range(NT):
                        values_tile(t, claim(g, "v", t))

                def all_values(tiles):
                    pe.wait_ge(s_split_v, 1)
                    for t in tiles:
                        if t >= 2:
                            pe.wait_ge(s_vals, t - 1)
                        values_tile(t, c.banks[3 + t % 2])

                def scores(g, h):
                    if rope:
                        pe.wait_ge(s_rope, proj_index(g, h, len(units(h))))
                    elif h > 1:
                        pe.wait_ge(s_taken, taken(g, ("proj", h), len(units(h)) - 1))
                    else:
                        pe.wait_ge(s_taken, taken(g, ("proj", GROUP + 1), len(units(h)) - 1) - U)
                    pe.wait_ge(s_exp, g * (GROUP * NT) + (h + 1) * NT)
                    nc.tensor.matmul(c.banks[0][:], c.ident_bf[:], c.causal[:].rearrange("p b k -> p (b k)"), start=True, stop=False)
                    for b in range(B):
                        i, at, width = scores_bank(b, 0)
                        last = nc.tensor.matmul(c.banks[i][:, at:at + width], queries[:, b * T:b * T + P], keys[:, b * T:b * T + width], start=False, stop=b == B - 1)
                    last.then_inc(s_scores, 1)
                    for b in range(B):
                        i, at, width = scores_bank(b, 1)
                        out = c.banks[i][:, at:at + width]
                        nc.tensor.matmul(out, queries[:, b * T + P:(b + 1) * T], keys[:, b * T:b * T + width], start=True, stop=False)
                        last = nc.tensor.matmul(out[:, width - P:], c.ident_bf[:], c.causal[:, 0], start=False, stop=True)
                        if at + width == BANK:
                            last.then_inc(s_scores, 1)

                def transposes(g, h, banks):
                    for slot in range(4 * banks.start, 4 * banks.stop):
                        b, j = slot // 3, slot % 3
                        bank = 3 + (3 * h + slot // 4) % 2
                        if slot % 4 == 0:
                            pe.wait_ge(s_pt_free, g * (3 * GROUP) + (3 * h + slot // 4 + 1))
                        if slot % 6 == 0:
                            pe.wait_ge(s_norm, g * (GROUP * 3) + (h * 3 + b // 2 + 2))
                        i, at, width = scores_bank(b, min(j, 1))
                        at += P if j == 2 else 0
                        last = nc.tensor.transpose(c.banks[bank][:, slot % 4 * P:(slot % 4 + 1) * P], probs[h % 2][:, i, at:at + P], c.ident[:])
                        if slot % 4 == 3:
                            last.then_inc(s_pt, 1)

                def pv(g, h):
                    if h == 0:
                        if rope:
                            pe.wait_ge(s_group_vals, g + 1)
                        else:
                            pe.wait_ge(s_taken, taken(g, "v", VU - 1) - U)
                    for half in range(2):
                        bank = claim(g, ("pv", h), half)
                        for i in range(2):
                            b = 2 * half + i
                            pe.wait_ge(s_pt_free, g * (3 * GROUP) + (3 * h + (3 * b + 2) // 4 + 1 + 2))
                            at = 3 * b * P
                            s = slice((h % KH) * DH, (h % KH + 1) * DH)
                            out = bank[:, i * T:(i + 1) * T]
                            nc.tensor.matmul(out, vals[:, 2 * b, s], probs_t[:, at:at + T], start=True, stop=False)
                            last = nc.tensor.matmul(out[:, P:], vals[:, 2 * b + 1, s], probs_t[:, at + T:at + T + P], start=False, stop=True)
                        last.then_inc(s_pv, 1)

                def output(g):
                    pe.wait_ge(s_split_o, g + 1)
                    for u in range(OU):
                        if u % (OU // 2) == 0:
                            pe.wait_ge(s_ot_lo, g * (2 * GROUP) + (2 * GROUP + 1 + u // (OU // 2)))
                        bank = claim(g, "o", u)
                        for i in range(2):
                            cols = slice((2 * u + i) * P, (2 * u + i + 1) * P)
                            for h in range(GROUP):
                                last = mm3(nc, bank[:, i * D:(i + 1) * D], ot_hi[:, h, cols], ot_lo[:, h, cols], weights.hi["o"][:, h], weights.lo["o"][:, h],
                                           h == 0, h == GROUP - 1)
                        last.then_inc(s_o, 1)

                def last_output(g, units, heads):
                    pe.wait_ge(s_split_o, g + 1)
                    pe.wait_ge(s_exp, (g + 1) * (GROUP * NT) + NT)
                    if 3 in units:
                        pe.wait_ge(s_pt_free, (g + 1) * (GROUP * 3) + 2)
                    for u in units:
                        if u == units.start or u == OU // 2:
                            pe.wait_ge(s_ot_lo, g * (2 * GROUP) + (2 * heads.stop + 1 + u // (OU // 2)))
                        if 0 in heads:
                            nc.tensor.matmul(c.banks[u][:], c.ident_bf[:], c.zero[:].broadcast_to([P, BANK]), start=True, stop=False)
                        for i in range(2):
                            cols = slice((2 * u + i) * P, (2 * u + i + 1) * P)
                            for h in heads:
                                last = mm3(nc, c.banks[u][:, i * D:(i + 1) * D], ot_hi[:, h, cols], ot_lo[:, h, cols], weights.hi["o"][:, h], weights.lo["o"][:, h],
                                           False, i == 1 and h == GROUP - 1)
                        if GROUP - 1 in heads:
                            last.then_inc(s_o, 1)

                def kept_transposes(g):
                    pe.wait_ge(s_kept, 1)
                    pe.wait_ge(s_taken, taken(g, ("pv", GROUP - 1), 1))
                    for b in range(B):
                        for i in range(2):
                            for j in range(2):
                                last = nc.tensor.transpose(c.banks[4 + b][:, i * T + j * P:i * T + (j + 1) * P], c.sim[:, 2 * b + j, i * P:(i + 1) * P], c.ident[:])
                        last.then_inc(s_kept_t, 1)

                def turn(g, more):
                    for h in range(1, GROUP + 1):
                        if more or h < GROUP:
                            scores(g, h)
                        count = len(units(h + 1)) if more or h + 1 < GROUP else 0
                        early = 0 if rope or not count else count - 1
                        late = rope and h == GROUP
                        if not late:
                            proj(g, h + 1, range(0, early))
                        if not more and h == GROUP:
                            last_output(g, range(0, 3), range(0, 2))
                        if early:
                            transposes(g, h - 1, range(0, 2))
                        if not late:
                            proj(g, h + 1, range(early, count))
                        transposes(g, h - 1, range(2 if early else 0, 3))
                        pv(g, h - 1)
                        if late:
                            proj(g, h + 1, range(count))
                    if more:
                        if not rope:
                            values(g)
                        output(g)
                    else:
                        last_output(g, range(0, 3), range(2, 3))
                        if not rope:
                            kept_transposes(g)
                        last_output(g, range(3, 4), range(0, 3))
                        last_output(g, range(0, 4), range(3, 4))

                proj(-1, GROUP, range(len(units(GROUP))))
                if rope:
                    all_values(range(0, NT // 2))
                scores(-1, GROUP)
                proj(-1, GROUP + 1, range(len(units(GROUP + 1))))
                if rope:
                    all_values(range(NT // 2, NT))
                    pe.wait_ge(s_vals, NT)
                else:
                    values(-1)
                with pe.Fori(0, GROUPS - 1) as g:
                    turn(g, True)
                turn(GROUPS - 1, False)

            @block.scalar
            def _(act):
                act.sem_inc(s_exp, NT)
                act.sem_inc(s_pt_free, 2)

                def exps(g, h):
                    for q in range(2):
                        for b in range(B):
                            i, at, width = scores_bank(b, q)
                            if at == 0:
                                act.wait_ge(s_peak, g * (3 * GROUP) + (3 * h + i + 1))
                            n = q * B + b
                            nc.scalar.activation(probs[h % 2][:, i, at:at + width], c.banks[i][:, at:at + width], ACT.Exp, bias=neg_peak[:, n:n + 1],
                                                 scale=SCALE, accum_out=row_sum[:, h % 2, n:n + 1]).then_inc(s_exp, 1)

                def pt(g, h):
                    for i in range(3):
                        act.wait_ge(s_pt, g * (3 * GROUP) + (3 * h + i + 1))
                        nc.scalar.activation(probs_t[:, i * BANK:(i + 1) * BANK], c.banks[3 + (3 * h + i) % 2][:], ACT.Copy).then_inc(s_pt_free, 1)

                def pv(g, h):
                    for half in range(2):
                        n = g * (2 * GROUP) + (2 * h + half)
                        act.wait_ge(s_pv, n + 1)
                        act.wait_ge(s_ot_lo, n + 1)
                        act.sem_inc(s_seen, 1)
                        dst, src = attended[:, half * HALF:(half + 1) * HALF], ring_bank(("pv", h), half)[:]
                        if rope:
                            last = nc.scalar.activation(dst, src, ACT.Copy, scale=scale_row[:, bass.ds(g * GROUP + h, 1)])
                        else:
                            last = nc.scalar.activation(dst, src, ACT.Identity, bias=c.bias_t[:, bass.ds(g * GROUP + (h + 2 * HEADS), 1)])
                        last.then_inc(s_attended, 1)
                        act.wait_ge(s_attended, g * (2 * GROUP) + (2 * h + half + 1))
                        cols = slice(half * HALF, (half + 1) * HALF)
                        nc.scalar.activation(ot_hi[:, h, cols], attended[:, cols], ACT.Copy).then_inc(s_ot_hi, 1)

                def tanhs():
                    act.wait_ge(s_split_proj, GROUPS * GROUP)
                    for half in range(2):
                        nc.scalar.activation(doubled[half], similar[half], ACT.Tanh, scale=0.5).then_inc(s_tanh, 1)

                def turn(g, more):
                    for h in range(1, GROUP + 1):
                        late = rope and h == GROUP
                        if not late and (more or h < GROUP - 1):
                            exps(g, h)
                        pt(g, h - 1)
                        if not more and h == GROUP - 1:
                            exps(g, h)
                        pv(g, h - 1)
                        if late and more:
                            exps(g, h)
                        if more and rope and h == GROUP:
                            group_values(g)
                        if not more and not rope and h == 1:
                            tanhs()

                if rope:
                    act.wait_ge(s_table, 48)
                def first_values(tiles):
                    for t in tiles:
                        act.wait_ge(s_v, t + 1 if rope else NT + t + 1)
                        dst, src = (all_vals, c.banks[3 + t % 2]) if rope else (vals, ring_bank("v", t))
                        nc.scalar.activation(dst[:, t], src[:], ACT.Copy).then_inc(s_vals, 1)

                def group_values(g):
                    nc.scalar.activation(vals[:], all_vals[:, :, bass.ds((g + 1) * DH, DH)], ACT.Copy).then_inc(s_group_vals, 1)

                early = NT // 2 if rope else 0
                first_values(range(0, early))
                exps(-1, GROUP)
                first_values(range(early, NT))
                if rope:
                    act.wait_ge(s_vals, NT)
                    group_values(-1)
                with act.Fori(0, GROUPS - 1) as g:
                    turn(g, True)
                turn(GROUPS - 1, False)

            @block.vector
            def _(dve):
                own = Count(s_dve)
                dve.sem_inc(s_taken, RING)

                def proj(g, h, u):
                    n = proj_index(g, h, u)
                    what, half = units(h)[u]
                    cols = slice(half * HALF, (half + 1) * HALF)
                    bank = ring_bank(("proj", h), u)
                    dve.wait_ge(s_proj, n + (PROJ + 1))
                    if rope:
                        two = lambda ap: ap.rearrange("p (b t) -> p b t", b=2)
                        many = lambda ap, size: ap.unsqueeze(1).broadcast_to([size, 2, T])
                        if not (isinstance(n, int) and n < 2):
                            dve.wait_ge(s_rope, n - 1)
                        nc.vector.tensor_tensor(two(along[:, u % 2]), two(bank[:]), many(cos[:], P), ALU.mult)
                        for to, at in ((0, HALF_BLOCK), (HALF_BLOCK, 0)):
                            last = nc.vector.tensor_tensor(two(across[to:to + HALF_BLOCK, u % 2]), two(bank[at:at + HALF_BLOCK]),
                                                           many(sin[at:at + HALF_BLOCK], HALF_BLOCK), ALU.mult)
                        last.then_inc(s_taken, 1)
                    else:
                        head = g * GROUP + (h + (0 if what == "q" else HEADS))
                        nc.vector.tensor_scalar((queries if what == "q" else keys)[:, cols], bank[:], c.bias_t[:, bass.ds(head, 1)], None,
                                                ALU.add).then_inc(s_taken, 1)

                def values(g, u):
                    dve.wait_ge(s_v, g * VU + (2 * VU + u + 1))
                    nc.vector.tensor_copy(vals[:, u], ring_bank("v", u)[:]).then_inc(s_taken, 1)

                def rows_of(i):
                    return (0, B) if i == 0 else (B + 2 * (i - 1), 2)

                def peaks(g, h):
                    for i in range(3):
                        dve.wait_ge(s_scores, g * (3 * GROUP) + (3 * h + i + 1))
                        n, rows = rows_of(i)
                        done = own.inc(nc.vector.tensor_reduce(peak[:, n:n + rows], c.banks[i][:].rearrange("p (r k) -> p r k", r=rows), AX.X, ALU.max))
                        dve.wait_ge(s_dve, done)
                        nc.vector.tensor_scalar(neg_peak[:, n:n + rows], peak[:, n:n + rows], -SCALE, None, ALU.mult).then_inc(s_peak, 1)

                def norm(g, h, i):
                    n, rows = rows_of(i)
                    dve.wait_ge(s_exp, g * (GROUP * NT) + ((h + 1) * NT + n + rows))
                    done = own.inc(nc.vector.reciprocal(row_inv[:, h % 2, n:n + rows], row_sum[:, h % 2, n:n + rows]))
                    dve.wait_ge(s_dve, done)
                    width = BANK // rows
                    for r in range(rows):
                        part = probs[h % 2][:, i, r * width:(r + 1) * width]
                        last = nc.vector.tensor_scalar(part, part, row_inv[:, h % 2, n + r:n + r + 1], None, ALU.mult)
                    last.then_inc(s_norm, 1)

                def pv(g, h):
                    dve.wait_ge(s_taken, number(g, ("pv", h), 0) + RING)
                    for half in range(2):
                        dve.wait_ge(s_attended, g * (2 * GROUP) + (2 * h + half + 1))
                        dve.sem_inc(s_taken, 1)

                def output(g, u, bank):
                    dve.wait_ge(s_o, g * OU + (OU + u + 1))
                    rows = c.x[:, 2 * u:2 * u + 2].rearrange("p t n -> p (t n)")
                    nc.vector.tensor_tensor(rows, rows, bank[:], ALU.add).then_inc(s_taken, 1)

                def skip(g, step, count):
                    dve.wait_ge(s_taken, number(g, step, 0) + RING)
                    dve.sem_inc(s_taken, count)

                ROUNDS = -(-KEEP // 8)

                def threshold(tile, begin, end):
                    if rope:
                        return
                    if begin == 0:
                        nc.vector.tensor_copy(work[0][:], c.sim[:, bass.ds(tile, 1)].rearrange("p t n -> p (t n)"))
                    for op in range(begin, end):
                        r = op // 2
                        dve.drain()
                        if op % 2 == 0:
                            nc.vector.max(top8[:], work[r % 2][:])
                        elif r < ROUNDS - 1:
                            nc.vector.match_replace(work[1 - r % 2][:], top8[:], work[r % 2][:], -3e38)
                        else:
                            nc.vector.tensor_copy(c.thr[:, bass.ds(tile, 1)], top8[:, (KEEP - 1) % 8:(KEEP - 1) % 8 + 1])

                PART = 2 * ROUNDS // GROUP

                def keep(tiles):
                    if len(tiles) > 1:
                        for half in range(2):
                            dve.wait_ge(s_tanh, half + 1)
                            nc.vector.tensor_scalar(doubled[half], doubled[half], 1.0, c.quarter[:], ALU.add, ALU.mult)
                    dve.drain()
                    for t in tiles:
                        last = nc.vector.scalar_tensor_tensor(c.sim[:, t], c.sim[:, t], c.thr[:, t:t + 1], doubled[t // 4][:, t % 4 * T:(t % 4 + 1) * T],
                                                              ALU.is_ge, ALU.mult)
                    if len(tiles) == 1:
                        last.then_inc(s_kept, 1)

                def symmetric():
                    for b in range(B):
                        dve.wait_ge(s_kept_t, b + 1)
                        rows = c.sim[:, 2 * b:2 * b + 2].rearrange("p t n -> p (t n)")
                        nc.vector.tensor_tensor(rows, rows, c.banks[4 + b][:], ALU.add)

                def turn(g, more):
                    for h in range(1, GROUP + 1):
                        count = len(units(h + 1))
                        search = (h - 1) * PART
                        late = rope and h == GROUP
                        left_out = not more and h + 1 >= GROUP
                        if left_out and not late:
                            skip(g, ("proj", h + 1), count)
                        if more or h < GROUP:
                            peaks(g, h)
                        if late:
                            pass
                        elif not left_out:
                            for u in range(count):
                                proj(g, h + 1, u)
                                if u < 2:
                                    threshold(g * 2, search + 2 * u, search + 2 * u + 2)
                            threshold(g * 2, search + 4, search + PART)
                        else:
                            threshold(g * 2, search, search + PART)
                        if not late and (more or h < GROUP):
                            for i in range(3):
                                norm(g, h, i)
                        elif not rope:
                            keep([2 * g])
                        pv(g, h - 1)
                        if late and more:
                            for u in range(count):
                                proj(g, h + 1, u)
                            for i in range(3):
                                norm(g, h, i)
                        elif late:
                            skip(g, ("proj", h + 1), count)
                        if not more and not rope and h == GROUP - 1:
                            keep([t for t in range(NT) if t != 2 * g])
                    if not more and not rope:
                        symmetric()
                    if more and not rope:
                        for u in range(VU):
                            values(g, u)
                            threshold(g * 2 + 1, u, u + 1)
                    for u in range(OU):
                        output(g, u, ring_bank("o", u) if more else c.banks[u])
                        if more:
                            threshold(g * 2 + 1, VU + u * 3, VU + u * 3 + 3)
                    if more and rope:
                        skip(g, "v", VU)

                if rope:
                    dve.wait_ge(s_table, 48)
                for u in range(len(units(GROUP))):
                    proj(-1, GROUP, u)
                peaks(-1, GROUP)
                skip(-1, ("pv", GROUP - 2), 2)
                if rope:
                    skip(-1, ("pv", GROUP - 1), 2)
                for u in range(len(units(GROUP + 1))):
                    proj(-1, GROUP + 1, u)
                    threshold(NT - 1, u, u + 1)
                if not rope:
                    skip(-1, ("pv", GROUP - 1), 2)
                search, rest = GROUP, 2 * ROUNDS - GROUP
                if rope:
                    skip(-1, "o", OU)
                dve.wait_ge(s_taken, number(-1, "v", 0) + RING)
                for u in range(VU):
                    if not rope:
                        dve.wait_ge(s_vals, u + 1)
                    dve.sem_inc(s_taken, 1)
                    threshold(NT - 1, search + rest * u // VU, search + rest * (u + 1) // VU)
                if not rope:
                    skip(-1, "o", OU)
                for i in range(3):
                    norm(-1, GROUP, i)
                if not rope:
                    dve.wait_ge(s_residual, 1)
                per_turn = GROUP * 6
                with dve.Fori(0, GROUPS - 1) as g:
                    own.enter(g, per_turn)
                    turn(g, True)
                own.leave(GROUPS - 1)
                turn(GROUPS - 1, False)


class Norm:

    def __init__(self, c, name, sb, summed=False):
        self.c, self.nc, self.summed = c, c.nc, summed
        if summed:
            self.sums, self.neg_mean = sb(f"{name}_sums", [P, NT]), sb(f"{name}_neg_mean", [P, NT])
            self.s_sum, self.s_mean = c.sem(f"{name}_sum"), c.sem(f"{name}_mean")
        self.stats, self.mv = sb(f"{name}_stats", [P, NT, 6]), sb(f"{name}_mv", [P, NT, 2])
        self.shifted, self.rstd = sb(f"{name}_shifted", [P, NT]), sb(f"{name}_rstd", [P, NT])
        self.s_var, self.s_rstd = c.sem(f"{name}_var"), c.sem(f"{name}_rstd")

    def moments(self, dve, tiles, half):
        for t in HALF_TILES[half]:
            self.nc.vector.bn_stats(self.stats[:, t], tiles(t))
        dve.drain()
        for t in HALF_TILES[half]:
            last = self.nc.vector.bn_aggr(self.mv[:, t], self.stats[:, t])
        last.then_inc(self.s_var, 1)

    def means(self, pool):
        for half in range(2):
            part = slice(HALF_TILES[half].start, HALF_TILES[half].stop)
            pool.wait_ge(self.s_sum, half + 1)
            self.nc.gpsimd.tensor_scalar(self.neg_mean[:, part], self.sums[:, part], -1.0 / D, None, ALU.mult).then_inc(self.s_mean, 1)

    def squares(self, act, scratch):
        for half in range(2):
            act.wait_ge(self.s_mean, half + 1)
            for t in HALF_TILES[half]:
                last = self.nc.scalar.activation(scratch[:, t], self.c.x[:, t], ACT.Square, bias=self.neg_mean[:, t:t + 1], accum_out=self.mv[:, t, 1:2])
            last.then_inc(self.s_var, 1)

    def root(self, pool, half, eps=EPS, factor=None, squares=None):
        part = slice(HALF_TILES[half].start, HALF_TILES[half].stop)
        pool.wait_ge(self.s_var, half + 1)
        if squares is None:
            self.nc.gpsimd.tensor_scalar(self.shifted[:, part], self.mv[:, part, 1], eps, None, ALU.add)
        else:
            self.nc.gpsimd.tensor_scalar(self.shifted[:, part], self.mv[:, part, 1], 1.0 / squares, eps, ALU.mult, ALU.add)
        pool.drain()
        last = self.nc.gpsimd.tensor_tensor(self.rstd[:, part], self.shifted[:, part], self.c.half_neg[:, part], ALU.pow)
        if factor is not None:
            pool.drain()
            last = self.nc.gpsimd.tensor_scalar(self.rstd[:, part], self.rstd[:, part], factor[:], None, ALU.mult)
        last.then_inc(self.s_rstd, 1)

    def roots(self, pool, factor=None):
        for half in range(2):
            self.root(pool, half, factor=factor, squares=D if self.summed else None)

    def wait(self, dve, half):
        dve.wait_ge(self.s_rstd, half + 1)

    def apply(self, dve, half, s_done):
        self.wait(dve, half)
        for t in HALF_TILES[half]:
            x = self.c.x[:, t]
            mean, op = (self.neg_mean[:, t:t + 1], ALU.add) if self.summed else (self.mv[:, t, 0:1], ALU.subtract)
            self.nc.vector.tensor_scalar(x, x, mean, self.rstd[:, t:t + 1], op, ALU.mult).then_inc(s_done, 1)


class Transposed:

    def __init__(self, c, name):
        self.c, self.nc = c, c.nc
        self.s_tr, self.s_hi, self.s_lo = (c.sem(f"{name}_{n}") for n in ("tr", "hi", "lo"))
        self.order = [(h, k) for h in range(2) for k in range(KC)]

    def pe(self, pe, s_ready, per_half):
        for n, (h, k) in enumerate(self.order):
            pe.wait_ge(s_ready, per_half * (h + 1))
            for t in range(4):
                last = self.nc.tensor.transpose(self.c.banks[4 + n][:, t * P:(t + 1) * P], self.c.x[:, 4 * h + t, k * P:(k + 1) * P], self.c.ident[:])
            last.then_inc(self.s_tr, 1)

    def act(self, act):
        for n, (h, k) in enumerate(self.order):
            act.wait_ge(self.s_tr, n + 1)
            self.nc.scalar.activation(self.c.xt_hi[:, k, h * HALF:(h + 1) * HALF], self.c.banks[4 + n][:], ACT.Copy).then_inc(self.s_hi, 1)

    def dve(self, dve):
        for n, (h, k) in enumerate(self.order):
            dve.wait_ge(self.s_hi, n + 1)
            cols = slice(h * HALF, (h + 1) * HALF)
            self.nc.vector.tensor_tensor(self.c.xt_lo[:, k, cols], self.c.banks[4 + n][:], f32(self.c.xt_hi[:, k, cols]), ALU.subtract).then_inc(self.s_lo, 1)

    def wait(self, pe, half=1):
        pe.wait_ge(self.s_lo, KC * (half + 1))


def again(ap, experts):
    return ap.unsqueeze(2).broadcast_to([P, KC, P // (2 * experts), experts])


class Router:

    def __init__(self, c, name, sb, w, experts, raw_banks, out):
        self.c, self.nc, self.w, self.experts, self.raw_banks, self.out = c, c.nc, w, experts, raw_banks, out
        self.flat = sb(f"{name}_flat", [2 * experts, NTOK])
        self.s_raw, self.s_flat, self.s_logits = (c.sem(f"{name}_{n}") for n in ("raw", "flat", "logits"))

    def pe(self, pe, turned):
        for half, bank in enumerate(self.raw_banks):
            turned.wait(pe, half)
            cols = slice(half * HALF, (half + 1) * HALF)
            for k in range(KC):
                w = self.w[:, k].rearrange("p r h e -> p (r h e)")
                self.nc.tensor.matmul(bank[:], w, self.c.xt_hi[:, k, cols], start=k == 0, stop=False)
                last = self.nc.tensor.matmul(bank[:], w, self.c.xt_lo[:, k, cols], start=False, stop=k == KC - 1)
            last.then_inc(self.s_raw, 1)
        for t in range(NT):
            if t % (NT // 2) == 0:
                pe.wait_ge(self.s_flat, t // (NT // 2) + 1)
            last = self.nc.tensor.matmul(self.out[:, t * self.experts:(t + 1) * self.experts], self.flat[:, t * P:(t + 1) * P],
                                         self.c.pick[self.experts][:], start=True, stop=True)
        last.then_inc(self.s_logits, 1)

    def act(self, act):
        for half, bank in enumerate(self.raw_banks):
            act.wait_ge(self.s_raw, half + 1)
            self.nc.scalar.activation(self.flat[:, half * HALF:(half + 1) * HALF], bank[0:2 * self.experts], ACT.Copy).then_inc(self.s_flat, 1)


def graph_and_masked_experts(c, weights):
    nc, a = c.nc, c.a
    PAIRS = EXPERTS0 // 2
    RING = 4
    with ExitStack() as ctx:
        sb = lambda name, shape, dt=F32: ctx.enter_context(nc.sbuf_tensor(f"b_{name}", shape, dt))
        norm1, norm2, norm3 = (Norm(c, f"b_norm{i}", sb, summed=i == 3) for i in (1, 2, 3))
        turned2, turned3 = Transposed(c, "b_turned2"), Transposed(c, "b_turned3")
        router = Router(c, "b_router", sb, c.rt, EXPERTS0, c.banks[0:2], c.banks[2])
        top, above, likely = sb("top", [P, NT]), sb("above", [P, NT, EXPERTS0]), sb("likely", [P, NT, EXPERTS0])
        total, weight = sb("total", [P, NT]), sb("weight", [P, NT])
        numbers, found, first = sb("numbers", [P, NT, EXPERTS0]), sb("found", [P, NT, EXPERTS0]), sb("first", [P, NT])
        chosen, gate = sb("chosen", [P, NT, EXPERTS0]), sb("gate", [P, NT, EXPERTS0])
        raw = [sb(f"raw{i}", [P, 2, KC, D]) for i in range(2)]
        masked = [sb(f"masked{i}", [P, 2, KC, D], BF16) for i in range(2)]
        w = [sb(f"w{i}", [P, KC, 2 * D], F32R) for i in range(2)]
        acc = [sb(f"acc{i}", [P, NT, D]) for i in range(2)]

        S = lambda name: c.sem(f"b_{name}")
        s_numbers, s_raw = S("numbers"), [S(f"raw{i}") for i in range(2)]
        s_norm2, s_norm3, s_sum = S("norm2"), S("norm3"), S("sum")
        s_above, s_likely, s_acc0 = S("above"), S("likely"), S("acc0")
        s_masked, s_turned, s_w = S("masked"), S("turned"), S("w")
        s_out, s_used = S("out"), S("used")

        def summed(engine, queue, half):
            part = slice(HALF_TILES[half].start, HALF_TILES[half].stop)
            engine.tensor_tensor(acc[0][:, part], acc[0][:, part], acc[1][:, part], ALU.add)
            queue.drain()
            wide = c.rows[:, ROW_SCALE].unsqueeze(1).broadcast_to([P, NT // 2, D])
            return engine.tensor_tensor(acc[0][:, part], acc[0][:, part], wide, ALU.mult)

        with nc.Block() as block:
            @block.sync
            def _(sp):
                sp.dma_start(numbers[:], a["numbers"]).then_inc(s_numbers, 16)
                weights.first_loads(sp)

                def load(i, j):
                    pair = i * 2 + j
                    sp.wait_ge(s_masked, pair + 1)
                    for e in range(2):
                        sp.dma_start(raw[j][:, e], a["L0_ffn_expert_masks"][bass.ds(pair * 2 + e, 1)].rearrange("n (k p) i -> p (n k) i", p=P)).then_inc(s_raw[j], 16)

                with sp.Fori(0, PAIRS // 2) as i:
                    load(i, 0)
                    load(i, 1)

            @block.gpsimd
            def _(pool):
                pool.sem_inc(s_masked, 2)
                norm1.roots(pool, c.one_less)
                for x in acc:
                    last = nc.gpsimd.memset(x[:], 0.0)
                last.then_inc(s_acc0, 1)
                norm2.roots(pool)

                def mask(i, j):
                    pair = i * 2 + j
                    pool.wait_ge(s_raw[j], i * 32 + 32)
                    pool.wait_ge(s_turned, pair + 1)
                    wide = c.tern[:].unsqueeze(1).broadcast_to([P, 2, KC, D])
                    nc.gpsimd.tensor_tensor(masked[j][:], raw[j][:], wide, ALU.mult).then_inc(s_masked, 1)

                with pool.Fori(0, PAIRS // 2) as i:
                    mask(i, 0)
                    mask(i, 1)
                weights.first_splits(pool)
                weights.second_splits(pool)
                pool.wait_ge(s_used, RING + (PAIRS - 1) * NT + NT // 2)
                summed(nc.gpsimd, pool, 0).then_inc(s_sum, 1)
                norm3.means(pool)
                norm3.roots(pool)

            @block.tensor
            def _(pe):
                pe.sem_inc(s_turned, 2)
                pe.sem_inc(s_out, 2 * NT)
                norm1.wait(pe, 1)
                keep_warm(c, 16)
                turned2.pe(pe, s_norm2, 4)
                router.pe(pe, turned2)

                def turn(i, j):
                    pair = i * 2 + j
                    pe.wait_ge(s_masked, pair + 3)
                    pe.wait_ge(s_w, pair + 1)
                    bank = c.banks[6 + j][:].bitcast(BF16)
                    for k in range(KC):
                        for e in range(2):
                            for o in range(KC):
                                at = k * 2 * D + e * D + o * P
                                last = nc.tensor.transpose(bank[:, at:at + P], masked[j][:, e, o, k * P:(k + 1) * P], c.ident_bf[:])
                    last.then_inc(s_turned, 1)

                def products(i, j):
                    pair = i * 2 + j
                    pe.wait_ge(s_w, pair + 3)
                    for t in range(NT):
                        pe.wait_ge(s_used, i * (2 * NT) + (j * NT + t + 1))
                        out = c.banks[t % RING][:]
                        cols = slice(t * P, (t + 1) * P)
                        for k in range(KC):
                            nc.tensor.matmul(out, c.xt_hi[:, k, cols], w[j][:, k], start=k == 0, stop=False)
                            last = nc.tensor.matmul(out, c.xt_lo[:, k, cols], w[j][:, k], start=False, stop=k == KC - 1)
                        last.then_inc(s_out, 1)

                turn(0, 0)
                pe.wait_ge(s_above, 1)
                with pe.Fori(0, PAIRS // 2 - 1) as i:
                    turn(i, 1)
                    products(i, 0)
                    turn(i + 1, 0)
                    products(i, 1)
                turn(PAIRS // 2 - 1, 1)
                products(PAIRS // 2 - 1, 0)
                products(PAIRS // 2 - 1, 1)
                pe.wait_ge(norm3.s_sum, 1)
                keep_warm(c, 15)
                turned3.pe(pe, s_norm3, 4)
                keep_warm(c, 6)

            @block.scalar
            def _(act):
                act.sem_inc(s_w, 2)
                turned2.act(act)
                router.act(act)
                act.wait_ge(s_above, 1)
                nc.scalar.activation(likely[:], above[:], ACT.Exp).then_inc(s_likely, 1)

                def weights(i, j):
                    pair = i * 2 + j
                    act.wait_ge(s_turned, pair + 3)
                    act.wait_ge(s_out, i * (2 * NT) + (j * NT + NT))
                    nc.scalar.activation(w[j][:].rearrange("p k n -> p (k n)"), c.banks[6 + j][:].bitcast(BF16), ACT.Copy).then_inc(s_w, 1)

                with act.Fori(0, PAIRS // 2) as i:
                    weights(i, 0)
                    weights(i, 1)
                norm3.squares(act, acc[1])
                turned3.act(act)

            @block.vector
            def _(dve):
                dve.sem_inc(s_used, RING)
                rows = lambda t: c.x[:, t]
                for half in range(2):
                    norm1.moments(dve, rows, half)
                for half in range(2):
                    norm1.wait(dve, half)
                    for t in HALF_TILES[half]:
                        nc.vector.scalar_tensor_tensor(c.x[:, t], c.x[:, t], norm1.rstd[:, t:t + 1], c.sim[:, t], ALU.mult, ALU.add)
                    dve.drain()
                    norm2.moments(dve, rows, half)
                for half in range(2):
                    norm2.apply(dve, half, s_norm2)
                turned2.dve(dve)

                dve.wait_ge(router.s_logits, 1)
                logits = router.out[:, 0:NT * EXPERTS0].rearrange("p (t e) -> p t e", t=NT)
                wide = lambda v: v[:].unsqueeze(2).broadcast_to([P, NT, EXPERTS0])
                nc.vector.tensor_reduce(top[:], logits, AX.X, ALU.max)
                dve.drain()
                nc.vector.tensor_tensor(above[:], logits, wide(top), ALU.subtract).then_inc(s_above, 1)
                dve.drain()
                nc.vector.tensor_scalar(found[:], above[:], 0.0, -float(EXPERTS0), ALU.is_ge, ALU.mult)
                dve.wait_ge(s_numbers, 16)
                dve.drain()
                nc.vector.tensor_tensor(found[:], found[:], numbers[:], ALU.add)
                dve.drain()
                nc.vector.tensor_reduce(first[:], found[:], AX.X, ALU.min)
                dve.drain()
                nc.vector.tensor_scalar(first[:], first[:], float(EXPERTS0), None, ALU.add)
                dve.drain()
                nc.vector.tensor_tensor(chosen[:], numbers[:], wide(first), ALU.is_equal)
                dve.wait_ge(s_likely, 1)
                nc.vector.tensor_reduce(total[:], likely[:], AX.X, ALU.add)
                dve.drain()
                nc.vector.reciprocal(weight[:], total[:])
                dve.drain()
                nc.vector.tensor_tensor(gate[:], chosen[:], wide(weight), ALU.mult)
                dve.wait_ge(s_acc0, 1)
                dve.drain()
                flat = gate[:].rearrange("p t e -> p (t e)")

                def add(i, j):
                    for t in range(NT):
                        dve.wait_ge(s_out, i * (2 * NT) + (2 * NT + j * NT + t + 1))
                        for e in range(2):
                            g = flat[:, bass.ds(i * 4 + (t * EXPERTS0 + 2 * j + e), 1)]
                            last = nc.vector.scalar_tensor_tensor(acc[e][:, t], c.banks[t % RING][:, e * D:(e + 1) * D], g, acc[e][:, t], ALU.mult, ALU.add)
                        last.then_inc(s_used, 1)

                with dve.Fori(0, PAIRS // 2) as i:
                    add(i, 0)
                    add(i, 1)
                dve.drain()
                summed(nc.vector, dve, 1)
                for half in range(2):
                    if half == 0:
                        dve.wait_ge(s_sum, 1)
                    dve.drain()
                    for t in HALF_TILES[half]:
                        last = nc.vector.scalar_tensor_tensor(c.x[:, t], acc[0][:, t], 1.0, c.x[:, t], ALU.mult, ALU.add, accum_out=norm3.sums[:, t:t + 1])
                    last.then_inc(norm3.s_sum, 1)
                for half in range(2):
                    norm3.apply(dve, half, s_norm3)
                turned3.dve(dve)


def cross_and_experts(c):
    nc, a = c.nc, c.a
    PIECES = EXPERTS1 + SHARED
    OUT = NT // 2
    with ExitStack() as ctx:
        sb = lambda name, shape, dt=F32: ctx.enter_context(nc.sbuf_tensor(f"d_{name}", shape, dt))
        norm4, norm_s = (Norm(c, f"d_norm{i}", sb) for i in "4s")
        norm5, norm6 = (Norm(c, f"d_norm{i}", sb, summed=True) for i in "56")
        turned4, turned5 = Transposed(c, "d_turned4"), Transposed(c, "d_turned5")
        ot = sb("ot", [P, NTOK], F32R)
        scores, probs = sb("scores", [P, NT, T]), sb("probs", [P, NT, T])
        peak, row_sum, row_inv = sb("peak", [P, NT]), sb("row_sum", [P, NT]), sb("row_inv", [P, NT])
        wr, wr_split = sb("wr", [P, KC, EXPERTS1]), sb("wr_split", [P, KC, P // (2 * EXPERTS1), 2, EXPERTS1], F32R)
        router = Router(c, "d_router", sb, wr_split, EXPERTS1, c.banks[0:2], c.banks[4])
        logits = sb("logits", [P, NT, EXPERTS1])
        best, others, more = sb("best", [P, NT, 8]), sb("others", [P, NT, EXPERTS1]), sb("more", [P, NT, EXPERTS1])
        above, likely = sb("above", [P, NT, EXPERTS1]), sb("likely", [P, NT, EXPERTS1])
        total, weight = sb("total", [P, NT]), sb("weight", [P, NT])
        gate, primed = sb("gate", [P, NT, PIECES]), sb("primed", [P, 1])
        raw = [sb(f"raw{i}", [P, 3, D]) for i in range(2)]
        w_hi, w_lo = ([sb(f"w_{n}{i}", [P, 3, D], F32R) for i in range(2)] for n in ("hi", "lo"))
        silu, act_full = sb("silu", [P, 2, HALF]), [sb(f"h{i}", [HID, NTOK]) for i in range(2)]
        h_hi, h_lo = ([sb(f"h_{n}{i}", [HID, NTOK], F32R) for i in range(2)] for n in ("hi", "lo"))

        S = lambda name: c.sem(f"d_{name}")
        s_wr, s_wr_hi, s_wr_lo = S("wr"), S("wr_hi"), S("wr_lo")
        s_norm4, s_ot, s_ot_hi, s_ot_lo = S("norm4"), S("ot"), S("ot_hi"), S("ot_lo")
        s_sim, s_peak, s_exp, s_norm5 = S("sim"), S("peak"), S("exp"), S("norm5")
        s_weighted = S("weighted")
        SIM, WEIGHTED = (2, 3, 0, 1), (4, 5, 6, 7)
        s_above, s_likely = S("above"), S("likely")
        s_raw_up, s_raw_down = ([S(f"raw_{n}{i}") for i in range(2)] for n in ("up", "down"))
        s_split_up, s_split_down, s_pool = S("split_up"), S("split_down"), S("pool")
        s_up, s_silu, s_h, s_h_hi, s_h_lo = S("up"), S("silu"), S("h"), S("h_hi"), S("h_lo")
        s_out, s_used, s_norm6, s_store = S("out"), S("used"), S("norm6"), S("store")

        with nc.Block() as block:
            @block.sync
            def _(sp):
                sp.dma_start(wr[:], a["L1_ffn_w_router"].rearrange("(k p) e -> p k e", p=P)).then_inc(s_wr, 16)

                def load(j, done, first, third, second):
                    sp.wait_ge(s_split_up, done)
                    sp.dma_start(raw[j][:, 0].rearrange("p (k n) -> p k n", k=KC), first).then_inc(s_raw_up[j], 16)
                    sp.dma_start(raw[j][:, 1].rearrange("p (k n) -> p k n", k=KC), third).then_inc(s_raw_up[j], 16)
                    sp.wait_ge(s_split_down, done)
                    sp.dma_start(raw[j][:, 2], second).then_inc(s_raw_down[j], 16)

                with sp.Fori(0, EXPERTS1 // 2) as i:
                    for j in range(2):
                        one = bass.ds(i * 2 + j, 1)
                        load(j, i * 2 + (j + 1), *(a[f"L1_ffn_we{n}"][one].rearrange("n (k p) h -> p (n k) h", p=P) for n in (1, 3)),
                             a["L1_ffn_we2"][one].rearrange("n h d -> h (n d)"))
                for e in range(EXPERTS1, PIECES):
                    cols = slice((e - EXPERTS1) * HID, (e - EXPERTS1 + 1) * HID)
                    load(e % 2, e + 1, *(a[f"L1_ffn_ws{n}"][:, cols].rearrange("(k p) h -> p k h", p=P) for n in (1, 3)), a["L1_ffn_ws2"][cols, :])
                for b in range(B):
                    sp.wait_ge(s_norm6, 2 * b + 2)
                    sp.dma_start(c.out[b].rearrange("(t p) d -> p t d", p=P), c.x[:, 2 * b:2 * b + 2]).then_inc(s_store, 16)
                sp.wait_ge(s_store, 16 * B)

            @block.gpsimd
            def _(pool):
                own = Count(s_pool)
                pool.sem_inc(s_split_up, 2)
                pool.sem_inc(s_split_down, 2)
                norm4.roots(pool)
                for half in range(2):
                    norm_s.root(pool, half, 256 * 1e-6, squares=T)
                norm5.means(pool)
                norm5.roots(pool)

                def split(j, part, done):
                    width = part.stop - part.start
                    n = own.inc(nc.gpsimd.tensor_tensor(w_hi[j][:, part], raw[j][:, part], c.one[:].unsqueeze(1).broadcast_to([P, width, D]), ALU.mult))
                    pool.wait_ge(s_pool, n)
                    nc.gpsimd.tensor_tensor(w_lo[j][:, part], raw[j][:, part], f32(w_hi[j][:, part]), ALU.subtract).then_inc(done, 1)

                def split_up(i, j):
                    pool.wait_ge(s_raw_up[j], i * 32 + 32)
                    pool.wait_ge(s_up, i * 8 + (4 * j + 4))
                    split(j, slice(0, 2), s_split_up)

                def split_down(i, j):
                    pool.wait_ge(s_raw_down[j], i * 16 + 16)
                    pool.wait_ge(s_out, i * (2 * OUT) + (j + 1) * OUT)
                    split(j, slice(2, 3), s_split_down)

                def low(i, j):
                    for half in range(2):
                        pool.wait_ge(s_h_hi, i * 4 + (2 * j + half + 1))
                        cols = slice(half * HALF, (half + 1) * HALF)
                        nc.gpsimd.tensor_tensor(h_lo[j][:, cols], act_full[j][:, cols], f32(h_hi[j][:, cols]), ALU.subtract).then_inc(s_h_lo, 1)

                def turn(i, more):
                    split_up(i, 1)
                    low(i, 0)
                    split_down(i, 0)
                    if more:
                        split_up(i + 1, 0)
                    else:
                        split_down(i, 1)
                    low(i, 1)
                    if more:
                        split_down(i, 1)

                split_up(0, 0)
                with pool.Fori(0, PIECES // 2 - 1) as i:
                    own.enter(i, 4)
                    turn(i, True)
                own.leave(PIECES // 2 - 1)
                turn(PIECES // 2 - 1, False)
                norm6.means(pool)
                norm6.roots(pool)

            @block.tensor
            def _(pe):
                pe.sem_inc(s_out, 2 * OUT)
                pe.sem_inc(s_up, 8)
                keep_warm(c, 20)
                turned4.pe(pe, s_norm4, 4)
                for b in range(B):
                    turned4.wait(pe, b // 2)
                    rows = slice(b * T, (b + 1) * T)
                    for k in range(KC):
                        last = mm3(nc, c.banks[b // 2][:, (b % 2) * T:(b % 2 + 1) * T], c.kv_hi[:, 2 * b + k], c.kv_lo[:, 2 * b + k],
                                   c.xt_hi[:, k, rows], c.xt_lo[:, k, rows], k == 0, k == KC - 1)
                    if b % 2:
                        last.then_inc(s_ot, 1)
                for half in range(2):
                    pe.wait_ge(s_ot_lo, half + 1)
                    for hi, lo, banks, s_done in ((c.kvt_hi, c.kvt_lo, SIM, s_sim), (c.kvg_hi, c.kvg_lo, WEIGHTED, s_weighted)):
                        for b in range(2 * half, 2 * half + 2):
                            keys = slice(b * T, (b + 1) * T)
                            for i in range(2):
                                rows = slice(b * T + i * P, b * T + (i + 1) * P)
                                last = mm_stacked(nc, c.banks[banks[b]][:, i * T:(i + 1) * T], ot[:, rows], hi[:, keys], lo[:, keys], False)
                            last.then_inc(s_done, 1)
                pe.wait_ge(norm5.s_sum, 1)
                keep_warm(c, 14)
                turned5.pe(pe, s_norm5, 4)
                pe.wait_ge(s_wr_lo, 1)
                router.pe(pe, turned5)

                def up(i, j):
                    piece = i * 2 + j
                    pe.wait_ge(s_split_up, piece + 3)
                    for half in range(2):
                        pe.wait_ge(s_h, piece * 2 + (half + 1))
                        cols = slice(half * HALF, (half + 1) * HALF)
                        for n in range(2):
                            for k in range(KC):
                                s = slice(k * HID, (k + 1) * HID)
                                last = mm3(nc, c.banks[2 * half + n][:], w_hi[j][:, n, s], w_lo[j][:, n, s], c.xt_hi[:, k, cols], c.xt_lo[:, k, cols],
                                           k == 0, k == KC - 1)
                            last.then_inc(s_up, 1)

                def down(i, j):
                    pe.wait_ge(s_split_down, i * 2 + (j + 3))
                    for u in range(OUT):
                        if u % (OUT // 2) == 0:
                            pe.wait_ge(s_h_lo, i * 4 + (2 * j + u // (OUT // 2) + 1))
                        pe.wait_ge(s_used, i * (2 * OUT) + (j * OUT + u + 1))
                        for t in range(2):
                            cols = slice((2 * u + t) * P, (2 * u + t + 1) * P)
                            last = mm3(nc, c.banks[4 + u][:, t * D:(t + 1) * D], h_hi[j][:, cols], h_lo[j][:, cols], w_hi[j][:, 2], w_lo[j][:, 2], True, True)
                        last.then_inc(s_out, 1)

                up(0, 0)
                pe.wait_ge(s_above, 1)
                with pe.Fori(0, PIECES // 2 - 1) as i:
                    up(i, 1)
                    down(i, 0)
                    up(i + 1, 0)
                    down(i, 1)
                up(PIECES // 2 - 1, 1)
                down(PIECES // 2 - 1, 0)
                down(PIECES // 2 - 1, 1)

            @block.scalar
            def _(act):
                act.wait_ge(s_wr, 16)
                nc.scalar.activation(wr_split[:, :, :, 0], again(wr[:], EXPERTS1), ACT.Copy).then_inc(s_wr_hi, 1)
                turned4.act(act)
                for h in range(2):
                    act.wait_ge(s_ot, h + 1)
                    nc.scalar.activation(ot[:, h * HALF:(h + 1) * HALF], c.banks[h][:], ACT.Copy).then_inc(s_ot_hi, 1)
                for half in range(2):
                    for t in HALF_TILES[half]:
                        act.wait_ge(s_sim, t // 2 + 1)
                        last = nc.scalar.activation(probs[:, t], c.banks[SIM[t // 2]][:, (t % 2) * T:(t % 2 + 1) * T], ACT.Square, accum_out=norm_s.mv[:, t, 1:2])
                    last.then_inc(norm_s.s_var, 1)
                for t in range(NT):
                    act.wait_ge(s_peak, t // 4 + 1)
                    nc.scalar.activation(probs[:, t], scores[:, t], ACT.Exp, bias=peak[:, t:t + 1], accum_out=row_sum[:, t:t + 1]).then_inc(s_exp, 1)
                norm5.squares(act, probs)
                turned5.act(act)
                router.act(act)
                act.wait_ge(s_above, 1)
                nc.scalar.activation(likely[:], above[:], ACT.Exp).then_inc(s_likely, 1)

                def hidden(i, j):
                    for half in range(2):
                        act.wait_ge(s_up, i * 8 + (8 + 4 * j + 2 * half + 1))
                        act.wait_ge(s_h, i * 4 + (2 * j + half + 1))
                        nc.scalar.activation(silu[:, half], c.banks[2 * half][:], ACT.Silu).then_inc(s_silu, 1)
                        act.wait_ge(s_h, i * 4 + (2 * j + half + 3))
                        cols = slice(half * HALF, (half + 1) * HALF)
                        nc.scalar.activation(h_hi[j][:, cols], act_full[j][:, cols], ACT.Copy).then_inc(s_h_hi, 1)

                nc.scalar.activation(primed[:], c.one[:], ACT.Silu)
                with act.Fori(0, PIECES // 2) as i:
                    hidden(i, 0)
                    hidden(i, 1)
                norm6.squares(act, probs)

            @block.vector
            def _(dve):
                dve.sem_inc(s_h, 2)
                dve.sem_inc(s_used, OUT)
                rows = lambda t: c.x[:, t]
                for half in range(2):
                    norm4.moments(dve, rows, half)
                dve.wait_ge(s_wr_hi, 1)
                nc.vector.tensor_tensor(wr_split[:, :, :, 1], again(wr[:], EXPERTS1), f32(wr_split[:, :, :, 0]), ALU.subtract).then_inc(s_wr_lo, 1)
                for half in range(2):
                    norm4.apply(dve, half, s_norm4)
                turned4.dve(dve)
                for h in range(2):
                    dve.wait_ge(s_ot_hi, h + 1)
                    cols = slice(h * HALF, (h + 1) * HALF)
                    nc.vector.tensor_tensor(ot[LOW, cols], c.banks[h][LOW], f32(ot[LOW, cols]), ALU.subtract).then_inc(s_ot_lo, 1)

                for half in range(2):
                    part = slice(HALF_TILES[half].start, HALF_TILES[half].stop)
                    norm_s.wait(dve, half)
                    dve.wait_ge(s_weighted, (half + 1) * B // 2)
                    for t in HALF_TILES[half]:
                        weighted = c.banks[WEIGHTED[t // 2]][:, (t % 2) * T:(t % 2 + 1) * T]
                        nc.vector.scalar_tensor_tensor(scores[:, t], weighted, norm_s.rstd[:, t:t + 1], c.rows[:, ROW_BETA], ALU.mult, ALU.add)
                    dve.drain()
                    nc.vector.tensor_reduce(peak[:, part], scores[:, part], AX.X, ALU.max)
                    dve.drain()
                    nc.vector.tensor_scalar(peak[:, part], peak[:, part], -1.0, None, ALU.mult).then_inc(s_peak, 1)
                for half in range(2):
                    part = slice(HALF_TILES[half].start, HALF_TILES[half].stop)
                    dve.wait_ge(s_exp, HALF_TILES[half].stop)
                    nc.vector.reciprocal(row_inv[:, part], row_sum[:, part])
                    dve.drain()
                    for t in HALF_TILES[half]:
                        last = nc.vector.scalar_tensor_tensor(c.x[:, t], probs[:, t], row_inv[:, t:t + 1], c.x[:, t], ALU.mult, ALU.add,
                                                              accum_out=norm5.sums[:, t:t + 1])
                    last.then_inc(norm5.s_sum, 1)
                for half in range(2):
                    norm5.apply(dve, half, s_norm5)
                turned5.dve(dve)

                wide = lambda v: v.broadcast_to([P, NT, EXPERTS1])
                dve.wait_ge(router.s_logits, 1)
                nc.vector.tensor_copy(logits[:], router.out[:, 0:NT * EXPERTS1].rearrange("p (t e) -> p t e", t=NT))
                dve.drain()
                for t in range(NT):
                    nc.vector.max(best[:, t], logits[:, t])
                dve.drain()
                nc.vector.tensor_tensor(above[:], logits[:], wide(best[:, :, 0:1]), ALU.subtract).then_inc(s_above, 1)
                nc.vector.memset(best[:, :, TOPK:], 3e38)
                dve.drain()
                for t in range(NT):
                    nc.vector.match_replace(others[:, t], best[:, t], logits[:, t], -3e38)
                dve.drain()
                nc.vector.tensor_tensor(more[:], logits[:], others[:], ALU.is_gt)
                dve.wait_ge(s_likely, 1)
                dve.drain()
                nc.vector.tensor_tensor(likely[:], likely[:], more[:], ALU.mult)
                dve.drain()
                nc.vector.tensor_reduce(total[:], likely[:], AX.X, ALU.add)
                nc.vector.memset(gate[:, :, EXPERTS1:], 1.0 / (TOPK + 1))
                dve.drain()
                nc.vector.reciprocal(weight[:], total[:])
                dve.drain()
                nc.vector.tensor_scalar(weight[:], weight[:], TOPK / (TOPK + 1), None, ALU.mult)
                dve.drain()
                nc.vector.tensor_tensor(gate[:, :, 0:EXPERTS1], likely[:], wide(weight[:].unsqueeze(2)), ALU.mult)
                dve.drain()
                flat = gate[:].rearrange("p t e -> p (t e)")

                def hidden(i, j):
                    for half in range(2):
                        dve.wait_ge(s_silu, i * 4 + (2 * j + half + 1))
                        dve.wait_ge(s_up, i * 8 + (8 + 4 * j + 2 * half + 2))
                        cols = slice(half * HALF, (half + 1) * HALF)
                        nc.vector.tensor_tensor(act_full[j][:, cols], silu[:, half], c.banks[2 * half + 1][:], ALU.mult).then_inc(s_h, 1)

                def add(i, j, units=range(OUT), norm=None):
                    for u in units:
                        dve.wait_ge(s_out, i * (2 * OUT) + (2 * OUT + j * OUT + u + 1))
                        for t in range(2 * u, 2 * u + 2):
                            g = flat[:, bass.ds(i * 2 + (t * PIECES + j), 1)]
                            last = nc.vector.scalar_tensor_tensor(c.x[:, t], c.banks[4 + u][:, (t % 2) * D:(t % 2 + 1) * D], g, c.x[:, t], ALU.mult, ALU.add,
                                                                  accum_out=norm.sums[:, t:t + 1] if norm else None)
                        if not norm:
                            last.then_inc(s_used, 1)
                        elif u == units[-1]:
                            last.then_inc(norm.s_sum, 1)

                hidden(0, 0)
                with dve.Fori(0, PIECES // 2 - 1) as i:
                    hidden(i, 1)
                    add(i, 0)
                    hidden(i + 1, 0)
                    add(i, 1)
                hidden(PIECES // 2 - 1, 1)
                add(PIECES // 2 - 1, 0)
                for half in range(2):
                    add(PIECES // 2 - 1, 1, range(half * OUT // 2, (half + 1) * OUT // 2), norm6)
                for half in range(2):
                    norm6.apply(dve, half, s_norm6)


_INS = ['x', 'ctx_512', 'L0_attn_w_q', 'L0_attn_b_q', 'L0_attn_w_k', 'L0_attn_b_k', 'L0_attn_w_v', 'L0_attn_b_v',
        'L0_attn_w_o', 'L0_attn_b_o', 'L0_xattn_Wq', 'L0_xattn_Wk', 'L0_xattn_gamma_raw', 'L0_ffn_weight', 'L0_ffn_scale',
        'L0_ffn_expert_masks', 'L0_ffn_router_w', 'L1_attn_Wq', 'L1_attn_Wk', 'L1_attn_Wv', 'L1_attn_Wo',
        'L1_attn_head_scale', 'L1_xattn_W_k', 'L1_xattn_b_k', 'L1_xattn_ln_gamma', 'L1_xattn_ln_beta', 'L1_ffn_w_router',
        'L1_ffn_we1', 'L1_ffn_we3', 'L1_ffn_we2', 'L1_ffn_ws1', 'L1_ffn_ws3', 'L1_ffn_ws2']


def constants():
    import numpy as np
    freq = (1.0 / np.float32(10000.0) ** (np.arange(0, DH, 2, dtype=np.float32) / np.float32(DH))).astype(np.float32)
    angle = np.arange(T, dtype=np.float32)[None, :] * freq[:, None]
    cos, sin = np.cos(angle).astype(np.float32), np.sin(angle).astype(np.float32)
    return {
        "ident": np.eye(P, dtype=np.float32),
        "causal": np.triu(np.full((P, P), -1e30, np.float32), 1),
        "numbers": np.tile(np.arange(EXPERTS0, dtype=np.float32), (P, NT, 1)),
        "cos": np.concatenate([cos, cos]),
        "sin": np.concatenate([sin, -sin]),
    }


def kernel(**inputs):
    import numpy as _np
    import concourse.bacc as _bacc
    from concourse.bass_utils import run_bass_kernel_spmd as _run

    nc = _bacc.Bacc("TRN2", target_bir_lowering=False, num_devices=1)
    arrays, args = {}, {}
    for name, value in [(n, inputs[n]) for n in _INS] + list(constants().items()):
        v = _np.ascontiguousarray(value)
        if v.ndim == 0:
            v = v.reshape(1)
        arrays[f"in_{name}_dram"] = v
        args[name] = nc.dram_tensor(f"in_{name}_dram", v.shape, mybir.dt.from_np(v.dtype), kind="ExternalInput").ap()
    out = nc.dram_tensor("out_0_dram", (B, T, D), F32, kind="ExternalOutput").ap()
    decoder(nc, args, out)
    r = _run(nc, [arrays], core_ids=[0])
    return r.results[0]["out_0_dram"]
```
